# Optimizing a Trainium2 kernel written in Bass

```python
import numpy as np
import jax
import jax.numpy as jnp

def _softmax(x, axis=-1):
    return jax.nn.softmax(x, axis=axis)

def _gelu(x):
    return jax.nn.gelu(x, approximate=True)

def _silu(x):
    return jax.nn.silu(x)

def _sigmoid(x):
    return jax.nn.sigmoid(x)

def _layernorm(x, axis=-1, eps=1e-05):
    m = jnp.mean(x, axis=axis, keepdims=True)
    v = jnp.var(x, axis=axis, keepdims=True)
    return (x - m) / jnp.sqrt(v + eps)

def _scatter_add(tgt, idx, src, axis=0):
    return tgt.at[idx].add(src)

def _segment_sum(src, seg, n):
    return jax.ops.segment_sum(src, seg, n)
kernel_name = 'mk_flamingo_gated_d2_seqx_r8_3041c0'

def setup_inputs(seed: int=0):
    np.random.seed(seed)
    _w = jnp.asarray

    def _rec_inputs():
        import jax
        import jax.numpy as jnp
        _rk = jax.random.key(seed)
        x = 0.0002417 + 0.9998 * jax.random.normal(jax.random.fold_in(_rk, 1), (32, 128, 128), jnp.float32)
        _lenS = 128 - jax.random.randint(jax.random.fold_in(_rk, 7), (32,), 0, max(1, 128 // 4) + 1, jnp.int32)
        _lenS2 = 128 - jax.random.randint(jax.random.fold_in(_rk, 8), (32,), 0, max(1, 128 // 4) + 1, jnp.int32)
        _ctx_1024P = jax.random.normal(jax.random.fold_in(_rk, 11), (32, 16, 128), jnp.float32)
        _ctx_1024c = jax.random.dirichlet(jax.random.fold_in(_rk, 511), 0.3 * jnp.ones((16,), jnp.float32), (32, 128))
        _ctx_1024t = jnp.einsum('bsk,bkd->bsd', _ctx_1024c, _ctx_1024P)
        _ctx_1024t = _ctx_1024t * jax.lax.rsqrt(jnp.mean(jnp.square(_ctx_1024t)) + 1e-12) * 0.953939
        ctx_1024 = 7.22013e-05 + 1.00017 * (_ctx_1024t + 0.3 * jax.random.normal(jax.random.fold_in(_rk, 611), (32, 128, 128), jnp.float32))
        _validS = jnp.arange(128)[None, :] < _lenS[:, None]
        _validS2 = jnp.arange(128)[None, :] < _lenS2[:, None]
        _causal = jnp.tril(jnp.ones((128, 128), dtype=bool))
        mask_BxS2_bk0 = jnp.logical_not(jnp.broadcast_to(_validS2[:, :], (32, 128)))
        _g = jax.random.normal(jax.random.fold_in(_rk, 9001), (2, 2), jnp.float32)
        _g = jnp.sign(_g) * jnp.maximum(jnp.abs(_g), 1.0) + (_g == 0) * 1.0
        g_xattn = _g[0]
        g_ffn = _g[1]
        return (x, ctx_1024, mask_BxS2_bk0, g_xattn, g_ffn)
    x, ctx_1024, mask_BxS2_bk0, g_xattn, g_ffn = _rec_inputs()

    def _L0_xattn_setup():
        import jax, jax.numpy as jnp
        import numpy as np
        EMB = 128
        HEADS = 16
        HEAD_DIM = EMB // HEADS
        key = jax.random.key(seed)
        ks = jax.random.split(key, 12)
        B, S = (4, 256)
        scale = 1.0 / np.sqrt(EMB)
        inp = {'values': jax.random.normal(ks[0], (B, S, EMB), jnp.float32), 'keys': jax.random.normal(ks[1], (B, S, EMB), jnp.float32), 'query': jax.random.normal(ks[2], (B, S, EMB), jnp.float32), 'Wv': jax.random.normal(ks[3], (EMB, EMB), jnp.float32) * scale, 'bv': jnp.zeros((EMB,), jnp.float32), 'Wk': jax.random.normal(ks[4], (EMB, EMB), jnp.float32) * scale, 'bk': jnp.zeros((EMB,), jnp.float32), 'Wq': jax.random.normal(ks[5], (EMB, EMB), jnp.float32) * scale, 'bq': jnp.zeros((EMB,), jnp.float32), 'Wo': jax.random.normal(ks[6], (EMB, EMB), jnp.float32) * scale, 'bo': jnp.zeros((EMB,), jnp.float32)}
        return inp
    _L0_xattn_all = _L0_xattn_setup()
    _L0_xattn_in = {k: v for k, v in _L0_xattn_all.items() if k in ('Wv', 'bv', 'Wk', 'bk', 'Wq', 'bq', 'Wo', 'bo')}
    del _L0_xattn_all

    def _L0_ffn_setup():
        import jax, jax.numpy as jnp
        import numpy as np
        B, C, D, O = (4, 512, 128, 128)
        PROJ = 32
        RANKS = [1, 2, 4, 8]
        E = len(RANKS)
        CLAMP_MAX = float(np.log(1.0 / 0.01))

        def _l2norm(v, axis):
            return v / jnp.maximum(jnp.linalg.norm(v, axis=axis, keepdims=True), 1e-12)
        key = jax.random.key(seed)
        ks = jax.random.split(key, 16)
        inp = {'x': jax.random.normal(ks[0], (B, C, D), dtype=jnp.float32), 'W': jax.random.normal(ks[1], (O, D), dtype=jnp.float32) / np.sqrt(D), 'Wp': jax.random.normal(ks[2], (PROJ, D), dtype=jnp.float32) / np.sqrt(D), 'bp': jnp.zeros((PROJ,), dtype=jnp.float32), 'sim': jax.random.normal(ks[3], (PROJ, E), dtype=jnp.float32) * 0.01, 'temp': jnp.full((1,), np.log(1.0 / 0.5), dtype=jnp.float32)}
        for i, r in enumerate(RANKS):
            inp[f'Wd{i}'] = jax.random.normal(ks[4 + 2 * i], (r, D), dtype=jnp.float32) / r
            inp[f'Wu{i}'] = jax.random.normal(ks[5 + 2 * i], (O, r), dtype=jnp.float32) * 0.01
        return inp
    _L0_ffn_all = _L0_ffn_setup()
    _L0_ffn_in = {k: v for k, v in _L0_ffn_all.items() if k in ('W', 'Wp', 'bp', 'sim', 'temp', 'Wd0', 'Wu0', 'Wd1', 'Wu1', 'Wd2', 'Wu2', 'Wd3', 'Wu3')}
    del _L0_ffn_all

    def _L1_xattn_setup():
        import jax, jax.numpy as jnp
        import numpy as np
        DIM = 128
        HEADS = 8
        DIM_HEAD = 64
        INNER = HEADS * DIM_HEAD
        LN_EPS = 1e-05

        def _layernorm(x, g, b):
            mu = jnp.mean(x, axis=-1, keepdims=True)
            var = jnp.var(x, axis=-1, keepdims=True)
            return (x - mu) * jax.lax.rsqrt(var + LN_EPS) * g + b
        key = jax.random.key(seed)
        ks = jax.random.split(key, 8)
        b, n, m = (4, 256, 64)
        x = jax.random.normal(ks[0], (b, n, DIM), dtype=jnp.float32)
        media = jax.random.normal(ks[1], (b, m, DIM), dtype=jnp.float32)
        media_mask = jax.random.randint(ks[2], (b, m), 0, 2).astype(jnp.bool_)
        media_mask = media_mask.at[:, 0].set(True)
        ln_g = jnp.ones((DIM,), jnp.float32)
        ln_b = jnp.zeros((DIM,), jnp.float32)
        s = 0.02
        Wq = jax.random.normal(ks[3], (DIM, INNER), jnp.float32) * s
        Wkv = jax.random.normal(ks[4], (DIM, 2 * INNER), jnp.float32) * s
        Wo = jax.random.normal(ks[5], (INNER, DIM), jnp.float32) * s
        return {'x': x, 'media': media, 'media_mask': media_mask, 'ln_g': ln_g, 'ln_b': ln_b, 'Wq': Wq, 'Wkv': Wkv, 'Wo': Wo}
    _L1_xattn_all = _L1_xattn_setup()
    _L1_xattn_in = {k: v for k, v in _L1_xattn_all.items() if k in ('ln_g', 'ln_b', 'Wq', 'Wkv', 'Wo')}
    del _L1_xattn_all

    def _L1_ffn_setup():
        import jax, jax.numpy as jnp
        import numpy as np
        E = 8
        K = 2
        CAPACITY_FACTOR = 1.25
        key = jax.random.key(seed)
        ks = jax.random.split(key, 4)
        B, T, C, H = (8, 256, 128, 512)
        x = jax.random.normal(ks[0], (B, T, C), jnp.float32)
        Wr = jax.random.normal(ks[1], (C, E), jnp.float32) * 0.02
        br = jnp.zeros((E,), jnp.float32)
        W1 = jax.random.normal(ks[2], (E, C, H), jnp.float32) * 0.02
        b1 = jnp.zeros((E, H), jnp.float32)
        W2 = jax.random.normal(ks[3], (E, H, C), jnp.float32) * 0.02
        b2 = jnp.zeros((E, C), jnp.float32)
        return {'x': x, 'Wr': Wr, 'br': br, 'W1': W1, 'b1': b1, 'W2': W2, 'b2': b2}
    _L1_ffn_all = _L1_ffn_setup()
    _L1_ffn_in = {k: v for k, v in _L1_ffn_all.items() if k in ('Wr', 'br', 'W1', 'b1', 'W2', 'b2')}
    del _L1_ffn_all
    return {'x': x, 'ctx_1024': ctx_1024, 'mask_BxS2_bk0': mask_BxS2_bk0, 'g_xattn': g_xattn, 'g_ffn': g_ffn, 'L0_xattn_Wv': _L0_xattn_in['Wv'], 'L0_xattn_bv': _L0_xattn_in['bv'], 'L0_xattn_Wk': _L0_xattn_in['Wk'], 'L0_xattn_bk': _L0_xattn_in['bk'], 'L0_xattn_Wq': _L0_xattn_in['Wq'], 'L0_xattn_bq': _L0_xattn_in['bq'], 'L0_xattn_Wo': _L0_xattn_in['Wo'], 'L0_xattn_bo': _L0_xattn_in['bo'], 'L0_ffn_W': _L0_ffn_in['W'], 'L0_ffn_Wp': _L0_ffn_in['Wp'], 'L0_ffn_bp': _L0_ffn_in['bp'], 'L0_ffn_sim': _L0_ffn_in['sim'], 'L0_ffn_temp': _L0_ffn_in['temp'], 'L0_ffn_Wd0': _L0_ffn_in['Wd0'], 'L0_ffn_Wu0': _L0_ffn_in['Wu0'], 'L0_ffn_Wd1': _L0_ffn_in['Wd1'], 'L0_ffn_Wu1': _L0_ffn_in['Wu1'], 'L0_ffn_Wd2': _L0_ffn_in['Wd2'], 'L0_ffn_Wu2': _L0_ffn_in['Wu2'], 'L0_ffn_Wd3': _L0_ffn_in['Wd3'], 'L0_ffn_Wu3': _L0_ffn_in['Wu3'], 'L1_xattn_ln_g': _L1_xattn_in['ln_g'], 'L1_xattn_ln_b': _L1_xattn_in['ln_b'], 'L1_xattn_Wq': _L1_xattn_in['Wq'], 'L1_xattn_Wkv': _L1_xattn_in['Wkv'], 'L1_xattn_Wo': _L1_xattn_in['Wo'], 'L1_ffn_Wr': _L1_ffn_in['Wr'], 'L1_ffn_br': _L1_ffn_in['br'], 'L1_ffn_W1': _L1_ffn_in['W1'], 'L1_ffn_b1': _L1_ffn_in['b1'], 'L1_ffn_W2': _L1_ffn_in['W2'], 'L1_ffn_b2': _L1_ffn_in['b2']}

def reference(x, ctx_1024, mask_BxS2_bk0, g_xattn, g_ffn, L0_xattn_Wv, L0_xattn_bv, L0_xattn_Wk, L0_xattn_bk, L0_xattn_Wq, L0_xattn_bq, L0_xattn_Wo, L0_xattn_bo, L0_ffn_W, L0_ffn_Wp, L0_ffn_bp, L0_ffn_sim, L0_ffn_temp, L0_ffn_Wd0, L0_ffn_Wu0, L0_ffn_Wd1, L0_ffn_Wu1, L0_ffn_Wd2, L0_ffn_Wu2, L0_ffn_Wd3, L0_ffn_Wu3, L1_xattn_ln_g, L1_xattn_ln_b, L1_xattn_Wq, L1_xattn_Wkv, L1_xattn_Wo, L1_ffn_Wr, L1_ffn_br, L1_ffn_W1, L1_ffn_b1, L1_ffn_W2, L1_ffn_b2):
    import jax
    import jax.numpy as jnp

    def _L0_xattn_ref(values, keys, query, Wv, bv, Wk, bk, Wq, bq, Wo, bo):
        import jax, jax.numpy as jnp
        import numpy as np
        EMB = 128
        HEADS = 16
        HEAD_DIM = EMB // HEADS
        B, S, _ = values.shape
        v = values @ Wv.T + bv
        k = keys @ Wk.T + bk
        q = query @ Wq.T + bq
        v = v.reshape(B, S, HEADS, HEAD_DIM)
        k = k.reshape(B, S, HEADS, HEAD_DIM)
        q = q.reshape(B, S, HEADS, HEAD_DIM)
        scores = jnp.einsum('bshd,bsgd->bshg', q, k) * HEAD_DIM ** (-0.5)
        attn = jax.nn.softmax(scores, axis=-1)
        out = jnp.einsum('bshg,bsgd->bshd', attn, v)
        out = out.reshape(B, S, EMB)
        return out @ Wo.T + bo

    def _L0_ffn_ref(x, W, Wp, bp, sim, temp, Wd0, Wu0, Wd1, Wu1, Wd2, Wu2, Wd3, Wu3):
        import jax, jax.numpy as jnp
        import numpy as np
        B, C, D, O = (4, 512, 128, 128)
        PROJ = 32
        RANKS = [1, 2, 4, 8]
        E = len(RANKS)
        CLAMP_MAX = float(np.log(1.0 / 0.01))

        def _l2norm(v, axis):
            return v / jnp.maximum(jnp.linalg.norm(v, axis=axis, keepdims=True), 1e-12)
        base = jnp.einsum('bcd,od->bco', x, W)
        xf = x.reshape(-1, x.shape[-1])
        proj = _l2norm(xf @ Wp.T + bp, axis=1)
        simn = _l2norm(sim, axis=0)
        scale = jnp.exp(jnp.minimum(temp, CLAMP_MAX))
        logits = proj @ simn * scale
        lw = jax.nn.softmax(logits, axis=1)
        top1 = jnp.argmax(lw, axis=1)
        ret = jnp.where(jnp.arange(E)[None, :] == top1[:, None], lw, 0.0)
        ret = ret.reshape(x.shape[0], x.shape[1], E)
        downs = (Wd0, Wd1, Wd2, Wd3)
        ups = (Wu0, Wu1, Wu2, Wu3)
        l = jnp.stack([jnp.einsum('bcr,or->bco', jnp.einsum('bcd,rd->bcr', x, d), u) for d, u in zip(downs, ups)], axis=2)
        res = jnp.sum(ret[..., None] * l, axis=2)
        return base + res

    def _L1_xattn_ref(x, media, media_mask, ln_g, ln_b, Wq, Wkv, Wo):
        import jax, jax.numpy as jnp
        import numpy as np
        DIM = 128
        HEADS = 8
        DIM_HEAD = 64
        INNER = HEADS * DIM_HEAD
        LN_EPS = 1e-05

        def _layernorm(x, g, b):
            mu = jnp.mean(x, axis=-1, keepdims=True)
            var = jnp.var(x, axis=-1, keepdims=True)
            return (x - mu) * jax.lax.rsqrt(var + LN_EPS) * g + b
        scale = DIM_HEAD ** (-0.5)
        xn = _layernorm(x, ln_g, ln_b)
        q = xn @ Wq
        kv = media @ Wkv
        k, v = jnp.split(kv, 2, axis=-1)

        def split_heads(t):
            b_, s_, _ = t.shape
            return t.reshape(b_, s_, HEADS, DIM_HEAD).transpose(0, 2, 1, 3)
        q, k, v = (split_heads(q) * scale, split_heads(k), split_heads(v))
        sim = jnp.einsum('bhid,bhjd->bhij', q, k)
        neg_inf = jnp.finfo(sim.dtype).min
        sim = jnp.where(media_mask[:, None, None, :], sim, neg_inf)
        attn = jax.nn.softmax(sim, axis=-1)
        out = jnp.einsum('bhij,bhjd->bhid', attn, v)
        out = out.transpose(0, 2, 1, 3).reshape(x.shape[0], x.shape[1], INNER)
        return out @ Wo

    def _L1_ffn_ref(x, Wr, br, W1, b1, W2, b2):
        import jax, jax.numpy as jnp
        import numpy as np
        E = 8
        K = 2
        CAPACITY_FACTOR = 1.25
        B, T, C = x.shape
        cap = max(1, int(T / E * CAPACITY_FACTOR))
        probs = jax.nn.softmax(x @ Wr + br, axis=-1)
        topk_p, topk_e = jax.lax.top_k(probs, K)
        e_flat = topk_e.reshape(B, T * K)
        p_flat = topk_p.reshape(B, T * K)
        oh = jax.nn.one_hot(e_flat, E, dtype=jnp.int32)
        pos_all = jnp.cumsum(oh, axis=1) - oh
        pos = jnp.take_along_axis(pos_all, e_flat[:, :, None], axis=2)[:, :, 0]
        keep = pos < cap
        b_idx = jnp.arange(B)[:, None]
        flat_idx = (e_flat * B + b_idx) * cap + jnp.minimum(pos, cap - 1)
        x_rep = jnp.broadcast_to(x[:, :, None, :], (B, T, K, C)).reshape(B, T * K, C)
        buf = jnp.zeros((E * B * cap, C), x.dtype).at[flat_idx.reshape(-1)].add((x_rep * keep[:, :, None].astype(x.dtype)).reshape(-1, C))
        buf = buf.reshape(E, B * cap, C)
        h = jax.nn.relu(jnp.einsum('enc,ech->enh', buf, W1) + b1[:, None, :])
        y = jnp.einsum('enh,ehc->enc', h, W2) + b2[:, None, :]
        y_tok = y.reshape(E * B * cap, C)[flat_idx.reshape(-1)].reshape(B, T * K, C)
        y_tok = y_tok * (p_flat * keep.astype(x.dtype))[:, :, None]
        return y_tok.reshape(B, T, K, C).sum(axis=2)
    x = x + jnp.tanh(g_xattn[0]) * _L0_xattn_ref(ctx_1024, ctx_1024, _layernorm(x, axis=-1), L0_xattn_Wv, L0_xattn_bv, L0_xattn_Wk, L0_xattn_bk, L0_xattn_Wq, L0_xattn_bq, L0_xattn_Wo, L0_xattn_bo)
    x = x + jnp.tanh(g_ffn[0]) * _L0_ffn_ref(_layernorm(x, axis=-1), L0_ffn_W, L0_ffn_Wp, L0_ffn_bp, L0_ffn_sim, L0_ffn_temp, L0_ffn_Wd0, L0_ffn_Wu0, L0_ffn_Wd1, L0_ffn_Wu1, L0_ffn_Wd2, L0_ffn_Wu2, L0_ffn_Wd3, L0_ffn_Wu3)
    x = x + jnp.tanh(g_xattn[1]) * _L1_xattn_ref(_layernorm(x, axis=-1), ctx_1024, mask_BxS2_bk0, L1_xattn_ln_g, L1_xattn_ln_b, L1_xattn_Wq, L1_xattn_Wkv, L1_xattn_Wo)
    x = x + jnp.tanh(g_ffn[1]) * _L1_ffn_ref(_layernorm(x, axis=-1), L1_ffn_Wr, L1_ffn_br, L1_ffn_W1, L1_ffn_b1, L1_ffn_W2, L1_ffn_b2)
    return x

_drawn_inputs = setup_inputs


def setup_inputs(seed=0):
    import zlib

    import numpy as np

    out = dict(_drawn_inputs(seed))
    spreads = {'g_ffn': (-1.0, 0.6),
     'L0_xattn_bv': (0.0, 0.278),
     'L0_xattn_bk': (0.0, 0.359),
     'L0_xattn_bq': (0.0, 0.31),
     'L0_xattn_bo': (0.0, 0.1),
     'L0_ffn_bp': (0.0, 0.8),
     'L1_xattn_ln_g': (1.0, 0.6),
     'L1_xattn_ln_b': (0.0, 0.8),
     'L1_ffn_br': (0.0, 0.727),
     'L1_ffn_b1': (0.0, 0.8),
     'L1_ffn_b2': (0.0, 0.693)}
    factors = {'L0_ffn_Wp': 3.634,
     'L0_ffn_sim': 3.455,
     'L0_ffn_Wd0': 4.061,
     'L0_ffn_Wu0': 3.759,
     'L0_ffn_Wd1': 6.974,
     'L0_ffn_Wu1': 6.934,
     'L0_ffn_Wd2': 8.0,
     'L0_ffn_Wu2': 8.0,
     'L0_ffn_Wd3': 8.0,
     'L0_ffn_Wu3': 8.0,
     'L1_xattn_Wq': 8.0,
     'L1_ffn_Wr': 4.44,
     'L1_ffn_W1': 8.0,
     'L1_ffn_W2': 6.425}
    for name, (base, spread) in spreads.items():
        noise = np.random.default_rng([zlib.crc32(name.encode()), seed]).standard_normal(out[name].shape)
        drawn = base * np.exp(spread * noise) if base else spread * noise
        out[name] = jnp.asarray(drawn.astype(out[name].dtype))
    for name, factor in factors.items():
        out[name] = (out[name] * factor).astype(out[name].dtype)
    return out
```

```python
from contextlib import ExitStack

import concourse.bass as bass
from concourse import mybir

ALU = mybir.AluOpType
ACT = mybir.ActivationFunctionType
F32 = mybir.dt.float32
BF16 = mybir.dt.bfloat16
U8 = mybir.dt.uint8
U32 = mybir.dt.uint32
X = mybir.AxisListType.X
ds = bass.ds

P = 128
B = 32
H0, D0 = 16, 8
H1, D1 = 8, 64
RANKS = (1, 2, 4, 8)
NR = sum(RANKS)
PROJ = 32
E = 8
HID = 512
HC = HID // P
CAP = 20
ES = E * CAP
HALF = ES // 2
MASKED = -float(2.0 ** 100)
CLAMP = 4.605170185988092

A1, A2, B1, B2, C1, C2, DD = range(7)
STAGES = 7
STEPS = B + STAGES - 1
LN_STAGES = (A1, B1, C1, DD)


def build(nc, a, out):
    ctx = ExitStack()
    with ctx:
        def sb(name, shape, dt=F32):
            return ctx.enter_context(nc.sbuf_tensor(name, shape, dt))

        def bank(name):
            return ctx.enter_context(nc.psum_tensor(name, [P, 512], F32))

        def sem(name):
            return ctx.enter_context(nc.semaphore(name))

        ident = sb("ident", [P, P])
        identb = sb("identb", [P, P], BF16)
        before = sb("before", [P, P], BF16)
        minus_head = sb("minus_head", [3 * H1, H1, P], BF16)
        ones_row = sb("ones_row", [1, P], BF16)
        ones32 = sb("ones32", [PROJ, PROJ])
        zeros8 = sb("zeros8", [P, H1])
        iota8 = sb("iota8", [P, E])
        iota_slot = sb("iota_slot", [P, CAP])
        key15 = sb("key15", [P, NR])
        share15 = sb("share15", [P, NR])
        ln_mul = sb("ln_mul", [P, 4])
        ln_add = sb("ln_add", [P, 4])
        minus_half = sb("minus_half", [P, 16])
        wqkv0 = sb("wqkv0", [P, 3 * P])
        bqkv0 = sb("bqkv0", [P, 3 * P])
        wo0 = sb("wo0", [P, P])
        bo0 = sb("bo0", [P, P])
        wffn0 = sb("wffn0", [P, P + PROJ + 2 * NR])
        bffn0 = sb("bffn0", [P, PROJ + 2 * NR])
        wu0 = sb("wu0", [NR, P])
        wp0 = sb("wp0", [PROJ, P])
        sim15 = sb("sim15", [PROJ, NR])
        simsq = sb("simsq", [PROJ, NR])
        simrn = sb("simrn", [PROJ, NR])
        bpcol = sb("bpcol", [PROJ, 1])
        bpwide = sb("bpwide", [PROJ, P])
        temp = sb("temp", [PROJ, 1])
        tscale = sb("tscale", [PROJ, 1])
        wq1 = sb("wq1", [P, H1 * D1])
        bq1 = sb("bq1", [P, 4])
        wkv1 = sb("wkv1", [P, 2 * H1 * D1])
        wo1 = sb("wo1", [P, 4, P])
        ln_g = sb("ln_g", [P, 1])
        ln_b = sb("ln_b", [P, 1])
        wr = sb("wr", [P, E])
        br = sb("br", [P, E])
        b1s = sb("b1s", [P, 2, HC])
        b2c = sb("b2c", [P, E])
        gates = sb("gates", [P, 4])
        tg = sb("tg", [P, 4])

        x_in = sb("x_in", [P, 2, P])
        ctx_a = sb("ctx_a", [P, 2, P])
        ctx_c = sb("ctx_c", [P, 2, P])
        mcol8 = sb("mcol8", [P, 2], U8)
        mrow8 = sb("mrow8", [1, 2, P], U8)
        mcol = sb("mcol", [P, 2])
        mrow = sb("mrow", [1, 2, P], BF16)
        xb = sb("xb", [P, 2, P])
        stats = sb("stats", [P, 4, 6])
        mv = sb("mv", [P, 4, 2])
        vr = sb("vr", [P, 4])
        vr2 = sb("vr2", [P, 4])
        rstd = sb("rstd", [P, 4])
        xn = sb("xn", [P, 4, P])
        xnT = sb("xnT", [P, 4, P])
        qkv = sb("qkv", [P, 2, 3 * P])
        prod_qk = sb("prod_qk", [P, H0 * H0 * D0])
        prod_av = sb("prod_av", [P, H0 * H0 * D0])
        s0 = sb("s0", [P, H0 * H0])
        s0m = sb("s0m", [P, H0 * H0])
        e0 = sb("e0", [P, H0 * H0])
        mx0 = sb("mx0", [P, H0])
        sum0 = sb("sum0", [P, H0])
        rs0 = sb("rs0", [P, H0])
        o0 = sb("o0", [P, P])
        o0n = sb("o0n", [P, P])
        o0T = sb("o0T", [P, P])
        x1 = sb("x1", [P, 2, P])
        x1b = sb("x1b", [P, 2, P])
        pj = sb("pj", [P, 2, PROJ + 2 * NR])
        sq = sb("sq", [P, PROJ])
        ss = sb("ss", [P, 2])
        ssm = sb("ssm", [P, 1])
        rn = sb("rn", [P, 1])
        lgB = sb("lgB", [P, NR])
        mxB = sb("mxB", [P, 1])
        dlB = sb("dlB", [P, NR])
        exB = sb("exB", [P, NR])
        exw = sb("exw", [P, NR])
        smB = sb("smB", [P, 1])
        rsB = sb("rsB", [P, 1])
        kk = sb("kk", [P, NR])
        km = sb("km", [P, 1])
        oh15 = sb("oh15", [P, NR])
        dw = sb("dw", [P, NR])
        dwT = sb("dwT", [NR, P])
        x2 = sb("x2", [P, 2, P])
        qT = sb("qT", [P, 2, 4, P])
        kT = sb("kT", [P, 2, 4, P])
        v1 = sb("v1", [P, 2, H1, D1 + 1])
        mx1 = sb("mx1", [P, H1])
        m_r1 = sb("m_r1", [P, H1])
        m_r2 = sb("m_r2", [P, H1])
        m_split = sb("m_split", [P, 3 * H1], BF16)
        mT = sb("mT", [3 * H1, 2, P], BF16)
        pT = sb("pT", [P, H1, P])
        rs1 = sb("rs1", [P, H1])
        o1 = sb("o1", [P, H1, D1])
        o1T = sb("o1T", [P, 4, P])
        x3 = sb("x3", [P, B, P])
        lgD = sb("lgD", [P, E])
        top8 = sb("top8", [P, 8])
        idx8 = sb("idx8", [P, 8], U32)
        idxf = sb("idxf", [P, 2])
        first = sb("first", [P, E])
        chosen = sb("chosen", [P, E])
        chosenb = sb("chosenb", [P, E], BF16)
        dlD = sb("dlD", [P, E])
        exD = sb("exD", [P, E])
        smD = sb("smD", [P, 1])
        rsD = sb("rsD", [P, 1])
        gD = sb("gD", [P, E])
        gate = sb("gate", [P, E])
        slot = sb("slot", [P, E])
        disp = sb("disp", [P, E, CAP])
        comb = sb("comb", [P, E, CAP])
        bufT = sb("bufT", [P, E, B * CAP])
        yT = sb("yT", [P, B, E, CAP])
        combT = sb("combT", [HALF, B, 2, P])
        w1s = sb("w1s", [P, 2, HID])
        w2s = sb("w2s", [P, 2, HC, P])
        hT = sb("hT", [P, 2, HC, B * CAP // 2])
        yTs = sb("yTs", [P, 2, ES])
        ys = sb("ys", [HALF, 2, 2, P])
        combs = sb("combs", [HALF, 2, 2, P])
        o_out = sb("o_out", [P, 2, P])

        psX, psQ, psB, psD = bank("psX"), bank("psQ"), bank("psB"), bank("psD")
        K0, K1, K2, K3 = bank("K0"), bank("K1"), bank("K2"), bank("K3")

        s_const = sem("s_const")
        s_tanh = sem("s_tanh")
        s_setup_pool = sem("s_setup_pool")
        s_setup_dve = sem("s_setup_dve")
        s_setup_pe = sem("s_setup_pe")
        s_setup_act = sem("s_setup_act")
        ln_stats, ln_mv, ln_v1, ln_v2, ln_rstd = (sem(n) for n in ("ln_stats", "ln_mv", "ln_v1", "ln_v2", "ln_rstd"))
        ln_xn, ln_turned, ln_xnT = sem("ln_xn"), sem("ln_turned"), sem("ln_xnT")
        x_loaded = [sem("x_loaded0"), sem("x_loaded1")]
        ctxa_loaded = [sem("ctxa_loaded0"), sem("ctxa_loaded1")]
        ctxc_loaded = [sem("ctxc_loaded0"), sem("ctxc_loaded1")]
        mask_loaded = [sem("mask_loaded0"), sem("mask_loaded1")]
        names = ("xb_ready qkv_mm qkv_ready qk_prod s0_ready mx0_ready s0m_ready e0_ready sum0_ready rs0_ready av_prod "
                 "o0_ready o0n_ready o0_turned o0T_ready y0_mm x1_ready "
                 "ffn0_mm pj_ready x1b_ready ss_ready ssm_ready rn_ready lgB_ready mxB_ready dlB_ready exB_ready exw_ready "
                 "smB_ready rsB_ready kk_ready km_ready oh15_ready dw_ready dw_turned dwT_ready res0_mm x2_ready "
                 "qT_mm kT_mm v_mm qT_ready kT_ready v_ready mcol_ready mrow_ready s1_mm mx1_ready m1_ready mr1_ready "
                 "m2_ready mr2_ready msplit_ready m_turned mT_ready "
                 "sT_mm0 sT_mm1 p_ready0 p_ready1 pv_mm rs1_ready o1_ready o1_turned o1T_ready y1_mm x3_ready "
                 "router_mm lgD_ready top_ready idx_ready idxf_ready first_ready chosen_ready chosenb_ready dlD_ready "
                 "exD_ready rsD_ready gD_ready gate_ready pos_mm slot_ready disp_ready comb_ready disp_mm comb_turned "
                 "bufT_ready combT_ready").split()
        S = {n: sem(n) for n in names}

        N_CONST = 34

        def done(eng, s, k):
            if isinstance(k, int):
                k = min(k, B - 1)
                if k < 0:
                    return
            eng.wait_ge(s, k + 1)

        def step_done(eng, s, t):
            if isinstance(t, int) and t < 0:
                return
            eng.wait_ge(s, t + 1)

        def loaded(eng, sems, i, par, lag):
            eng.wait_ge(sems[(par - lag) % 2], 16 * (i + (par - lag) // 2 + 1))

        def live(t, stage):
            return (not isinstance(t, int)) or 0 <= t - stage < B

        def ln_slots(t):
            on = [n for n, st in enumerate(LN_STAGES) if live(t, st)]
            return on[0], on[-1] + 1

        def steps(eng, body):
            lo = STAGES + 1
            hi = B
            for t in range(lo):
                body(t // 2, t % 2, t)
            with eng.Fori(lo // 2, hi // 2) as i:
                body(i, 0, 2 * i)
                body(i, 1, 2 * i + 1)
            for t in range(hi, STEPS):
                body(t // 2, t % 2, t)

        ln_in = {}

        def ln_input(n, i, par):
            st = LN_STAGES[n]
            if st == DD:
                k = 2 * i + par - DD
                return x3[:, k, :] if isinstance(k, int) else x3[:, ds(k, 1), :].rearrange("p a c -> p (a c)")
            return {A1: x_in, B1: x1, C1: x2}[st][:, (par - st) % 2, :]

        def x3_at(k):
            return x3[:, k, :] if isinstance(k, int) else x3[:, ds(k, 1), :].rearrange("p a c -> p (a c)")

        def bc(ap, axis, n):
            ap = ap.unsqueeze(axis)
            shape = list(ap.shape)
            shape[axis] = n
            return ap.broadcast_to(shape)

        E_LOOP = E // 2
        HB = B * CAP // 2
        e_w_loaded = [sem("e_w_loaded0"), sem("e_w_loaded1")]
        e_h_mm = [sem("e_h_mm0"), sem("e_h_mm1")]
        e_h_ready = [sem("e_h_ready0"), sem("e_h_ready1")]
        e_y_mm = [sem("e_y_mm0"), sem("e_y_mm1")]
        e_y_ready = [sem("e_y_ready0"), sem("e_y_ready1")]
        f_yTs, f_turned, f_ys, f_mm, f_out = sem("f_yTs"), sem("f_turned"), sem("f_ys"), sem("f_mm"), sem("f_out")
        f_combs = sem("f_combs")
        f_stored = [sem("f_stored0"), sem("f_stored1")]
        block = ctx.enter_context(nc.Block())

        consts = [
            (ident[:, :], a["ident"]), (identb[:, :], a["identb"]), (before[:, :], a["before"]),
            (minus_head[:, :, :], a["minus_head"]), (ones_row[:, :], a["ones_row"]), (iota8[:, :], a["iota8"]),
            (iota_slot[:, :], a["iota_slot"]), (key15[:, :], a["key15"]), (share15[:, :], a["share15"]),
            (ln_mul[:, :], a["ln_mul"]), (ln_add[:, :], a["ln_add"]),
            (wqkv0[:, :], a["wqkv0T"]), (bqkv0[:, :], a["bqkv0"].partition_broadcast(P)),
            (wo0[:, :], a["wo0T"]), (bo0[:, :], a["bo0"].partition_broadcast(P)),
            (wffn0[:, 0:P], a["w0T"]), (wffn0[:, P:P + PROJ], a["wp0T"]), (wffn0[:, P + PROJ + NR:], a["wd0T"]),
            (bffn0[:, 0:PROJ], a["bp0"].partition_broadcast(P)), (wu0[:, :], a["wu0T"]), (wp0[:, :], a["wp0"]),
            (sim15[:, :], a["sim15"]), (bpcol[:, :], a["bp0"].rearrange("(p o) -> p o", o=1)),
            (temp[:, :], a["temp"].partition_broadcast(PROJ)),
            (wq1[:, :], a["wq1"]), (wkv1[:, :], a["wkv1"]), (wo1[:, :, :], a["wo1"].rearrange("(c p) n -> p c n", p=P)),
            (ln_g[:, :], a["ln_g"].rearrange("(p o) -> p o", o=1)), (ln_b[:, :], a["ln_b"].rearrange("(p o) -> p o", o=1)),
            (wr[:, :], a["wr"]), (br[:, :], a["br"].partition_broadcast(P)),
            (b2c[:, :], a["b2T"]),
            (gates[:, 0:2], a["g_xattn"].partition_broadcast(P)), (gates[:, 2:4], a["g_ffn"].partition_broadcast(P)),
        ]

        assert N_CONST == len(consts)

        @block.sync
        def _(sp):
            for dst, src in consts:
                sp.dma_start(dst, src).then_inc(s_const, 16)

            def load(i, par, t):
                def sample(dram, k):
                    return dram[k] if isinstance(k, int) else dram[ds(k, 1)].rearrange("a p c -> (a p) c")

                if live(t, A1):
                    done(sp, S["xb_ready"], t - 2)
                    step_done(sp, ln_xn, t - 2)
                    sp.dma_start(x_in[:, par, :], sample(a["x"], t)).then_inc(x_loaded[par], 16)
                    done(sp, S["qkv_mm"], t - 2)
                    sp.dma_start(ctx_a[:, par, :], sample(a["ctxT"], t)).then_inc(ctxa_loaded[par], 16)
                if live(t, C1):
                    k, p = t - C1, (par - C1) % 2
                    done(sp, S["kT_mm"], k - 2)
                    done(sp, S["v_mm"], k - 2)
                    done(sp, S["mcol_ready"], k - 2)
                    done(sp, S["mrow_ready"], k - 2)
                    sp.dma_start(ctx_c[:, p, :], sample(a["ctxT"], k)).then_inc(ctxc_loaded[p], 16)
                    mk = a["mask"][k] if isinstance(k, int) else a["mask"][ds(k, 1)].rearrange("a p -> (a p)")
                    sp.dma_start(mcol8[:, p:p + 1], mk.rearrange("(p o) -> p o", o=1)).then_inc(mask_loaded[p], 16)
                    sp.dma_start(mrow8[:, p, :], mk.rearrange("(o p) -> o p", o=1)).then_inc(mask_loaded[p], 16)

            steps(sp, load)

            def weights(i, e, p, n):
                if not (isinstance(e, int) and e < 2):
                    sp.wait_ge(e_h_mm[1], HC * (n - 1))
                    sp.wait_ge(e_y_mm[1], n - 1)
                    sp.wait_ge(e_h_ready[1], HC * (n - 1))
                w1 = a["W1"][e] if isinstance(e, int) else a["W1"][ds(e, 1)].rearrange("a p c -> (a p) c")
                b1 = a["b1T"][e] if isinstance(e, int) else a["b1T"][ds(e, 1)].rearrange("a p c -> (a p) c")
                w2 = a["W2"][e] if isinstance(e, int) else a["W2"][ds(e, 1)].rearrange("a p c -> (a p) c")
                sp.dma_start(w1s[:, p, :], w1).then_inc(e_w_loaded[p], 16)
                sp.dma_start(b1s[:, p, :], b1).then_inc(e_w_loaded[p], 16)
                sp.dma_start(w2s[:, p, :, :], w2.rearrange("(c p) n -> p c n", p=P)).then_inc(e_w_loaded[p], 16)

            weights(0, 0, 0, 0)
            weights(0, 1, 1, 1)
            with sp.Fori(1, E_LOOP) as i:
                weights(i, 2 * i, 0, 2 * i)
                weights(i, 2 * i + 1, 1, 2 * i + 1)

            def store(i, p, k):
                sp.wait_ge(f_out, k + 1)
                o = out[k] if isinstance(k, int) else out[ds(k, 1)].rearrange("a p c -> (a p) c")
                sp.dma_start(o, o_out[:, p, :]).then_inc(f_stored[p], 16)

            with sp.Fori(0, B // 2) as i:
                store(i, 0, 2 * i)
                store(i, 1, 2 * i + 1)
            for p in range(2):
                sp.wait_ge(f_stored[p], 16 * (B // 2))

        @block.gpsimd
        def _(pool):
            nc.gpsimd.memset(minus_half[:, :], -0.5).then_inc(s_setup_pool, 1)
            nc.gpsimd.memset(ones32[:, :], 1.0).then_inc(s_setup_pool, 1)
            nc.gpsimd.memset(v1[:, 0, :, D1:D1 + 1], 1.0).then_inc(s_setup_pool, 1)
            nc.gpsimd.memset(v1[:, 1, :, D1:D1 + 1], 1.0).then_inc(s_setup_pool, 1)
            nc.gpsimd.memset(zeros8[:, :], 0.0).then_inc(s_setup_pool, 1)
            pool.wait_ge(s_const, 16 * N_CONST)
            nc.gpsimd.tensor_tensor(simsq[:, :], sim15[:, :], sim15[:, :], ALU.mult).then_inc(s_setup_pool, 1)
            pool.wait_ge(s_setup_dve, 1)
            pool.wait_ge(s_setup_pool, 6)
            nc.gpsimd.tensor_tensor(simrn[:, :], simrn[:, :], minus_half[0:PROJ, 0:NR], ALU.pow).then_inc(s_setup_pool, 1)

            def step(i, par, t):
                lo, hi = ln_slots(t)
                step_done(pool, ln_mv, t)
                nc.gpsimd.tensor_tensor(vr[:, lo:hi], mv[:, lo:hi, 1], ln_mul[:, lo:hi], ALU.mult).then_inc(ln_v1, 1)
                pool.wait_ge(ln_v1, t + 1)
                nc.gpsimd.tensor_tensor(vr2[:, lo:hi], vr[:, lo:hi], ln_add[:, lo:hi], ALU.add).then_inc(ln_v2, 1)
                pool.wait_ge(ln_v2, t + 1)
                step_done(pool, ln_xn, t - 1)
                nc.gpsimd.tensor_tensor(rstd[:, lo:hi], vr2[:, lo:hi], minus_half[:, lo:hi], ALU.pow).then_inc(ln_rstd, 1)
                if live(t, B2):
                    k = t - B2
                    done(pool, S["ssm_ready"], k)
                    done(pool, S["lgB_ready"], k - 1)
                    nc.gpsimd.tensor_tensor(rn[:, :], ssm[:, :], minus_half[:, 0:1], ALU.pow).then_inc(S["rn_ready"], 1)
                if live(t, A1):
                    loaded(pool, x_loaded, i, par, A1)
                    done(pool, S["x1_ready"], t - 2)
                    nc.gpsimd.tensor_tensor(xb[:, par, :], x_in[:, par, :], bo0[:, :], ALU.add).then_inc(S["xb_ready"], 1)
                if live(t, A2):
                    k, p = t - A2, (par - A2) % 2
                    done(pool, S["e0_ready"], k)
                    done(pool, S["qkv_ready"], k)
                    done(pool, S["o0_ready"], k - 1)
                    pav = prod_av[:, :].rearrange("p (h d g) -> p h d g", h=H0, d=D0)
                    ev = bc(e0[:, :].rearrange("p (h g) -> p h g", h=H0), 2, D0)
                    vv = bc(qkv[:, p, 2 * P:3 * P].rearrange("p (g d) -> p d g", g=H0), 1, H0)
                    nc.gpsimd.tensor_tensor(pav, ev, vv, ALU.mult).then_inc(S["av_prod"], 1)
                if live(t, C1):
                    k = t - C1
                    done(pool, S["mx1_ready"], k)
                    done(pool, S["m_turned"], k - 1)
                    nc.gpsimd.tensor_tensor(m_split[:, 0:H1], mx1[:, :], zeros8[:, :], ALU.add).then_inc(S["m1_ready"], 1)
                    done(pool, S["m1_ready"], k)
                    nc.gpsimd.tensor_tensor(m_r1[:, :], mx1[:, :], m_split[:, 0:H1], ALU.subtract).then_inc(S["mr1_ready"], 1)
                    done(pool, S["mr1_ready"], k)
                    nc.gpsimd.tensor_tensor(m_split[:, H1:2 * H1], m_r1[:, :], zeros8[:, :], ALU.add).then_inc(S["m2_ready"], 1)
                    done(pool, S["m2_ready"], k)
                    nc.gpsimd.tensor_tensor(m_r2[:, :], m_r1[:, :], m_split[:, H1:2 * H1],
                                            ALU.subtract).then_inc(S["mr2_ready"], 1)
                    done(pool, S["mr2_ready"], k)
                    nc.gpsimd.tensor_tensor(m_split[:, 2 * H1:3 * H1], m_r2[:, :], zeros8[:, :], ALU.add).then_inc(S["msplit_ready"], 1)

            steps(pool, step)

        @block.scalar
        def _(act):
            act.wait_ge(s_const, 16 * N_CONST)
            nc.scalar.activation(tg[:, :], gates[:, :], ACT.Tanh).then_inc(s_tanh, 1)
            act.wait_ge(s_setup_dve, 2)
            nc.scalar.activation(tscale[:, :], temp[:, :], ACT.Exp).then_inc(s_setup_act, 1)

            def step(i, par, t):
                if live(t, C2):
                    k, p = t - C2, (par - C2) % 2
                    done(act, S["mcol_ready"], k)
                    done(act, S["sT_mm0"], k)
                    done(act, S["pv_mm"], k - 1)
                    nc.scalar.activation(pT[:, 0::2, :], K0[:, :].rearrange("p (h n) -> p h n", h=4), ACT.Exp,
                                         bias=mcol[:, p:p + 1]).then_inc(S["p_ready0"], 1)
                    done(act, S["sT_mm1"], k)
                    nc.scalar.activation(pT[:, 1::2, :], K1[:, :].rearrange("p (h n) -> p h n", h=4), ACT.Exp,
                                         bias=mcol[:, p:p + 1]).then_inc(S["p_ready1"], 1)
                lo, hi = ln_slots(t)
                step_done(act, ln_turned, t)
                nc.scalar.copy(xnT[:, lo:hi, :], psX[:, lo * P:hi * P].rearrange("p (s n) -> p s n", n=P)).then_inc(ln_xnT, 1)
                if live(t, C1):
                    k, p = t - C1, (par - C1) % 2
                    done(act, S["qT_mm"], k)
                    done(act, S["sT_mm1"], k - 2)
                    for c in range(4):
                        q = nc.scalar.activation(qT[:, p, c, :], K0[:, c * P:(c + 1) * P], ACT.Identity, bias=bq1[:, c:c + 1])
                    q.then_inc(S["qT_ready"], 1)
                    done(act, S["kT_mm"], k)
                    nc.scalar.copy(kT[:, p, :, :], K1[:, :].rearrange("p (c n) -> p c n", c=4)).then_inc(S["kT_ready"], 1)
                if live(t, A2):
                    k = t - A2
                    done(act, S["s0m_ready"], k)
                    done(act, S["av_prod"], k - 1)
                    done(act, S["sum0_ready"], k - 1)
                    nc.scalar.activation(e0[:, :], s0m[:, :], ACT.Exp, scale=float(D0) ** -0.5).then_inc(S["e0_ready"], 1)
                if live(t, C2):
                    k = t - C2
                    done(act, S["o1_turned"], k)
                    done(act, S["y1_mm"], k - 1)
                    nc.scalar.copy(o1T[:, :, :], psX[:, :].rearrange("p (c n) -> p c n", c=4)).then_inc(S["o1T_ready"], 1)
                if live(t, B1):
                    k, p = t - B1, (par - B1) % 2
                    done(act, S["pj_ready"], k)
                    done(act, S["ssm_ready"], k - 2)
                    nc.scalar.activation(sq[:, :], pj[:, p, 0:PROJ], ACT.Square, accum_out=ss[:, p:p + 1]).then_inc(S["ss_ready"], 1)
                if live(t, B2):
                    k = t - B2
                    done(act, S["dlB_ready"], k)
                    done(act, S["exw_ready"], k - 1)
                    nc.scalar.activation(exB[:, :], dlB[:, :], ACT.Exp).then_inc(S["exB_ready"], 1)
                if live(t, DD):
                    k = t - DD
                    done(act, S["dlD_ready"], k)
                    done(act, S["gD_ready"], k - 1)
                    nc.scalar.activation(exD[:, :], dlD[:, :], ACT.Exp, accum_out=smD[:, :]).then_inc(S["exD_ready"], 1)
                if live(t, C1):
                    k, p = t - C1, (par - C1) % 2
                    done(act, S["v_mm"], k)
                    done(act, S["pv_mm"], k - 2)
                    nc.scalar.copy(v1[:, p, :, 0:D1], K0[:, :].rearrange("p (h d) -> p h d", h=H1)).then_inc(S["v_ready"], 1)
                if live(t, B2):
                    k = t - B2
                    done(act, S["dw_turned"], k)
                    done(act, S["res0_mm"], k - 1)
                    nc.scalar.copy(dwT[:, :], psB[0:NR, 256:256 + P]).then_inc(S["dwT_ready"], 1)
                if live(t, C1):
                    k, p = t - C1, (par - C1) % 2
                    done(act, S["m_turned"], k)
                    done(act, S["sT_mm1"], k - 2)
                    nc.scalar.copy(mT[:, p, :], K2[:, :].bitcast(BF16)[0:3 * H1, 0:P]).then_inc(S["mT_ready"], 1)
                if live(t, A2):
                    k = t - A2
                    done(act, S["o0_turned"], k)
                    done(act, S["y0_mm"], k - 1)
                    if live(t, DD):
                        done(act, S["disp_mm"], t - DD)
                        done(act, S["comb_turned"], t - DD)
                    nc.scalar.copy(o0T[:, :], psQ[:, 384:512]).then_inc(S["o0T_ready"], 1)
                if live(t, DD):
                    k = t - DD
                    if not live(t, A2):
                        done(act, S["disp_mm"], k)
                        done(act, S["comb_turned"], k)
                    b = bufT[:, :, k * CAP:(k + 1) * CAP] if isinstance(k, int) else bufT[:, :, ds(k * CAP, CAP)]
                    nc.scalar.copy(b, psD[:, 0:ES].rearrange("p (e s) -> p e s", e=E)).then_inc(S["bufT_ready"], 1)
                    c = combT[:, k, :, :] if isinstance(k, int) else combT[:, ds(k, 1), :, :].rearrange("p a c n -> p (a c) n")
                    nc.scalar.copy(c, psD[0:HALF, 256:512].rearrange("p (c n) -> p c n", c=2)).then_inc(S["combT_ready"], 1)

            steps(act, step)

            def expert(i, n, p):
                act.wait_ge(e_w_loaded[p], 48 * (i + 1))
                for half in range(2):
                    for c in range(HC):
                        act.wait_ge(e_h_mm[half], HC * n + c + 1)
                        if not (isinstance(n, int) and n == 0):
                            act.wait_ge(e_y_mm[half], n)
                        nc.scalar.activation(hT[:, half, c, :], (K0, K1, K2, K3)[c][:, 0:HB], ACT.Relu,
                                             bias=b1s[:, p, c:c + 1]).then_inc(e_h_ready[half], 1)

            expert(0, 0, 0)
            expert(0, 1, 1)
            with act.Fori(1, E_LOOP) as i:
                expert(i, 2 * i, 0)
                expert(i, 2 * i + 1, 1)

            def combine(i, p, k):
                act.wait_ge(f_turned, k + 1)
                if not isinstance(i, int):
                    act.wait_ge(f_mm, k - 1)
                nc.scalar.copy(ys[:, p, :, :], (K0, K1)[p][0:HALF, 0:2 * P].rearrange("p (c n) -> p c n", c=2)).then_inc(f_ys, 1)

            combine(0, 0, 0)
            combine(0, 1, 1)
            with act.Fori(1, B // 2) as i:
                combine(i, 0, 2 * i)
                combine(i, 1, 2 * i + 1)

        @block.tensor
        def _(pe):
            mm = nc.tensor.matmul
            pe.wait_ge(s_const, 16 * N_CONST)
            pe.wait_ge(s_setup_pool, 6)
            mm(psB[0:PROJ, 0:NR], ones32[:, :], simsq[:, :], start=True, stop=True).then_inc(s_setup_pe, 1)
            pe.wait_ge(s_setup_dve, 3)
            mm(psQ[:, 0:NR], wp0[:, :], sim15[:, :], start=True, stop=True).then_inc(s_setup_pe, 1)
            mm(psX[:, 0:NR], bpwide[:, :], sim15[:, :], start=True, stop=True).then_inc(s_setup_pe, 1)
            for c in range(4):
                last = mm(psD[:, c:c + 1], wq1[:, c * P:(c + 1) * P], ln_b[:, :], start=True, stop=True)
            last.then_inc(s_setup_pe, 1)
            pe.wait_ge(s_setup_dve, 9)

            def step(i, par, t):
                lo, hi = ln_slots(t)
                if live(t, C2):
                    k, p = t - C2, (par - C2) % 2
                    done(pe, S["v_ready"], k)
                    done(pe, S["kT_ready"], k)
                    done(pe, S["qT_ready"], k)
                    done(pe, S["mT_ready"], k)
                    for h in range(H1):
                        r = slice(D1 * (h % 2), D1 * (h % 2) + D1)
                        mm((K0, K1)[h % 2][:, (h // 2) * P:(h // 2 + 1) * P], kT[r, p, h // 2, :], qT[r, p, h // 2, :],
                           start=(h < 2), stop=False, skip_group_check=True)
                    for b in range(2):
                        for j in range(4):
                            last = mm((K0, K1)[b][:, j * P:(j + 1) * P], minus_head[:, 2 * j + b, :], mT[:, p, :],
                                      start=False, stop=(j == 3), skip_group_check=True)
                        last.then_inc(S[f"sT_mm{b}"], 1)
                step_done(pe, ln_xn, t)
                done(pe, S["x3_ready"], t - 1 - C2)
                for n in range(lo, hi):
                    last = nc.tensor.transpose(psX[:, n * P:(n + 1) * P], xn[:, n, :], ident[:, :])
                last.then_inc(ln_turned, 1)
                if live(t, C2):
                    k, p = t - C2, (par - C2) % 2
                    done(pe, S["m_turned"], k)
                    done(pe, S["mT_ready"], k)
                    for h in range(H1):
                        if h < 2:
                            done(pe, S[f"p_ready{h}"], k)
                        o = (K2, K3)[h // 4][:, (h % 4) * (D1 + 1):(h % 4 + 1) * (D1 + 1)]
                        last = mm(o, pT[:, h, :], v1[:, p, h, :], start=True, stop=True)
                    last.then_inc(S["pv_mm"], 1)
                step_done(pe, ln_xnT, t)
                if live(t, A1):
                    loaded(pe, ctxa_loaded, i, par, A1)
                    done(pe, S["x1_ready"], t - 2)
                    mm(psQ[:, 0:P], xnT[:, 0, :], wqkv0[:, 0:P], start=True, stop=True)
                    mm(psQ[:, P:3 * P], ctx_a[:, par, :], wqkv0[:, P:3 * P], start=True, stop=True).then_inc(S["qkv_mm"], 1)
                if live(t, C1):
                    k, p = t - C1, (par - C1) % 2
                    done(pe, S["p_ready0"], k - 1)
                    for c in range(4):
                        last = mm(K0[:, c * P:(c + 1) * P], wq1[:, c * P:(c + 1) * P], xnT[:, 2, :], start=True, stop=True)
                    last.then_inc(S["qT_mm"], 1)
                    loaded(pe, ctxc_loaded, i, par, C1)
                    done(pe, S["p_ready1"], k - 1)
                    for c in range(4):
                        last = mm(K1[:, c * P:(c + 1) * P], wkv1[:, c * P:(c + 1) * P], ctx_c[:, p, :], start=True, stop=True)
                    last.then_inc(S["kT_mm"], 1)
                if live(t, DD):
                    k = t - DD
                    done(pe, S["combT_ready"], k - 1)
                    mm(psD[:, 0:E], xnT[:, 3, :], wr[:, :], start=True, stop=True).then_inc(S["router_mm"], 1)
                if live(t, B1):
                    k = t - B1
                    done(pe, S["x2_ready"], k - 2)
                    mm(psB[:, 0:P + PROJ + 2 * NR], xnT[:, 1, :], wffn0[:, :], start=True, stop=True).then_inc(S["ffn0_mm"], 1)
                if live(t, C2):
                    k = t - C2
                    done(pe, S["o1_ready"], k)
                    for c in range(4):
                        last = nc.tensor.transpose(psX[:, c * P:(c + 1) * P], o1[:, 2 * c:2 * c + 2, :], ident[:, :])
                    last.then_inc(S["o1_turned"], 1)
                if live(t, C1):
                    k, p = t - C1, (par - C1) % 2
                    done(pe, S["qT_ready"], k)
                    done(pe, S["kT_ready"], k)
                    done(pe, S["mrow_ready"], k)
                    done(pe, S["o1_ready"], k - 1)
                    for h in range(H1):
                        r = slice(D1 * (h % 2), D1 * (h % 2) + D1)
                        mm((K2, K3)[h % 2][:, (h // 2) * P:(h // 2 + 1) * P], qT[r, p, h // 2, :], kT[r, p, h // 2, :],
                           start=(h < 2), stop=False, skip_group_check=True)
                    for b in range(2):
                        last = mm((K2, K3)[b][:, :], ones_row[:, :], bc(mrow[:, p, :], 1, 4), start=False, stop=True,
                                  skip_group_check=True)
                    last.then_inc(S["s1_mm"], 1)
                    mm(K0[:, :], ctx_c[:, p, :], wkv1[:, H1 * D1:], start=True, stop=True).then_inc(S["v_mm"], 1)
                if live(t, DD):
                    k = t - DD
                    done(pe, S["chosenb_ready"], k)
                    mm(psD[:, E:2 * E], before[:, :], chosenb[:, :], start=True, stop=True).then_inc(S["pos_mm"], 1)
                if live(t, C2):
                    k = t - C2
                    done(pe, S["o1T_ready"], k)
                    for c in range(4):
                        last = mm(psX[:, 0:P], o1T[:, c, :], wo1[:, c, :], start=(c == 0), stop=(c == 3))
                    last.then_inc(S["y1_mm"], 1)
                if live(t, B2):
                    k = t - B2
                    done(pe, S["dw_ready"], k)
                    done(pe, S["x1b_ready"], t - B1)
                    nc.tensor.transpose(psB[0:NR, 256:256 + P], dw[:, :], ident[:, :]).then_inc(S["dw_turned"], 1)
                    done(pe, S["dwT_ready"], k)
                    mm(psB[:, 384:512], dwT[:, :], wu0[:, :], start=True, stop=True).then_inc(S["res0_mm"], 1)
                if live(t, C1):
                    k = t - C1
                    done(pe, S["msplit_ready"], k)
                    nc.tensor.transpose(K2[:, :].bitcast(BF16)[0:3 * H1, 0:P], m_split[:, :],
                                        identb[:, :]).then_inc(S["m_turned"], 1)
                if live(t, DD):
                    k = t - DD
                    done(pe, S["slot_ready"], k)
                    done(pe, S["disp_ready"], k)
                    mm(psD[:, 0:ES], xn[:, 3, :], disp[:, :, :].rearrange("p e s -> p (e s)"), start=True,
                       stop=True).then_inc(S["disp_mm"], 1)
                    done(pe, S["comb_ready"], k)
                    cm = comb[:, :, :].rearrange("p e s -> p (e s)")
                    for c in range(2):
                        last = nc.tensor.transpose(psD[0:HALF, 256 + c * P:256 + (c + 1) * P], cm[:, c * HALF:(c + 1) * HALF],
                                                   ident[:, :])
                    last.then_inc(S["comb_turned"], 1)
                if live(t, A2):
                    k = t - A2
                    done(pe, S["o0n_ready"], k)
                    done(pe, S["qkv_ready"], t)
                    nc.tensor.transpose(psQ[:, 384:512], o0n[:, :], ident[:, :]).then_inc(S["o0_turned"], 1)
                    done(pe, S["o0T_ready"], k)
                    mm(psQ[:, 0:P], o0T[:, :], wo0[:, :], start=True, stop=True).then_inc(S["y0_mm"], 1)

            steps(pe, step)

            pe.wait_ge(S["bufT_ready"], B)
            pe.wait_ge(S["combT_ready"], B)

            def up(e, p, n, half):
                for c in range(HC):
                    if half == 1 or not (isinstance(n, int) and n == 0):
                        pe.wait_ge(e_h_ready[1 - half], HC * (n - 1 + half) + c + 1)
                    rhs = bufT[:, e, half * HB:(half + 1) * HB] if isinstance(e, int) else \
                        bufT[:, ds(e, 1), half * HB:(half + 1) * HB].rearrange("p a n -> p (a n)")
                    mm((K0, K1, K2, K3)[c][:, 0:HB], w1s[:, p, c * P:(c + 1) * P], rhs, start=True,
                       stop=True).then_inc(e_h_mm[half], 1)

            def down(e, p, n, half):
                if not (isinstance(n, int) and n == 0):
                    pe.wait_ge(e_y_ready[half], n)
                pe.wait_ge(e_h_ready[half], HC * (n + 1))
                for c in range(HC):
                    last = mm((psX, psQ)[half][:, 0:HB], w2s[:, p, c, :], hT[:, half, c, :], start=(c == 0), stop=(c == HC - 1))
                last.then_inc(e_y_mm[half], 1)

            def expert(i, e, p):
                pe.wait_ge(e_w_loaded[p], 48 * (i + 1))
                up(e, p, e, 0)
                up(e, p, e, 1)
                down(e, p, e, 0)
                down(e, p, e, 1)

            expert(0, 0, 0)
            expert(0, 1, 1)
            with pe.Fori(1, E_LOOP) as i:
                expert(i, 2 * i, 0)
                expert(i, 2 * i + 1, 1)

            def combine(i, p, k):
                pe.wait_ge(f_yTs, k + 1)
                if not isinstance(i, int):
                    pe.wait_ge(f_ys, k - 1)
                for c in range(2):
                    last = nc.tensor.transpose((K0, K1)[p][0:HALF, c * P:(c + 1) * P], yTs[:, p, c * HALF:(c + 1) * HALF],
                                               ident[:, :])
                last.then_inc(f_turned, 1)
                pe.wait_ge(f_ys, k + 1)
                pe.wait_ge(f_combs, k + 1)
                if not isinstance(i, int):
                    pe.wait_ge(f_out, k - 1)
                for c in range(2):
                    last = mm((K2, K3)[p][:, 0:P], combs[:, p, c, :], ys[:, p, c, :], start=(c == 0), stop=(c == 1))
                last.then_inc(f_mm, 1)

            combine(0, 0, 0)
            combine(0, 1, 1)
            with pe.Fori(1, B // 2) as i:
                combine(i, 0, 2 * i)
                combine(i, 1, 2 * i + 1)

        @block.vector
        def _(dve):
            tt, ts = nc.vector.tensor_tensor, nc.vector.tensor_scalar
            dve.wait_ge(s_const, 16 * N_CONST)
            dve.wait_ge(s_setup_pe, 1)
            ts(simrn[:, :], psB[0:PROJ, 0:NR], 1e-24, None, ALU.max).then_inc(s_setup_dve, 1)
            ts(temp[:, :], temp[:, :], CLAMP, None, ALU.min).then_inc(s_setup_dve, 1)
            dve.wait_ge(s_setup_pool, 7)
            dve.wait_ge(s_setup_act, 1)
            nc.vector.scalar_tensor_tensor(sim15[:, :], simrn[:, :], tscale[:, 0:1], sim15[:, :], ALU.mult, ALU.mult)
            nc.vector.tensor_copy(bpwide[:, :], bpcol[:, 0:1].broadcast_to([PROJ, P])).then_inc(s_setup_dve, 1)
            dve.wait_ge(s_tanh, 1)
            ts(wo0[:, :], wo0[:, :], tg[:, 0:1], None, ALU.mult)
            ts(bo0[:, :], bo0[:, :], tg[:, 0:1], None, ALU.mult)
            ts(wffn0[:, 0:P], wffn0[:, 0:P], tg[:, 2:3], None, ALU.mult)
            ts(wu0[:, :], wu0[:, :], tg[0:NR, 2:3], None, ALU.mult)
            ts(wo1[:, :, :], wo1[:, :, :], tg[:, 1:2], None, ALU.mult)
            nc.vector.memset(bffn0[:, PROJ + NR:], 0.0).then_inc(s_setup_dve, 1)
            dve.wait_ge(s_setup_pe, 2)
            nc.vector.tensor_copy(wffn0[:, P + PROJ:P + PROJ + NR], psQ[:, 0:NR]).then_inc(s_setup_dve, 1)
            dve.wait_ge(s_setup_pe, 3)
            nc.vector.tensor_copy(bffn0[:, PROJ:PROJ + NR], psX[:, 0:NR]).then_inc(s_setup_dve, 1)
            dve.wait_ge(s_setup_pe, 4)
            ts(bq1[:, :], psD[:, 0:4], float(D1) ** -0.5, None, ALU.mult).then_inc(s_setup_dve, 1)
            ts(wq1[:, :], wq1[:, :], ln_g[:, 0:1], float(D1) ** -0.5, ALU.mult, ALU.mult).then_inc(s_setup_dve, 1)
            nc.vector.memset(first[:, :], 0.0).then_inc(s_setup_dve, 1)

            def step(i, par, t):
                lo, hi = ln_slots(t)
                if live(t, A1):
                    loaded(dve, x_loaded, i, par, A1)
                if live(t, B1):
                    done(dve, S["x1_ready"], t - B1)
                if live(t, C1):
                    done(dve, S["x2_ready"], t - C1)
                if live(t, DD):
                    done(dve, S["x3_ready"], t - DD)
                for n in range(lo, hi):
                    last = nc.vector.bn_stats(stats[:, n, :], ln_input(n, i, par))
                last.then_inc(ln_stats, 1)
                dve.wait_ge(ln_stats, t + 1)
                step_done(dve, ln_v1, t - 1)
                if live(t, B2):
                    k, p = t - B2, (par - B2) % 2
                    done(dve, S["ss_ready"], k)
                    done(dve, S["rn_ready"], k - 1)
                    ts(ssm[:, :], ss[:, p:p + 1], 1e-24, None, ALU.max).then_inc(S["ssm_ready"], 1)
                for n in range(lo, hi):
                    last = nc.vector.bn_aggr(mv[:, n, :], stats[:, n, :])
                last.then_inc(ln_mv, 1)
                if live(t, A2):
                    k, p = t - A2, (par - A2) % 2
                    done(dve, S["qkv_ready"], k)
                    pqk = prod_qk[:, :].rearrange("p (h g d) -> p h g d", h=H0, g=H0)
                    qv = bc(qkv[:, p, 0:P].rearrange("p (h d) -> p h d", h=H0), 2, H0)
                    kv = bc(qkv[:, p, P:2 * P].rearrange("p (g d) -> p g d", g=H0), 1, H0)
                    tt(pqk, qv, kv, ALU.mult).then_inc(S["qk_prod"], 1)
                step_done(dve, ln_rstd, t)
                dve.wait_ge(ln_mv, t + 1)
                step_done(dve, ln_turned, t - 1)
                done(dve, S["disp_mm"], t - 1 - DD)
                for n in range(lo, hi):
                    last = ts(xn[:, n, :], ln_input(n, i, par), mv[:, n, 0:1], rstd[:, n:n + 1], ALU.subtract, ALU.mult)
                last.then_inc(ln_xn, 1)
                if live(t, A2):
                    k = t - A2
                    done(dve, S["qk_prod"], k)
                    nc.vector.reduce_sum(s0[:, :], prod_qk[:, :].rearrange("p (s d) -> p s d", d=D0), X).then_inc(S["s0_ready"], 1)
                    done(dve, S["s0_ready"], k)
                    s3 = s0[:, :].rearrange("p (h g) -> p h g", h=H0)
                    nc.vector.reduce_max(mx0[:, :], s3, X).then_inc(S["mx0_ready"], 1)
                    done(dve, S["mx0_ready"], k)
                    done(dve, S["e0_ready"], k - 1)
                    tt(s0m[:, :].rearrange("p (h g) -> p h g", h=H0), s3, bc(mx0[:, :], 2, H0),
                       ALU.subtract).then_inc(S["s0m_ready"], 1)
                if live(t, C2):
                    k = t - C2
                    done(dve, S["pv_mm"], k)
                    done(dve, S["o1_turned"], k - 1)
                    kv2 = [kb[:, 0:4 * (D1 + 1)].rearrange("p (h d) -> p h d", h=4) for kb in (K2, K3)]
                    for n in range(2):
                        last = nc.vector.reciprocal(rs1[:, 4 * n:4 * n + 4], kv2[n][:, :, D1])
                    last.then_inc(S["rs1_ready"], 1)
                    done(dve, S["rs1_ready"], k)
                    for n in range(2):
                        last = tt(o1[:, 4 * n:4 * n + 4, :], kv2[n][:, :, 0:D1], bc(rs1[:, 4 * n:4 * n + 4], 2, D1), ALU.mult)
                    last.then_inc(S["o1_ready"], 1)
                if live(t, A1):
                    done(dve, S["qkv_mm"], t)
                    done(dve, S["av_prod"], t - 2)
                    tt(qkv[:, par, :], psQ[:, 0:3 * P], bqkv0[:, :], ALU.add).then_inc(S["qkv_ready"], 1)
                if live(t, B1):
                    k, p = t - B1, (par - B1) % 2
                    done(dve, S["ffn0_mm"], k)
                    done(dve, S["ss_ready"], k - 2)
                    tt(pj[:, p, :], psB[:, P:P + PROJ + 2 * NR], bffn0[:, :], ALU.add).then_inc(S["pj_ready"], 1)
                if live(t, C1):
                    k, p = t - C1, (par - C1) % 2
                    dve.wait_ge(mask_loaded[p], 32 * (i + (par - C1) // 2 + 1))
                    done(dve, S["p_ready1"], k - 2)
                    ts(mcol[:, p:p + 1], mcol8[:, p:p + 1], -MASKED, MASKED, ALU.mult, ALU.add).then_inc(S["mcol_ready"], 1)
                    done(dve, S["s1_mm"], k - 2)
                    ts(mrow[:, p, :], mrow8[:, p, :], -MASKED, MASKED, ALU.mult, ALU.add).then_inc(S["mrow_ready"], 1)
                if live(t, DD):
                    k = t - DD
                    done(dve, S["router_mm"], k)
                    tt(lgD[:, :], psD[:, 0:E], br[:, :], ALU.add).then_inc(S["lgD_ready"], 1)
                    done(dve, S["lgD_ready"], k)
                if live(t, B1):
                    k, p = t - B1, (par - B1) % 2
                    done(dve, S["ffn0_mm"], k)
                    tt(x1b[:, p, :], x1[:, p, :], psB[:, 0:P], ALU.add).then_inc(S["x1b_ready"], 1)
                if live(t, DD):
                    k = t - DD
                    nc.vector.max(top8[:, :], lgD[:, :]).then_inc(S["top_ready"], 1)
                    done(dve, S["top_ready"], k)
                    done(dve, S["exD_ready"], k - 1)
                    ts(dlD[:, :], lgD[:, :], top8[:, 0:1], None, ALU.subtract).then_inc(S["dlD_ready"], 1)
                    nc.vector.max_index(idx8[:, :], top8[:, :], lgD[:, :]).then_inc(S["idx_ready"], 1)
                    done(dve, S["idx_ready"], k)
                    nc.vector.tensor_copy(idxf[:, :], idx8[:, 0:2]).then_inc(S["idxf_ready"], 1)
                    done(dve, S["idxf_ready"], k)
                    ts(first[:, :], iota8[:, :], idxf[:, 0:1], None, ALU.is_equal).then_inc(S["first_ready"], 1)
                    done(dve, S["first_ready"], k)
                    nc.vector.scalar_tensor_tensor(chosen[:, :], iota8[:, :], idxf[:, 1:2], first[:, :], ALU.is_equal,
                                                   ALU.add).then_inc(S["chosen_ready"], 1)
                    done(dve, S["chosen_ready"], k)
                    done(dve, S["pos_mm"], k - 1)
                    nc.vector.tensor_copy(chosenb[:, :], chosen[:, :]).then_inc(S["chosenb_ready"], 1)
                if live(t, A2):
                    k = t - A2
                    done(dve, S["e0_ready"], k)
                    nc.vector.reduce_sum(sum0[:, :], e0[:, :].rearrange("p (h g) -> p h g", h=H0), X).then_inc(S["sum0_ready"], 1)
                    done(dve, S["sum0_ready"], k)
                    nc.vector.reciprocal(rs0[:, :], sum0[:, :]).then_inc(S["rs0_ready"], 1)
                if live(t, B2):
                    k, p = t - B2, (par - B2) % 2
                    done(dve, S["rn_ready"], k)
                    done(dve, S["pj_ready"], k)
                    ts(lgB[:, :], pj[:, p, PROJ:PROJ + NR], rn[:, 0:1], None, ALU.mult).then_inc(S["lgB_ready"], 1)
                    done(dve, S["lgB_ready"], k)
                    nc.vector.reduce_max(mxB[:, :], lgB[:, :], X).then_inc(S["mxB_ready"], 1)
                    done(dve, S["mxB_ready"], k)
                    done(dve, S["exB_ready"], k - 1)
                    ts(dlB[:, :], lgB[:, :], mxB[:, 0:1], None, ALU.subtract).then_inc(S["dlB_ready"], 1)
                    done(dve, S["dlB_ready"], k)
                    nc.vector.scalar_tensor_tensor(kk[:, :], dlB[:, :], 0.0, key15[:, :], ALU.is_ge,
                                                   ALU.mult).then_inc(S["kk_ready"], 1)
                    done(dve, S["kk_ready"], k)
                    nc.vector.reduce_max(km[:, :], kk[:, :], X).then_inc(S["km_ready"], 1)
                if live(t, C1):
                    k = t - C1
                    done(dve, S["s1_mm"], k)
                    done(dve, S["mr1_ready"], k - 1)
                    for n in range(2):
                        last = nc.vector.reduce_max(mx1[:, n::2], (K2, K3)[n][:, :].rearrange("p (h n) -> p h n", h=4), X)
                    last.then_inc(S["mx1_ready"], 1)
                if live(t, B2):
                    k, p = t - B2, (par - B2) % 2
                    done(dve, S["exB_ready"], k)
                    tt(exw[:, :], exB[:, :], share15[:, :], ALU.mult).then_inc(S["exw_ready"], 1)
                    done(dve, S["exw_ready"], k)
                    nc.vector.reduce_sum(smB[:, :], exw[:, :], X).then_inc(S["smB_ready"], 1)
                    done(dve, S["smB_ready"], k)
                    nc.vector.reciprocal(rsB[:, :], smB[:, :]).then_inc(S["rsB_ready"], 1)
                    done(dve, S["rsB_ready"], k)
                    done(dve, S["km_ready"], k)
                    ts(oh15[:, :], kk[:, :], km[:, 0:1], rsB[:, 0:1], ALU.is_equal, ALU.mult).then_inc(S["oh15_ready"], 1)
                    done(dve, S["oh15_ready"], k)
                    done(dve, S["dw_turned"], k - 1)
                    tt(dw[:, :], oh15[:, :], pj[:, p, PROJ + NR:], ALU.mult).then_inc(S["dw_ready"], 1)
                if live(t, DD):
                    k = t - DD
                    done(dve, S["exD_ready"], k)
                    nc.vector.reciprocal(rsD[:, :], smD[:, :]).then_inc(S["rsD_ready"], 1)
                    done(dve, S["rsD_ready"], k)
                    ts(gD[:, :], exD[:, :], rsD[:, 0:1], tg[:, 3:4], ALU.mult, ALU.mult).then_inc(S["gD_ready"], 1)
                    done(dve, S["gD_ready"], k)
                    tt(gate[:, :], gD[:, :], chosen[:, :], ALU.mult).then_inc(S["gate_ready"], 1)
                    done(dve, S["pos_mm"], k)
                    nc.vector.scalar_tensor_tensor(slot[:, :], psD[:, E:2 * E], 1.0, chosen[:, :], ALU.add,
                                                   ALU.mult).then_inc(S["slot_ready"], 1)
                    done(dve, S["slot_ready"], k)
                    done(dve, S["disp_mm"], k - 1)
                    tt(disp[:, :, :], bc(iota_slot[:, :], 1, E), bc(slot[:, :], 2, CAP), ALU.is_equal).then_inc(S["disp_ready"], 1)
                    done(dve, S["disp_ready"], k)
                    done(dve, S["gate_ready"], k)
                    done(dve, S["comb_turned"], k - 1)
                    tt(comb[:, :, :], disp[:, :, :], bc(gate[:, :], 2, CAP), ALU.mult).then_inc(S["comb_ready"], 1)
                if live(t, C2):
                    k, p = t - C2, (par - C2) % 2
                    done(dve, S["y1_mm"], k)
                    tt(x3_at(k), x2[:, p, :], psX[:, 0:P], ALU.add).then_inc(S["x3_ready"], 1)
                if live(t, A2):
                    k = t - A2
                    done(dve, S["av_prod"], k)
                    nc.vector.reduce_sum(o0[:, :], prod_av[:, :].rearrange("p (c g) -> p c g", g=H0), X).then_inc(S["o0_ready"], 1)
                    done(dve, S["o0_ready"], k)
                    done(dve, S["rs0_ready"], k)
                    done(dve, S["o0_turned"], k - 1)
                    tt(o0n[:, :].rearrange("p (h d) -> p h d", h=H0), o0[:, :].rearrange("p (h d) -> p h d", h=H0),
                       bc(rs0[:, :], 2, D0), ALU.mult).then_inc(S["o0n_ready"], 1)
                if live(t, B2):
                    k, p = t - B2, (par - B2) % 2
                    done(dve, S["res0_mm"], k)
                    done(dve, S["x3_ready"], k - 2)
                    tt(x2[:, p, :], x1b[:, p, :], psB[:, 384:512], ALU.add).then_inc(S["x2_ready"], 1)
                if live(t, A2):
                    k, p = t - A2, (par - A2) % 2
                    done(dve, S["y0_mm"], k)
                    done(dve, S["xb_ready"], k)
                    tt(x1[:, p, :], xb[:, p, :], psQ[:, 0:P], ALU.add).then_inc(S["x1_ready"], 1)

            steps(dve, step)

            def expert(e):
                for half in range(2):
                    dve.wait_ge(e_y_mm[half], e + 1)
                    r = slice(half * B // 2, (half + 1) * B // 2)
                    dst = yT[:, r, e, :] if isinstance(e, int) else yT[:, r, ds(e, 1), :].rearrange("p b a s -> p b (a s)")
                    bias = b2c[:, e:e + 1] if isinstance(e, int) else b2c[:, ds(e, 1)]
                    ts(dst, (psX, psQ)[half][:, 0:HB].rearrange("p (b s) -> p b s", s=CAP), bias, None,
                       ALU.add).then_inc(e_y_ready[half], 1)

            with dve.Fori(0, E) as e:
                expert(e)

            dve.wait_ge(S["combT_ready"], B)
            dve.wait_ge(e_y_ready[1], E)

            def gather(i, p, k):
                if not (isinstance(k, int) and k < 2):
                    dve.wait_ge(f_turned, k - 1)
                src = yT[:, k, :, :] if isinstance(k, int) else yT[:, ds(k, 1), :, :].rearrange("p a e s -> p (a e) s")
                ts(yTs[:, p, :].rearrange("p (e s) -> p e s", e=E), src, 1.0, None, ALU.mult).then_inc(f_yTs, 1)
                if not (isinstance(k, int) and k < 2):
                    dve.wait_ge(f_mm, k - 1)
                src = combT[:, k, :, :] if isinstance(k, int) else combT[:, ds(k, 1), :, :].rearrange("p a c n -> p (a c) n")
                ts(combs[:, p, :, :], src, 1.0, None, ALU.mult).then_inc(f_combs, 1)

            def finish(i, p, k):
                dve.wait_ge(f_mm, k + 1)
                if not (isinstance(k, int) and k < 2):
                    dve.wait_ge(f_stored[p], 16 * i)
                tt(o_out[:, p, :], x3_at(k), (K2, K3)[p][:, 0:P], ALU.add).then_inc(f_out, 1)

            gather(0, 0, 0)
            gather(0, 1, 1)
            finish(0, 0, 0)
            gather(1, 0, 2)
            finish(0, 1, 1)
            with dve.Fori(1, B // 2 - 1) as i:
                gather(i, 1, 2 * i + 1)
                finish(i, 0, 2 * i)
                gather(i, 0, 2 * i + 2)
                finish(i, 1, 2 * i + 1)
            gather(B // 2 - 1, 1, B - 1)
            finish(B // 2 - 1, 0, B - 2)
            finish(B // 2 - 1, 1, B - 1)


def kernel(**inputs):
    import numpy as np
    import concourse.bacc as bacc
    from concourse.bass_utils import run_bass_kernel_spmd

    def t(name):
        return np.ascontiguousarray(np.asarray(inputs[name]).T)

    f32 = np.float32
    import ml_dtypes
    bf16 = ml_dtypes.bfloat16
    arange = np.arange
    arrays = {
        "x": np.asarray(inputs["x"]),
        "ctxT": np.ascontiguousarray(np.asarray(inputs["ctx_1024"]).transpose(0, 2, 1)),
        "mask": np.asarray(inputs["mask_BxS2_bk0"]),
        "g_xattn": np.asarray(inputs["g_xattn"]), "g_ffn": np.asarray(inputs["g_ffn"]),
        "wqkv0T": np.concatenate([t("L0_xattn_Wq"), t("L0_xattn_Wk"), t("L0_xattn_Wv")], axis=1),
        "bqkv0": np.concatenate([np.asarray(inputs[f"L0_xattn_b{c}"]) for c in "qkv"]),
        "wo0T": t("L0_xattn_Wo"), "bo0": np.asarray(inputs["L0_xattn_bo"]),
        "w0T": t("L0_ffn_W"), "wp0T": t("L0_ffn_Wp"), "wp0": np.asarray(inputs["L0_ffn_Wp"]),
        "bp0": np.asarray(inputs["L0_ffn_bp"]), "temp": np.asarray(inputs["L0_ffn_temp"]),
        "sim15": np.repeat(np.asarray(inputs["L0_ffn_sim"]), RANKS, axis=1),
        "wd0T": np.concatenate([t(f"L0_ffn_Wd{n}") for n in range(4)], axis=1),
        "wu0T": np.concatenate([t(f"L0_ffn_Wu{n}") for n in range(4)], axis=0),
        "ln_g": np.asarray(inputs["L1_xattn_ln_g"]), "ln_b": np.asarray(inputs["L1_xattn_ln_b"]),
        "wq1": np.asarray(inputs["L1_xattn_Wq"]), "wkv1": np.asarray(inputs["L1_xattn_Wkv"]),
        "wo1": np.asarray(inputs["L1_xattn_Wo"]),
        "wr": np.asarray(inputs["L1_ffn_Wr"]), "br": np.asarray(inputs["L1_ffn_br"]),
        "W1": np.asarray(inputs["L1_ffn_W1"]), "W2": np.asarray(inputs["L1_ffn_W2"]),
        "b1T": np.ascontiguousarray(np.asarray(inputs["L1_ffn_b1"]).reshape(E, HC, P).transpose(0, 2, 1)),
        "b2T": t("L1_ffn_b2"),
        "ident": np.eye(P, dtype=f32), "identb": np.eye(P, dtype=f32).astype(bf16),
        "before": (arange(P)[:, None] < arange(P)[None, :]).astype(bf16),
        "minus_head": np.broadcast_to(-(arange(3 * H1)[:, None, None] % H1 == arange(H1)[None, :, None]).astype(f32),
                                      (3 * H1, H1, P)).astype(bf16),
        "ones_row": np.ones((1, P), f32).astype(bf16),
        "iota8": np.broadcast_to(arange(E, dtype=f32), (P, E)).copy(),
        "iota_slot": np.broadcast_to(arange(1, CAP + 1, dtype=f32), (P, CAP)).copy(),
        "key15": np.broadcast_to(np.repeat(arange(4, 0, -1).astype(f32), RANKS), (P, NR)).copy(),
        "share15": np.broadcast_to(np.repeat(1.0 / np.array(RANKS, f32), RANKS).astype(f32), (P, NR)).copy(),
        "ln_mul": np.broadcast_to(np.array([1, 1, 1 + 1e-5, 1], f32), (P, 4)).copy(),
        "ln_add": np.broadcast_to(np.array([1e-5, 1e-5, 1e-10, 1e-5], f32), (P, 4)).copy(),
    }
    nc = bacc.Bacc("TRN2", target_bir_lowering=False, num_devices=1)
    feed, args = {}, {}
    for name, arr in arrays.items():
        feed[f"in_{name}"] = arr
        args[name] = nc.dram_tensor(f"in_{name}", arr.shape, mybir.dt.from_np(arr.dtype), kind="ExternalInput").ap()
    out = nc.dram_tensor("out_0", (B, P, P), F32, kind="ExternalOutput").ap()
    build(nc, args, out)
    r = run_bass_kernel_spmd(nc, [feed], core_ids=[0])
    return r.results[0]["out_0"]
```

```python
from contextlib import ExitStack

import concourse.bass as bass
from concourse import mybir

ALU = mybir.AluOpType
ACT = mybir.ActivationFunctionType
F32 = mybir.dt.float32
BF16 = mybir.dt.bfloat16
U8 = mybir.dt.uint8
U32 = mybir.dt.uint32
X = mybir.AxisListType.X
ds = bass.ds

P = 128
B = 32
H0, D0 = 16, 8
H1, D1 = 8, 64
RANKS = (1, 2, 4, 8)
NR = sum(RANKS)
PROJ = 32
NG = NR + len(RANKS)
PJ = PROJ + NG + NR
H_DVE = 12
E = 8
HID = 512
HC = HID // P
CAP = 20
ES = E * CAP
HALF = ES // 2
MASKED = -float(2.0 ** 100)
CLAMP = 4.605170185988092


def layout(widths):
    at, out = 0, {}
    for name, w in widths:
        out[name] = (at, w)
        at += w
    return out, at


LAYOUT_A, WIDTH_A = layout([("ident", P), ("iota8", E), ("iota_slot", CAP), ("key15", NR), ("ln_mul", 4),
                            ("ln_add", 4), ("wqkv0", 3 * P), ("wo0", P), ("wffn0", P + PJ), ("wr", E), ("b2c", E)])
LAYOUT_B, WIDTH_B = layout([("wq1", H1 * D1), ("wkv1", 2 * H1 * D1), ("wo1", 4 * P), ("ln_g", 1), ("ln_b", 1)])
BIAS_AT, BIASES = layout([("qkv0", 3 * P), ("bo0", P), ("ffn0", P + PJ), ("br", E), ("q1", H1 * D1)])

LAG = {
    "x_loaded": 0, "ctxa_loaded": 1, "xres_loaded": 3, "ctxc_loaded": 3, "ln_stats": 0, "ln_mv": 0, "ln_v2": 1,
    "ln_rstd": 1, "ln_shift": 1, "ln_xn": 0, "ln_turned": 2, "ln_xnT": 1, "qkv_mm": 2, "qkv_ready": 1, "qk_prod": 1,
    "qk_prod_rest": 1, "s0_ready": 1, "mx0_ready": 1, "s0m_ready": 1, "e0_ready": 1, "sum0_ready": 2, "rs0_ready": 2,
    "av_prod0": 2, "av_prod1": 2, "o0_ready0": 2, "o0_ready1": 2, "o0n_ready": 2, "o0_turned": 3, "o0T_ready": 2,
    "y0_mm": 3, "x1_ready": 2, "ffn0_mm": 4, "pj_ready": 3, "ss_ready": 3, "ssm_ready": 3, "rn_ready": 4, "mxB_ready": 3,
    "dlB_ready": 3, "kk_ready": 3, "km_ready": 3, "exB_ready": 3, "rsB_ready": 3, "oh15_ready": 3, "dw_ready": 3,
    "dw_turned": 4, "dwT_ready": 3, "res0_mm": 4, "x2_ready": 3, "qT_mm": 5, "qT_ready": 4, "kT_mm": 3, "kT_ready": 2,
    "v_mm": 4, "v_ready": 4, "s1_mm0": 5, "s1_mm1": 5, "nmx_ready0": 4, "nmx_ready1": 4, "p1_ready0": 4, "p1_ready1": 4,
    "p_turned0": 5, "p_turned1": 5, "pT_ready0": 4, "pT_ready1": 4, "pv_mm0": 6, "pv_mm1": 6, "rs1_ready0": 5,
    "rs1_ready1": 5, "o1_ready0": 5, "o1_ready1": 5, "o1_turned": 6, "o1T_ready": 5, "y1_mm": 6, "x3_ready": 5,
    "router_mm": 7, "top_ready": 6, "idx_ready": 7, "idxf_ready": 7, "first_ready": 7, "chosen_ready": 7, "exD_ready": 7,
    "rsD_ready": 7, "gate_ready": 8, "pos_mm": 8, "slot_ready": 7, "disp_ready": 7, "comb_ready": 8, "disp_mm": 9,
    "bufT_ready": 8, "comb_turned": 10, "combT_ready": 9,
}
LN_LAG = (0, 2, 3, 5)
LN_ROUNDS = B + LN_LAG[3]
BANK = {
    "ln_turned": 7, "qkv_mm": 0, "o0_turned": 1, "y0_mm": 7, "ffn0_mm": 4, "dw_turned": 0, "qT_mm": 0, "kT_mm": 6,
    "v_mm": 6, "s1_mm0": 5, "s1_mm1": 3, "p_turned0": 0, "p_turned1": 4, "pv_mm0": 2, "pv_mm1": 4, "o1_turned": 2,
    "y1_mm": 7, "router_mm": 2, "pos_mm": 3, "disp_mm": 1, "comb_turned": 5,
}
MAX_LAG = max(LAG.values())
STEPS = B + MAX_LAG


def build(nc, a, out):
    ctx = ExitStack()
    with ctx:
        def sb(name, shape, dt=F32):
            return ctx.enter_context(nc.sbuf_tensor(name, shape, dt))

        def bank(name):
            return ctx.enter_context(nc.psum_tensor(name, [P, 512], F32))

        def sem(name):
            return ctx.enter_context(nc.semaphore(name))

        pack_a = sb("pack_a", [P, WIDTH_A])
        pack_b = sb("pack_b", [P, WIDTH_B])
        pack_h = sb("pack_h", [P, P], BF16)

        def part(pack, layout, name):
            o, w = layout[name]
            return pack[:, o:o + w]

        ident, iota8, iota_slot, key15, ln_mul, ln_add, wqkv0, wo0, wffn0, wr, b2c = (
            part(pack_a, LAYOUT_A, n) for n in
            "ident iota8 iota_slot key15 ln_mul ln_add wqkv0 wo0 wffn0 wr b2c".split())
        wq1, wkv1, wo1f, ln_g, ln_b = (part(pack_b, LAYOUT_B, n) for n in "wq1 wkv1 wo1 ln_g ln_b".split())
        wo1 = wo1f.rearrange("p (c n) -> p c n", c=4)
        before = pack_h
        ones_rows = sb("ones_rows", [3, P], BF16)
        ones32 = sb("ones32", [PROJ, PROJ])
        minus_half = sb("minus_half", [P, NG])
        wu0 = sb("wu0", [NR, P])
        wp0 = sb("wp0", [PROJ, P])
        sim19 = sb("sim19", [PROJ, NG])
        simsq = sb("simsq", [PROJ, NG])
        simrn = sb("simrn", [PROJ, NG])
        bpcol = sb("bpcol", [PROJ, 1])
        bpwide = sb("bpwide", [PROJ, P])
        temp = sb("temp", [PROJ, 1])
        tscale = sb("tscale", [PROJ, 1])
        gates = sb("gates", [P, 4])
        tg = sb("tg", [P, 4])
        bias_rows = sb("bias_rows", [3, BIASES], BF16)
        lnb_wide = sb("lnb_wide", [P, 3])

        x_in = sb("x_in", [P, 2, P])
        ctx_a = sb("ctx_a", [P, 2, P])
        ctx_c = sb("ctx_c", [P, 2, P])
        mask8 = sb("mask8", [1, B * P], U8)
        mask_rows = sb("mask_rows", [1, B * P], BF16)
        x_res = sb("x_res", [P, 2, P])
        stats = sb("stats", [P, 4, 6])
        mv = sb("mv", [P, 4, 2])
        vr = sb("vr", [P, 4])
        vr2 = sb("vr2", [P, 4])
        rstd = sb("rstd", [P, 4])
        shift = sb("shift", [P, 4])
        xn = sb("xn", [P, 2, 4, P])
        xnT = sb("xnT", [P, 2, 4, P])
        qkv = sb("qkv", [P, 2, 3 * P])
        prod_qk = sb("prod_qk", [P, H0 * H0 * D0])
        prod_av = sb("prod_av", [P, H0 * H0 * D0])
        s0 = sb("s0", [P, H0 * H0])
        s0m = sb("s0m", [P, H0 * H0])
        e0 = sb("e0", [P, 2, H0 * H0])
        mx0 = sb("mx0", [P, H0])
        sum0 = sb("sum0", [P, H0])
        rs0 = sb("rs0", [P, H0])
        o0 = sb("o0", [P, P])
        o0n = sb("o0n", [P, P])
        o0T = sb("o0T", [P, P])
        x1 = sb("x1", [P, 2, P])
        pj = sb("pj", [P, 2, PJ])
        sq = sb("sq", [P, PROJ])
        ss = sb("ss", [P, 1])
        ssm = sb("ssm", [P, 1])
        rn = sb("rn", [P, 1])
        mxB = sb("mxB", [P, 1])
        dlB = sb("dlB", [P, NG])
        exB = sb("exB", [P, NG - NR])
        smB = sb("smB", [P, 1])
        rsB = sb("rsB", [P, 1])
        kk = sb("kk", [P, NR])
        km = sb("km", [P, 1])
        oh15 = sb("oh15", [P, NR])
        dw = sb("dw", [P, NR])
        dwT = sb("dwT", [NR, P])
        x2 = sb("x2", [P, 2, P])
        qT = sb("qT", [P, 2, 4, P])
        kT = sb("kT", [P, 2, 4, P])
        v1 = sb("v1", [P, 2, H1, D1 + 1])
        nmx1 = sb("nmx1", [P, 2, 4])
        p1 = sb("p1", [P, 2, 4, P])
        pT = sb("pT", [P, 2, 4, P])
        rs1 = sb("rs1", [P, 2, 4])
        o1 = sb("o1", [P, H1, D1])
        o1T = sb("o1T", [P, 4, P])
        x3 = sb("x3", [P, B, P])
        top8 = sb("top8", [P, 8])
        idx8 = sb("idx8", [P, 8], U32)
        idxf = sb("idxf", [P, 2])
        first = sb("first", [P, E])
        chosen = sb("chosen", [P, E], BF16)
        dlD = sb("dlD", [P, E])
        exD = sb("exD", [P, E])
        smD = sb("smD", [P, 1])
        rsD = sb("rsD", [P, 1])
        gate = sb("gate", [P, E])
        slot = sb("slot", [P, E])
        disp = sb("disp", [P, E, CAP])
        comb = sb("comb", [P, E, CAP])
        bufT = sb("bufT", [P, E, B * CAP])
        scratch = bufT[0:3, :, :].rearrange("p e n -> p (e n)")
        bias = scratch[:, 0:BIASES]
        bias_r = [scratch[:, n * BIASES:(n + 1) * BIASES] for n in (1, 2)]
        bias_p = [scratch[:, 3 * BIASES + n * (BIASES // 2):3 * BIASES + (n + 1) * (BIASES // 2)].bitcast(BF16)
                  for n in range(2)]
        bias_p.append(scratch[:, BIASES:BIASES + BIASES // 2].bitcast(BF16))
        yT = sb("yT", [P, B, E, CAP])
        combT = sb("combT", [HALF, B, 2, P])
        b1s = sb("b1s", [P, 2, HC])
        w1s = sb("w1s", [P, 2, HID])
        w2s = sb("w2s", [P, 2, HC, P])
        hT = sb("hT", [P, 2, HC, B * CAP // 2])
        yTs = sb("yTs", [P, 2, ES])
        ys = sb("ys", [HALF, 2, 2, P])
        combs = sb("combs", [HALF, 2, 2, P])
        o_out = sb("o_out", [P, 2, P])

        banks = [bank(f"bank{n}") for n in range(8)]
        PB = {piece: banks[n] for piece, n in BANK.items()}
        K0, K1, K2, K3, psX, psQ, psB, psD = banks

        s_small = sem("s_small")
        s_late = sem("s_late")
        s_bias = sem("s_bias")
        s_tanh = sem("s_tanh")
        s_setup_pool = sem("s_setup_pool")
        s_setup_dve = sem("s_setup_dve")
        s_setup_pe = sem("s_setup_pe")
        s_setup_act = sem("s_setup_act")
        ln_stats, ln_mv, ln_v1, ln_v2, ln_rstd, ln_shift = (
            sem(n) for n in ("ln_stats", "ln_mv", "ln_v1", "ln_v2", "ln_rstd", "ln_shift"))
        ln_xn, ln_turned, ln_xnT = sem("ln_xn"), sem("ln_turned"), sem("ln_xnT")
        x_loaded = [sem("x_loaded0"), sem("x_loaded1")]
        ctxa_loaded = [sem("ctxa_loaded0"), sem("ctxa_loaded1")]
        ctxc_loaded = [sem("ctxc_loaded0"), sem("ctxc_loaded1")]
        xres_loaded = [sem("xres_loaded0"), sem("xres_loaded1")]
        S = {n: sem(n) for n in LAG if not n.startswith("ln_") and not n.endswith("_loaded")}

        def done(eng, s, k):
            if isinstance(k, int):
                k = min(k, B - 1)
                if k < 0:
                    return
            eng.wait_ge(s, k + 1)

        def ln_done(eng, s, r):
            if isinstance(r, int):
                r = min(r, LN_ROUNDS - 1)
                if r < 0:
                    return
            eng.wait_ge(s, r + 1)

        def loaded(eng, sems, i, par, lag):
            if isinstance(i, int) and not 0 <= 2 * i + par - lag < B:
                return
            eng.wait_ge(sems[(par - lag) % 2], 16 * (i + (par - lag) // 2 + 1))

        def bank_free(eng, t, latest, earlier):
            for s, k in latest + (earlier if isinstance(t, int) else []):
                (ln_done if s is ln_xnT else done)(eng, s, k)

        def live(t, piece):
            count = LN_ROUNDS if piece.startswith("ln_") else B
            return (not isinstance(t, int)) or 0 <= t - LAG[piece] < count

        def slot_live(r, n):
            return (not isinstance(r, int)) or 0 <= r - LN_LAG[n] < B

        def ln_slots(r):
            on = [n for n in range(4) if slot_live(r, n)]
            return on[0], on[-1] + 1

        def steps(eng, body, before_step=()):
            lo = MAX_LAG + 4 + MAX_LAG % 2
            hi = B
            for t in range(lo):
                if before_step and t == before_step[0]:
                    before_step[1]()
                body(t // 2, t % 2, t)
            with eng.Fori(lo // 2, hi // 2) as i:
                body(i, 0, 2 * i)
                body(i, 1, 2 * i + 1)
            for t in range(hi, STEPS):
                body(t // 2, t % 2, t)

        def x3_at(k):
            return x3[:, k, :] if isinstance(k, int) else x3[:, ds(k, 1), :].rearrange("p a c -> p (a c)")

        def ln_input(n, i, par, piece):
            if n == 3:
                return x3_at(2 * i + par - LAG[piece] - LN_LAG[3])
            return (x_in, x1, x2)[n][:, (par - LAG[piece] - LN_LAG[n]) % 2, :]

        def xn_of(n, par, piece):
            return xn[:, (par - LAG[piece] + LN_LAG[n]) % 2, n, :]

        def xnT_of(n, par, piece):
            return xnT[:, (par - LAG[piece] + LN_LAG[n]) % 2, n, :]

        def mask_row(k):
            row = mask_rows[:, k * P:(k + 1) * P] if isinstance(k, int) else mask_rows[:, ds(k * P, P)]
            return bc(row, 1, 4)

        def pv_bank(g):
            return PB[f"pv_mm{g}"][:, 0:4 * (D1 + 1)].rearrange("p (h d) -> p h d", h=4)

        def bc(ap, axis, n):
            ap = ap.unsqueeze(axis)
            shape = list(ap.shape)
            shape[axis] = n
            return ap.broadcast_to(shape)

        E_LOOP = E // 2
        HB = B * CAP // 2
        e_w_loaded = [sem("e_w_loaded0"), sem("e_w_loaded1")]
        e_h_mm = [sem("e_h_mm0"), sem("e_h_mm1")]
        e_h_ready = [sem("e_h_ready0"), sem("e_h_ready1")]
        e_y_mm = [sem("e_y_mm0"), sem("e_y_mm1")]
        e_y_ready = [sem("e_y_ready0"), sem("e_y_ready1")]
        f_yTs, f_turned, f_ys, f_mm, f_out = sem("f_yTs"), sem("f_turned"), sem("f_ys"), sem("f_mm"), sem("f_out")
        f_combs = sem("f_combs")
        f_stored = [sem("f_stored0"), sem("f_stored1")]
        block = ctx.enter_context(nc.Block())

        small = [
            (pack_a[:, :], a["pack_a"]), (gates[:, 0:2], a["g_xattn"].partition_broadcast(P)),
            (gates[:, 2:4], a["g_ffn"].partition_broadcast(P)), (bias[:, :], a["biases"].partition_broadcast(3)),
            (sim19[:, :], a["sim19"]), (temp[:, :], a["temp"].partition_broadcast(PROJ)), (wp0[:, :], a["wp0"]),
            (bpcol[:, :], a["bp0"].rearrange("(p o) -> p o", o=1)), (wu0[:, :], a["wu0T"]),
        ]
        late = [(mask8[:, :], a["mask"].rearrange("b p -> (b p)").rearrange("(o n) -> o n", o=1)),
                (pack_b[:, :], a["pack_b"]), (pack_h[:, :], a["before"])]

        @block.sync
        def _(sp):
            def sample(dram, k):
                return dram[k] if isinstance(k, int) else dram[ds(k, 1)].rearrange("a p c -> (a p) c")

            def step(i, par, t):
                if live(t, "ctxc_loaded"):
                    k, p = t - LAG["ctxc_loaded"], (par - LAG["ctxc_loaded"]) % 2
                    done(sp, S["v_mm"], k - 2)
                    sp.dma_start(ctx_c[:, p, :], sample(a["ctxT"], k)).then_inc(ctxc_loaded[p], 16)
                if live(t, "xres_loaded"):
                    k, p = t - LAG["xres_loaded"], (par - LAG["xres_loaded"]) % 2
                    sp.dma_start(x_res[:, p, :], sample(a["x"], k)).then_inc(xres_loaded[p], 16)
                if live(t, "x_loaded"):
                    k, p = t - LAG["x_loaded"], (par - LAG["x_loaded"]) % 2
                    ln_done(sp, ln_xn, k - 2)
                    sp.dma_start(x_in[:, p, :], sample(a["x"], k)).then_inc(x_loaded[p], 16)
                if live(t, "ctxa_loaded"):
                    k, p = t - LAG["ctxa_loaded"], (par - LAG["ctxa_loaded"]) % 2
                    sp.dma_start(ctx_a[:, p, :], sample(a["ctxT"], k)).then_inc(ctxa_loaded[p], 16)

            for dst, src in small:
                sp.dma_start(dst, src).then_inc(s_small, 16)
            steps(sp, step, (0, lambda: [sp.dma_start(dst, src).then_inc(s_late, 16) for dst, src in late]))

            def weights(i, e, p, n):
                if not (isinstance(e, int) and e < 2):
                    sp.wait_ge(e_h_mm[1], HC * (n - 1))
                    sp.wait_ge(e_y_mm[1], n - 1)
                    sp.wait_ge(e_h_ready[1], HC * (n - 1))
                w1 = a["W1"][e] if isinstance(e, int) else a["W1"][ds(e, 1)].rearrange("a p c -> (a p) c")
                b1 = a["b1T"][e] if isinstance(e, int) else a["b1T"][ds(e, 1)].rearrange("a p c -> (a p) c")
                w2 = a["W2"][e] if isinstance(e, int) else a["W2"][ds(e, 1)].rearrange("a p c -> (a p) c")
                sp.dma_start(w1s[:, p, :], w1).then_inc(e_w_loaded[p], 16)
                sp.dma_start(b1s[:, p, :], b1).then_inc(e_w_loaded[p], 16)
                sp.dma_start(w2s[:, p, :, :], w2.rearrange("(c p) n -> p c n", p=P)).then_inc(e_w_loaded[p], 16)

            weights(0, 0, 0, 0)
            weights(0, 1, 1, 1)
            with sp.Fori(1, E_LOOP) as i:
                weights(i, 2 * i, 0, 2 * i)
                weights(i, 2 * i + 1, 1, 2 * i + 1)

            def store(i, p, k):
                sp.wait_ge(f_out, k + 1)
                o = out[k] if isinstance(k, int) else out[ds(k, 1)].rearrange("a p c -> (a p) c")
                sp.dma_start(o, o_out[:, p, :]).then_inc(f_stored[p], 16)

            with sp.Fori(0, B // 2) as i:
                store(i, 0, 2 * i)
                store(i, 1, 2 * i + 1)
            for p in range(2):
                sp.wait_ge(f_stored[p], 16 * (B // 2))

        @block.gpsimd
        def _(pool):
            nc.gpsimd.memset(minus_half[:, :], -0.5).then_inc(s_setup_pool, 1)
            nc.gpsimd.memset(ones32[:, :], 1.0).then_inc(s_setup_pool, 1)
            nc.gpsimd.memset(v1[:, 0, :, D1:D1 + 1], 1.0).then_inc(s_setup_pool, 1)
            nc.gpsimd.memset(v1[:, 1, :, D1:D1 + 1], 1.0).then_inc(s_setup_pool, 1)
            nc.gpsimd.memset(ones_rows[:, :], 1.0).then_inc(s_setup_pool, 1)
            pool.wait_ge(s_small, 16 * len(small))
            nc.gpsimd.tensor_tensor(simsq[:, :], sim19[:, :], sim19[:, :], ALU.mult).then_inc(s_setup_pool, 1)
            pool.wait_ge(s_setup_dve, 1)
            pool.wait_ge(s_setup_pool, 6)
            nc.gpsimd.tensor_tensor(simrn[:, :], simrn[:, :], minus_half[0:PROJ, 0:NG], ALU.pow).then_inc(s_setup_pool, 1)

            def step(i, par, t):
                if live(t, "rn_ready"):
                    k = t - LAG["rn_ready"]
                    done(pool, S["ssm_ready"], k)
                    nc.gpsimd.tensor_tensor(rn[:, :], ssm[:, :], minus_half[:, 0:1], ALU.pow).then_inc(S["rn_ready"], 1)
                if live(t, "av_prod0"):
                    k, p = t - LAG["av_prod0"], (par - LAG["av_prod0"]) % 2
                    done(pool, S["e0_ready"], k)
                    h = slice(0 * H0 // 2, 1 * H0 // 2)
                    pav = prod_av[:, :].rearrange("p (h d g) -> p h d g", h=H0, d=D0)[:, h, :, :]
                    ev = bc(e0[:, p, :].rearrange("p (h g) -> p h g", h=H0)[:, h, :], 2, D0)
                    vv = bc(qkv[:, (par - LAG["av_prod0"]) % 2, 2 * P:3 * P].rearrange("p (g d) -> p d g", g=H0), 1, H0 // 2)
                    nc.gpsimd.tensor_tensor(pav, ev, vv, ALU.mult).then_inc(S["av_prod0"], 1)
                if live(t, "ln_v2"):
                    r = t - LAG["ln_v2"]
                    ln_done(pool, ln_mv, r)
                    lo, hi = ln_slots(r)
                    nc.gpsimd.tensor_tensor(vr[:, lo:hi], mv[:, lo:hi, 1], ln_mul[:, lo:hi], ALU.mult).then_inc(ln_v1, 1)
                    pool.wait_ge(ln_v1, r + 1)
                    nc.gpsimd.tensor_tensor(vr2[:, lo:hi], vr[:, lo:hi], ln_add[:, lo:hi], ALU.add).then_inc(ln_v2, 1)
                if live(t, "ln_rstd"):
                    r = t - LAG["ln_rstd"]
                    ln_done(pool, ln_v2, r)
                    lo, hi = ln_slots(r)
                    nc.gpsimd.tensor_tensor(rstd[:, lo:hi], vr2[:, lo:hi], minus_half[:, lo:hi], ALU.pow).then_inc(ln_rstd, 1)
                if live(t, "av_prod1"):
                    k, p = t - LAG["av_prod1"], (par - LAG["av_prod1"]) % 2
                    h = slice(1 * H0 // 2, 2 * H0 // 2)
                    pav = prod_av[:, :].rearrange("p (h d g) -> p h d g", h=H0, d=D0)[:, h, :, :]
                    ev = bc(e0[:, p, :].rearrange("p (h g) -> p h g", h=H0)[:, h, :], 2, D0)
                    vv = bc(qkv[:, (par - LAG["av_prod1"]) % 2, 2 * P:3 * P].rearrange("p (g d) -> p d g", g=H0), 1, H0 // 2)
                    nc.gpsimd.tensor_tensor(pav, ev, vv, ALU.mult).then_inc(S["av_prod1"], 1)
                if live(t, "comb_ready"):
                    k = t - LAG["comb_ready"]
                    done(pool, S["gate_ready"], k)
                    done(pool, S["comb_turned"], k - 1)
                    nc.gpsimd.tensor_tensor(comb[:, :, :], disp[:, :, :], bc(gate[:, :], 2, CAP), ALU.mult).then_inc(S["comb_ready"], 1)
                if live(t, "qk_prod_rest"):
                    k, p = t - LAG["qk_prod_rest"], (par - LAG["qk_prod_rest"]) % 2
                    done(pool, S["qkv_ready"], k)
                    h = slice(H_DVE, H0)
                    pqk = prod_qk[:, :].rearrange("p (h g d) -> p h g d", h=H0, g=H0)[:, h, :, :]
                    qv = bc(qkv[:, p, 0:P].rearrange("p (h d) -> p h d", h=H0)[:, h, :], 2, H0)
                    kv = bc(qkv[:, p, P:2 * P].rearrange("p (g d) -> p g d", g=H0), 1, h.stop - h.start)
                    nc.gpsimd.tensor_tensor(pqk, qv, kv, ALU.mult).then_inc(S["qk_prod_rest"], 1)
                if live(t, "o0n_ready"):
                    k, p = t - LAG["o0n_ready"], (par - LAG["o0n_ready"]) % 2
                    done(pool, S["o0_ready1"], k)
                    nc.gpsimd.tensor_tensor(o0n[:, :].rearrange("p (h d) -> p h d", h=H0), o0[:, :].rearrange("p (h d) -> p h d", h=H0),
                                            bc(rs0[:, :], 2, D0), ALU.mult).then_inc(S["o0n_ready"], 1)

            steps(pool, step)

        @block.scalar
        def _(act):
            act.wait_ge(s_small, 16 * len(small))
            nc.scalar.activation(tg[:, :], gates[:, :], ACT.Tanh).then_inc(s_tanh, 1)
            act.wait_ge(s_setup_dve, 2)
            nc.scalar.activation(tscale[:, :], temp[:, :], ACT.Exp).then_inc(s_setup_act, 1)

            def step(i, par, t):
                if live(t, "ln_xnT"):
                    r, p = t - LAG["ln_xnT"], (par - LAG["ln_xnT"]) % 2
                    ln_done(act, ln_turned, r)
                    lo, hi = ln_slots(r)
                    nc.scalar.copy(xnT[:, p, lo:hi, :], PB["ln_turned"][:, lo * P:hi * P].rearrange("p (s n) -> p s n", n=P)).then_inc(ln_xnT, 1)
                if live(t, "qkv_ready"):
                    k, p = t - LAG["qkv_ready"], (par - LAG["qkv_ready"]) % 2
                    done(act, S["qkv_mm"], k)
                    nc.scalar.copy(qkv[:, p, :], PB["qkv_mm"][:, 0:3 * P]).then_inc(S["qkv_ready"], 1)
                if live(t, "v_ready"):
                    k, p = t - LAG["v_ready"], (par - LAG["v_ready"]) % 2
                    nc.scalar.copy(v1[:, p, :, 0:D1], PB["v_mm"][:, :].rearrange("p (h d) -> p h d", h=H1)).then_inc(S["v_ready"], 1)
                if live(t, "o1T_ready"):
                    k, p = t - LAG["o1T_ready"], (par - LAG["o1T_ready"]) % 2
                    done(act, S["o1_turned"], k)
                    nc.scalar.copy(o1T[:, :, :], PB["o1_turned"][:, :].rearrange("p (c n) -> p c n", c=4)).then_inc(S["o1T_ready"], 1)
                if live(t, "pj_ready"):
                    k, p = t - LAG["pj_ready"], (par - LAG["pj_ready"]) % 2
                    done(act, S["ffn0_mm"], k)
                    nc.scalar.copy(pj[:, p, :], PB["ffn0_mm"][:, P:P + PJ]).then_inc(S["pj_ready"], 1)
                if live(t, "exD_ready"):
                    k = t - LAG["exD_ready"]
                    done(act, S["gate_ready"], k - 1)
                    nc.scalar.activation(exD[:, :], dlD[:, :], ACT.Exp, accum_out=smD[:, :]).then_inc(S["exD_ready"], 1)
                if live(t, "ss_ready"):
                    k, p = t - LAG["ss_ready"], (par - LAG["ss_ready"]) % 2
                    done(act, S["pj_ready"], k)
                    nc.scalar.activation(sq[:, :], pj[:, p, 0:PROJ], ACT.Square, accum_out=ss[:, :]).then_inc(S["ss_ready"], 1)
                if live(t, "bufT_ready"):
                    k = t - LAG["bufT_ready"]
                    done(act, S["disp_mm"], k)
                if live(t, "qT_ready"):
                    k, p = t - LAG["qT_ready"], (par - LAG["qT_ready"]) % 2
                    done(act, S["qT_mm"], k)
                    nc.scalar.copy(qT[:, p, :, :], PB["qT_mm"][:, :].rearrange("p (c n) -> p c n", c=4)).then_inc(S["qT_ready"], 1)
                if live(t, "bufT_ready"):
                    k, p = t - LAG["bufT_ready"], (par - LAG["bufT_ready"]) % 2
                    b = bufT[:, :, k * CAP:(k + 1) * CAP] if isinstance(k, int) else bufT[:, :, ds(k * CAP, CAP)]
                    nc.scalar.copy(b, PB["disp_mm"][:, 0:ES].rearrange("p (e s) -> p e s", e=E)).then_inc(S["bufT_ready"], 1)
                if live(t, "o0T_ready"):
                    k = t - LAG["o0T_ready"]
                    done(act, S["o0_turned"], k)
                    nc.scalar.copy(o0T[:, :], PB["o0_turned"][:, 0:P]).then_inc(S["o0T_ready"], 1)
                if live(t, "combT_ready"):
                    k = t - LAG["combT_ready"]
                    done(act, S["comb_turned"], k)
                if live(t, "exB_ready"):
                    k = t - LAG["exB_ready"]
                    done(act, S["rn_ready"], k)
                    done(act, S["dlB_ready"], k)
                    nc.scalar.activation(exB[:, :], dlB[:, NR:NG], ACT.Exp, scale=rn[:, 0:1], accum_out=smB[:, :]).then_inc(S["exB_ready"], 1)
                if live(t, "combT_ready"):
                    k, p = t - LAG["combT_ready"], (par - LAG["combT_ready"]) % 2
                    c = combT[:, k, :, :] if isinstance(k, int) else combT[:, ds(k, 1), :, :].rearrange("p a c n -> p (a c) n")
                    nc.scalar.copy(c, PB["comb_turned"][0:HALF, 0:2 * P].rearrange("p (c n) -> p c n", c=2)).then_inc(S["combT_ready"], 1)
                if live(t, "e0_ready"):
                    k, p = t - LAG["e0_ready"], (par - LAG["e0_ready"]) % 2
                    done(act, S["s0m_ready"], k)
                    nc.scalar.activation(e0[:, p, :], s0m[:, :], ACT.Exp, scale=float(D0) ** -0.5).then_inc(S["e0_ready"], 1)
                if live(t, "dwT_ready"):
                    k = t - LAG["dwT_ready"]
                    done(act, S["dw_turned"], k)
                    nc.scalar.copy(dwT[:, :], PB["dw_turned"][0:NR, 0:P]).then_inc(S["dwT_ready"], 1)
                if live(t, "kT_ready"):
                    k, p = t - LAG["kT_ready"], (par - LAG["kT_ready"]) % 2
                    nc.scalar.copy(kT[:, p, :, :], PB["kT_mm"][:, :].rearrange("p (c n) -> p c n", c=4)).then_inc(S["kT_ready"], 1)
                if live(t, "p1_ready1"):
                    k = t - LAG["p1_ready1"]
                    done(act, S["nmx_ready1"], k)
                    for c in range(4):
                        last = nc.scalar.activation(p1[:, 1, c, :], PB["s1_mm1"][:, c * P:(c + 1) * P], ACT.Exp, bias=nmx1[:, 1, c:c + 1])
                    last.then_inc(S["p1_ready1"], 1)
                if live(t, "p1_ready0"):
                    k = t - LAG["p1_ready0"]
                    done(act, S["nmx_ready0"], k)
                    for c in range(4):
                        last = nc.scalar.activation(p1[:, 0, c, :], PB["s1_mm0"][:, c * P:(c + 1) * P], ACT.Exp, bias=nmx1[:, 0, c:c + 1])
                    last.then_inc(S["p1_ready0"], 1)
                if live(t, "pT_ready1"):
                    k, p = t - LAG["pT_ready1"], (par - LAG["pT_ready1"]) % 2
                    done(act, S["p_turned1"], k)
                    nc.scalar.copy(pT[:, 1, :, :], PB["p_turned1"][:, :].rearrange("p (h n) -> p h n", h=4)).then_inc(S["pT_ready1"], 1)
                if live(t, "pT_ready0"):
                    k, p = t - LAG["pT_ready0"], (par - LAG["pT_ready0"]) % 2
                    done(act, S["p_turned0"], k)
                    nc.scalar.copy(pT[:, 0, :, :], PB["p_turned0"][:, :].rearrange("p (h n) -> p h n", h=4)).then_inc(S["pT_ready0"], 1)
                if live(t, "ln_xn"):
                    r, p = t - LAG["ln_xn"], (par - LAG["ln_xn"]) % 2
                    ln_done(act, ln_shift, r)
                    done(act, S["disp_mm"], r - LN_LAG[3] - 2)
                    lo, hi = ln_slots(r)
                    for n in range(lo, hi):
                        last = nc.scalar.activation(xn[:, p, n, :], ln_input(n, i, par, "ln_xn"), ACT.Identity, bias=shift[:, n:n + 1],
                                                    scale=rstd[:, n:n + 1])
                    last.then_inc(ln_xn, 1)

            steps(act, step)

            def expert(i, n, p):
                act.wait_ge(e_w_loaded[p], 48 * (i + 1))
                for half in range(2):
                    for c in range(HC):
                        act.wait_ge(e_h_mm[half], HC * n + c + 1)
                        if not (isinstance(n, int) and n == 0):
                            act.wait_ge(e_y_mm[half], n)
                        nc.scalar.activation(hT[:, half, c, :], (K0, K1, K2, K3)[c][:, 0:HB], ACT.Relu,
                                             bias=b1s[:, p, c:c + 1]).then_inc(e_h_ready[half], 1)

            expert(0, 0, 0)
            expert(0, 1, 1)
            with act.Fori(1, E_LOOP) as i:
                expert(i, 2 * i, 0)
                expert(i, 2 * i + 1, 1)

            def combine(i, p, k):
                act.wait_ge(f_turned, k + 1)
                if not isinstance(i, int):
                    act.wait_ge(f_mm, k - 1)
                nc.scalar.activation(ys[:, p, :, :], (K0, K1)[p][0:HALF, 0:2 * P].rearrange("p (c n) -> p c n", c=2), ACT.Copy,
                                     scale=tg[0:HALF, 3:4]).then_inc(f_ys, 1)

            combine(0, 0, 0)
            combine(0, 1, 1)
            with act.Fori(1, B // 2) as i:
                combine(i, 0, 2 * i)
                combine(i, 1, 2 * i + 1)

        @block.tensor
        def _(pe):
            mm = nc.tensor.matmul
            pe.wait_ge(s_small, 16 * len(small))
            pe.wait_ge(s_setup_pool, 6)
            mm(psB[0:PROJ, 0:NG], ones32[:, :], simsq[:, :], start=True, stop=True).then_inc(s_setup_pe, 1)
            pe.wait_ge(s_setup_dve, 3)
            mm(psQ[:, 0:NG], wp0[:, :], sim19[:, :], start=True, stop=True).then_inc(s_setup_pe, 1)
            mm(psX[:, 0:NG], bpwide[:, :], sim19[:, :], start=True, stop=True).then_inc(s_setup_pe, 1)
            pe.wait_ge(s_setup_dve, 6)

            def biased(o, name, *operands, rows=slice(0, P)):
                at, w = BIAS_AT[name]
                mm(o, *operands, start=True, stop=False)
                return mm(o, ones_rows[:, :], bias_rows[:, at:at + w], start=False, stop=True)

            def layer1_setup():
                pe.wait_ge(s_late, 16 * len(late))
                pe.wait_ge(s_setup_dve, 7)
                mm(K0[0:3, :], lnb_wide[:, :], wq1[:, :], start=True, stop=True).then_inc(s_setup_pe, 1)
                pe.wait_ge(s_setup_dve, 10)

            def step(i, par, t):
                if live(t, "comb_turned"):
                    k, p = t - LAG["comb_turned"], (par - LAG["comb_turned"]) % 2
                    done(pe, S["comb_ready"], k)
                    bank_free(pe, t, [(S["p1_ready0"], t - 1 - LAG["s1_mm0"])], [(S["combT_ready"], t - 1 - LAG["comb_turned"])])
                    cm = comb[:, :, :].rearrange("p e s -> p (e s)")
                    for c in range(2):
                        last = nc.tensor.transpose(PB["comb_turned"][0:HALF, c * P:(c + 1) * P], cm[:, c * HALF:(c + 1) * HALF], ident[:, :])
                    last.then_inc(S["comb_turned"], 1)
                if live(t, "disp_mm"):
                    k, p = t - LAG["disp_mm"], (par - LAG["disp_mm"]) % 2
                    done(pe, S["disp_ready"], k)
                    mm(PB["disp_mm"][:, 0:ES], xn_of(3, par, "disp_mm"), disp[:, :, :].rearrange("p e s -> p (e s)"),
                       start=True, stop=True).then_inc(S["disp_mm"], 1)
                if live(t, "pv_mm1"):
                    k, p = t - LAG["pv_mm1"], (par - LAG["pv_mm1"]) % 2
                    done(pe, S["pT_ready1"], k)
                    for c in range(4):
                        last = mm(PB["pv_mm1"][:, c * (D1 + 1):(c + 1) * (D1 + 1)], pT[:, 1, c, :], v1[:, p, 2 * c + 1, :], start=True, stop=True)
                    last.then_inc(S["pv_mm1"], 1)
                if live(t, "pv_mm0"):
                    k, p = t - LAG["pv_mm0"], (par - LAG["pv_mm0"]) % 2
                    done(pe, S["pT_ready0"], k)
                    bank_free(pe, t, [(S["idx_ready"], t - 1 - LAG["router_mm"])], [(S["o1T_ready"], t - 1 - LAG["o1_turned"]), (S["o1_ready0"], t - 1 - LAG["pv_mm0"])])
                    for c in range(4):
                        last = mm(PB["pv_mm0"][:, c * (D1 + 1):(c + 1) * (D1 + 1)], pT[:, 0, c, :], v1[:, p, 2 * c + 0, :], start=True, stop=True)
                    last.then_inc(S["pv_mm0"], 1)
                if live(t, "ln_turned"):
                    r, p = t - LAG["ln_turned"], (par - LAG["ln_turned"]) % 2
                    ln_done(pe, ln_xn, r)
                    lo, hi = ln_slots(r)
                    for n in range(lo, hi):
                        last = nc.tensor.transpose(PB["ln_turned"][:, n * P:(n + 1) * P], xn[:, p, n, :], ident[:, :])
                    last.then_inc(ln_turned, 1)
                if live(t, "o1_turned"):
                    k = t - LAG["o1_turned"]
                    done(pe, S["o1_ready0"], k)
                    for c in range(4):
                        last = nc.tensor.transpose(PB["o1_turned"][:, c * P:(c + 1) * P], o1[:, 2 * c:2 * c + 2, :], ident[:, :])
                    last.then_inc(S["o1_turned"], 1)
                if live(t, "pos_mm"):
                    k = t - LAG["pos_mm"]
                    done(pe, S["chosen_ready"], k)
                    mm(PB["pos_mm"][:, 0:E], before[:, :], chosen[:, :], start=True, stop=True).then_inc(S["pos_mm"], 1)
                if live(t, "qkv_mm"):
                    k, p = t - LAG["qkv_mm"], (par - LAG["qkv_mm"]) % 2
                    loaded(pe, ctxa_loaded, i, par, 2)
                    ln_done(pe, ln_xnT, k)
                    at, _ = BIAS_AT["qkv0"]
                    mm(PB["qkv_mm"][:, 0:P], xnT_of(0, par, "qkv_mm"), wqkv0[:, 0:P], start=True, stop=False, skip_group_check=True)
                    mm(PB["qkv_mm"][:, P:3 * P], ctx_a[:, p, :], wqkv0[:, P:3 * P], start=False, stop=False, skip_group_check=True)
                    mm(PB["qkv_mm"][:, 0:3 * P], ones_rows[:, :], bias_rows[:, at:at + 3 * P], start=False, stop=True,
                       skip_group_check=True).then_inc(S["qkv_mm"], 1)
                if live(t, "ffn0_mm"):
                    k = t - LAG["ffn0_mm"]
                    ln_done(pe, ln_xnT, k + LN_LAG[1])
                    biased(PB["ffn0_mm"][:, 0:P + PJ], "ffn0", xnT_of(1, par, "ffn0_mm"), wffn0[:, :]).then_inc(S["ffn0_mm"], 1)
                if live(t, "qT_mm"):
                    k = t - LAG["qT_mm"]
                    ln_done(pe, ln_xnT, k + LN_LAG[2])
                    bank_free(pe, t, [(S["qkv_ready"], t - LAG["qkv_mm"])], [(S["pT_ready0"], t - 1 - LAG["p_turned0"]), (S["dwT_ready"], t - 1 - LAG["dw_turned"]), (S["qT_ready"], t - 1 - LAG["qT_mm"])])
                    at, _ = BIAS_AT["q1"]
                    for c in range(4):
                        o = PB["qT_mm"][:, c * P:(c + 1) * P]
                        mm(o, wq1[:, c * P:(c + 1) * P], xnT_of(2, par, "qT_mm"), start=True, stop=False)
                        last = mm(o, bias_rows[:, at + c * P:at + (c + 1) * P], ones_rows[:, :], start=False, stop=True)
                    last.then_inc(S["qT_mm"], 1)
                if live(t, "kT_mm"):
                    k, p = t - LAG["kT_mm"], (par - LAG["kT_mm"]) % 2
                    loaded(pe, ctxc_loaded, i, par, 3)
                    bank_free(pe, t, [(S["v_ready"], t - 1 - LAG["v_mm"])], [(S["kT_ready"], t - 1 - LAG["kT_mm"])])
                    for c in range(4):
                        last = mm(PB["kT_mm"][:, c * P:(c + 1) * P], wkv1[:, c * P:(c + 1) * P], ctx_c[:, p, :], start=True, stop=True)
                    last.then_inc(S["kT_mm"], 1)
                if live(t, "y1_mm"):
                    k = t - LAG["y1_mm"]
                    done(pe, S["o1T_ready"], k)
                    for c in range(4):
                        last = mm(PB["y1_mm"][:, 0:P], o1T[:, c, :], wo1[:, c, :], start=(c == 0), stop=(c == 3))
                    last.then_inc(S["y1_mm"], 1)
                if live(t, "o0_turned"):
                    k = t - LAG["o0_turned"]
                    done(pe, S["o0n_ready"], k)
                    bank_free(pe, t, [(S["bufT_ready"], t - LAG["disp_mm"])], [(S["o0T_ready"], t - 1 - LAG["o0_turned"])])
                    nc.tensor.transpose(PB["o0_turned"][:, 0:P], o0n[:, :], ident[:, :]).then_inc(S["o0_turned"], 1)
                if live(t, "s1_mm1"):
                    k, p = t - LAG["s1_mm1"], (par - LAG["s1_mm1"]) % 2
                    done(pe, S["qT_ready"], k)
                    bank_free(pe, t, [(S["slot_ready"], t - LAG["pos_mm"])], [(S["p1_ready1"], t - 1 - LAG["s1_mm1"])])
                    r = slice(1 * D1, 2 * D1)
                    for c in range(4):
                        mm(PB["s1_mm1"][:, c * P:(c + 1) * P], qT[r, p, c, :], kT[r, p, c, :], start=(c == 0), stop=False, skip_group_check=True)
                    mm(PB["s1_mm1"][:, :], ones_rows[0:1, :], mask_row(k), start=False, stop=True, skip_group_check=True).then_inc(S["s1_mm1"], 1)
                if live(t, "s1_mm0"):
                    k, p = t - LAG["s1_mm0"], (par - LAG["s1_mm0"]) % 2
                    bank_free(pe, t, [(S["combT_ready"], t - LAG["comb_turned"])], [(S["p1_ready0"], t - 1 - LAG["s1_mm0"])])
                    r = slice(0 * D1, 1 * D1)
                    for c in range(4):
                        mm(PB["s1_mm0"][:, c * P:(c + 1) * P], qT[r, p, c, :], kT[r, p, c, :], start=(c == 0), stop=False, skip_group_check=True)
                    mm(PB["s1_mm0"][:, :], ones_rows[0:1, :], mask_row(k), start=False, stop=True, skip_group_check=True).then_inc(S["s1_mm0"], 1)
                if live(t, "dw_turned"):
                    k = t - LAG["dw_turned"]
                    done(pe, S["dw_ready"], k)
                    nc.tensor.transpose(PB["dw_turned"][0:NR, 0:P], dw[:, :], ident[:, :]).then_inc(S["dw_turned"], 1)
                if live(t, "y0_mm"):
                    k = t - LAG["y0_mm"]
                    done(pe, S["o0T_ready"], k)
                    bank_free(pe, t, [(S["x3_ready"], t - LAG["y1_mm"])], [(ln_xnT, t - LAG["ln_turned"]), (S["x1_ready"], t - 1 - LAG["y0_mm"])])
                    biased(PB["y0_mm"][:, 0:P], "bo0", o0T[:, :], wo0[:, :]).then_inc(S["y0_mm"], 1)
                if live(t, "router_mm"):
                    k = t - LAG["router_mm"]
                    ln_done(pe, ln_xnT, k + LN_LAG[3])
                    biased(PB["router_mm"][:, 0:E], "br", xnT_of(3, par, "router_mm"), wr[:, :]).then_inc(S["router_mm"], 1)
                if live(t, "res0_mm"):
                    k = t - LAG["res0_mm"]
                    done(pe, S["dwT_ready"], k)
                    mm(PB["ffn0_mm"][:, 0:P], dwT[:, :], wu0[:, :], start=False, stop=True, skip_group_check=True).then_inc(S["res0_mm"], 1)
                if live(t, "v_mm"):
                    k, p = t - LAG["v_mm"], (par - LAG["v_mm"]) % 2
                    bank_free(pe, t, [(S["kT_ready"], t - LAG["kT_mm"])], [(S["v_ready"], t - 1 - LAG["v_mm"])])
                    mm(PB["v_mm"][:, :], ctx_c[:, p, :], wkv1[:, H1 * D1:], start=True, stop=True).then_inc(S["v_mm"], 1)
                if live(t, "p_turned1"):
                    k = t - LAG["p_turned1"]
                    done(pe, S["p1_ready1"], k)
                    bank_free(pe, t, [(S["x2_ready"], t - LAG["ffn0_mm"])], [(S["o1_ready1"], t - LAG["pv_mm1"]), (S["pT_ready1"], t - 1 - LAG["p_turned1"])])
                    for c in range(4):
                        last = nc.tensor.transpose(PB["p_turned1"][:, c * P:(c + 1) * P], p1[:, 1, c, :], ident[:, :])
                    last.then_inc(S["p_turned1"], 1)
                if live(t, "p_turned0"):
                    k = t - LAG["p_turned0"]
                    done(pe, S["p1_ready0"], k)
                    for c in range(4):
                        last = nc.tensor.transpose(PB["p_turned0"][:, c * P:(c + 1) * P], p1[:, 0, c, :], ident[:, :])
                    last.then_inc(S["p_turned0"], 1)

            steps(pe, step, (0, layer1_setup))

            pe.wait_ge(S["bufT_ready"], B)
            pe.wait_ge(S["combT_ready"], B)

            def up(e, p, n, half):
                for c in range(HC):
                    if half == 1 or not (isinstance(n, int) and n == 0):
                        pe.wait_ge(e_h_ready[1 - half], HC * (n - 1 + half) + c + 1)
                    rhs = bufT[:, e, half * HB:(half + 1) * HB] if isinstance(e, int) else \
                        bufT[:, ds(e, 1), half * HB:(half + 1) * HB].rearrange("p a n -> p (a n)")
                    mm((K0, K1, K2, K3)[c][:, 0:HB], w1s[:, p, c * P:(c + 1) * P], rhs, start=True,
                       stop=True).then_inc(e_h_mm[half], 1)

            def down(e, p, n, half):
                if not (isinstance(n, int) and n == 0):
                    pe.wait_ge(e_y_ready[half], n)
                pe.wait_ge(e_h_ready[half], HC * (n + 1))
                for c in range(HC):
                    last = mm((psX, psQ)[half][:, 0:HB], w2s[:, p, c, :], hT[:, half, c, :], start=(c == 0), stop=(c == HC - 1))
                last.then_inc(e_y_mm[half], 1)

            def expert(i, e, p):
                pe.wait_ge(e_w_loaded[p], 48 * (i + 1))
                up(e, p, e, 0)
                up(e, p, e, 1)
                down(e, p, e, 0)
                down(e, p, e, 1)

            expert(0, 0, 0)
            expert(0, 1, 1)
            with pe.Fori(1, E_LOOP) as i:
                expert(i, 2 * i, 0)
                expert(i, 2 * i + 1, 1)

            def turn(i, p, k):
                pe.wait_ge(f_yTs, k + 1)
                if not (isinstance(k, int) and k < 2):
                    pe.wait_ge(f_ys, k - 1)
                for c in range(2):
                    last = nc.tensor.transpose((K0, K1)[p][0:HALF, c * P:(c + 1) * P], yTs[:, p, c * HALF:(c + 1) * HALF],
                                               ident[:, :])
                last.then_inc(f_turned, 1)

            def combine(i, p, k):
                pe.wait_ge(f_ys, k + 1)
                pe.wait_ge(f_combs, k + 1)
                if not (isinstance(k, int) and k < 2):
                    pe.wait_ge(f_out, k - 1)
                for c in range(2):
                    last = mm((K2, K3)[p][:, 0:P], combs[:, p, c, :], ys[:, p, c, :], start=(c == 0), stop=(c == 1))
                last.then_inc(f_mm, 1)

            turn(0, 0, 0)
            turn(0, 1, 1)
            combine(0, 0, 0)
            turn(1, 0, 2)
            combine(0, 1, 1)
            with pe.Fori(1, B // 2 - 1) as i:
                turn(i, 1, 2 * i + 1)
                combine(i, 0, 2 * i)
                turn(i, 0, 2 * i + 2)
                combine(i, 1, 2 * i + 1)
            turn(B // 2 - 1, 1, B - 1)
            combine(B // 2 - 1, 0, B - 2)
            combine(B // 2 - 1, 1, B - 1)

        @block.vector
        def _(dve):
            tt, ts = nc.vector.tensor_tensor, nc.vector.tensor_scalar
            dve.wait_ge(s_small, 16 * len(small))
            ts(temp[:, :], temp[:, :], CLAMP, None, ALU.min)
            dve.wait_ge(s_setup_pe, 1)
            ts(simrn[:, :], psB[0:PROJ, 0:NG], 1e-24, None, ALU.max).then_inc(s_setup_dve, 2)
            dve.wait_ge(s_tanh, 1)
            ts(wo0[:, :], wo0[:, :], tg[:, 0:1], None, ALU.mult)
            ts(wffn0[:, 0:P], wffn0[:, 0:P], tg[:, 2:3], None, ALU.mult)
            ts(wu0[:, :], wu0[:, :], tg[0:NR, 2:3], None, ALU.mult)
            at, w = BIAS_AT["bo0"]
            ts(bias[:, at:at + w], bias[:, at:at + w], tg[0:3, 0:1], None, ALU.mult)
            dve.wait_ge(s_setup_pool, 7)
            dve.wait_ge(s_setup_act, 1)
            nc.vector.scalar_tensor_tensor(sim19[:, :], simrn[:, :], tscale[:, 0:1], sim19[:, :], ALU.mult, ALU.mult)
            nc.vector.tensor_copy(bpwide[:, :], bpcol[:, 0:1].broadcast_to([PROJ, P])).then_inc(s_setup_dve, 1)
            dve.wait_ge(s_setup_pe, 2)
            nc.vector.tensor_copy(wffn0[:, P + PROJ:P + PROJ + NG], psQ[:, 0:NG]).then_inc(s_setup_dve, 1)
            dve.wait_ge(s_setup_pe, 3)
            at, w = BIAS_AT["ffn0"]
            nc.vector.tensor_copy(bias[:, at + P + PROJ:at + P + PROJ + NG], psX[0:3, 0:NG]).then_inc(s_setup_dve, 1)

            def split(r, n, signal):
                dve.wait_ge(s_setup_dve, n[0])
                nc.vector.tensor_copy(bias_p[0][:, r], bias[:, r]).then_inc(s_bias, 1)
                dve.wait_ge(s_bias, n[1] + 1)
                tt(bias_r[0][:, r], bias[:, r], bias_p[0][:, r], ALU.subtract).then_inc(s_bias, 1)
                dve.wait_ge(s_bias, n[1] + 2)
                nc.vector.tensor_copy(bias_p[1][:, r], bias_r[0][:, r]).then_inc(s_bias, 1)
                dve.wait_ge(s_bias, n[1] + 3)
                tt(bias_r[1][:, r], bias_r[0][:, r], bias_p[1][:, r], ALU.subtract).then_inc(s_bias, 1)
                dve.wait_ge(s_bias, n[1] + 4)
                nc.vector.tensor_copy(bias_p[2][:, r], bias_r[1][:, r]).then_inc(s_bias, 1)
                dve.wait_ge(s_bias, n[1] + 5)
                ts(bias_rows[:, r], bias_p[0][:, r], ident[0:3, 0:1], None, ALU.mult).then_inc(s_bias, 1)
                dve.wait_ge(s_bias, n[1] + 6)
                nc.vector.scalar_tensor_tensor(bias_rows[:, r], bias_p[1][:, r], ident[0:3, 1:2], bias_rows[:, r],
                                               ALU.mult, ALU.add).then_inc(s_bias, 1)
                dve.wait_ge(s_bias, n[1] + 7)
                nc.vector.scalar_tensor_tensor(bias_rows[:, r], bias_p[2][:, r], ident[0:3, 2:3], bias_rows[:, r],
                                               ALU.mult, ALU.add).then_inc(signal, 1)

            early = slice(0, BIAS_AT["q1"][0])
            split(early, (5, 0), s_setup_dve)

            def layer1_setup():
                dve.wait_ge(s_late, 16 * len(late))
                nc.vector.tensor_copy(lnb_wide[:, :], ln_b.broadcast_to([P, 3])).then_inc(s_setup_dve, 1)
                dve.wait_ge(s_setup_pe, 4)
                at, w = BIAS_AT["q1"]
                ts(bias[:, at:at + w], K0[0:3, :], float(D1) ** -0.5, None, ALU.mult)
                ts(wo1[:, :, :], wo1[:, :, :], tg[:, 1:2], None, ALU.mult)
                ts(wq1[:, :], wq1[:, :], ln_g[:, 0:1], float(D1) ** -0.5, ALU.mult, ALU.mult).then_inc(s_setup_dve, 1)
                split(slice(at, at + w), (8, 7), s_setup_dve)
                ts(mask_rows[:, :], mask8[:, :], -MASKED, MASKED, ALU.mult, ALU.add).then_inc(s_setup_dve, 1)

            def step(i, par, t):
                if live(t, "idx_ready"):
                    k = t - LAG["idx_ready"]
                    done(dve, S["top_ready"], k)
                    ts(dlD[:, :], PB["router_mm"][:, 0:E], top8[:, 0:1], None, ALU.subtract)
                    nc.vector.max_index(idx8[:, :], top8[:, :], PB["router_mm"][:, 0:E]).then_inc(S["idx_ready"], 1)
                if live(t, "o0_ready0"):
                    k, p = t - LAG["o0_ready0"], (par - LAG["o0_ready0"]) % 2
                    done(dve, S["av_prod0"], k)
                    c = slice(0 * P // 2, 1 * P // 2)
                    nc.vector.reduce_sum(o0[:, c], prod_av[:, :].rearrange("p (c g) -> p c g", g=H0)[:, c, :], X).then_inc(S["o0_ready0"], 1)
                if live(t, "idxf_ready"):
                    k = t - LAG["idxf_ready"]
                    done(dve, S["idx_ready"], k)
                    nc.vector.tensor_copy(idxf[:, :], idx8[:, 0:2]).then_inc(S["idxf_ready"], 1)
                if live(t, "ln_shift"):
                    r = t - LAG["ln_shift"]
                    ln_done(dve, ln_rstd, r)
                    lo, hi = ln_slots(r)
                    nc.vector.scalar_tensor_tensor(shift[:, lo:hi], mv[:, lo:hi, 0], -1.0, rstd[:, lo:hi], ALU.mult,
                                                   ALU.mult).then_inc(ln_shift, 1)
                if live(t, "sum0_ready"):
                    k, p = t - LAG["sum0_ready"], (par - LAG["sum0_ready"]) % 2
                    nc.vector.reduce_sum(sum0[:, :], e0[:, p, :].rearrange("p (h g) -> p h g", h=H0), X).then_inc(S["sum0_ready"], 1)
                if live(t, "rs1_ready1"):
                    k = t - LAG["rs1_ready1"]
                    done(dve, S["pv_mm1"], k)
                    nc.vector.reciprocal(rs1[:, 1, :], pv_bank(1)[:, :, D1]).then_inc(S["rs1_ready1"], 1)
                if live(t, "gate_ready"):
                    k = t - LAG["gate_ready"]
                    done(dve, S["rsD_ready"], k)
                    nc.vector.scalar_tensor_tensor(gate[:, :], exD[:, :], rsD[:, 0:1], chosen[:, :], ALU.mult, ALU.mult).then_inc(S["gate_ready"], 1)
                if live(t, "o1_ready1"):
                    k = t - LAG["o1_ready1"]
                    done(dve, S["rs1_ready1"], k)
                    tt(o1[:, 1::2, :], pv_bank(1)[:, :, 0:D1], bc(rs1[:, 1, :], 2, D1), ALU.mult).then_inc(S["o1_ready1"], 1)
                if live(t, "rs1_ready0"):
                    k = t - LAG["rs1_ready0"]
                    done(dve, S["pv_mm0"], k)
                    nc.vector.reciprocal(rs1[:, 0, :], pv_bank(0)[:, :, D1]).then_inc(S["rs1_ready0"], 1)
                if live(t, "o1_ready0"):
                    k = t - LAG["o1_ready0"]
                    done(dve, S["rs1_ready0"], k)
                    tt(o1[:, 0::2, :], pv_bank(0)[:, :, 0:D1], bc(rs1[:, 0, :], 2, D1), ALU.mult).then_inc(S["o1_ready0"], 1)
                if live(t, "first_ready"):
                    k = t - LAG["first_ready"]
                    done(dve, S["idxf_ready"], k)
                    ts(first[:, :], iota8[:, :], idxf[:, 0:1], None, ALU.is_equal).then_inc(S["first_ready"], 1)
                if live(t, "rs0_ready"):
                    k = t - LAG["rs0_ready"]
                    done(dve, S["sum0_ready"], k)
                    nc.vector.reciprocal(rs0[:, :], sum0[:, :]).then_inc(S["rs0_ready"], 1)
                if live(t, "chosen_ready"):
                    k = t - LAG["chosen_ready"]
                    done(dve, S["first_ready"], k)
                    nc.vector.scalar_tensor_tensor(chosen[:, :], iota8[:, :], idxf[:, 1:2], first[:, :], ALU.is_equal, ALU.add).then_inc(S["chosen_ready"], 1)
                if live(t, "slot_ready"):
                    k = t - LAG["slot_ready"]
                    done(dve, S["pos_mm"], k)
                    nc.vector.scalar_tensor_tensor(slot[:, :], PB["pos_mm"][:, 0:E], 1.0, chosen[:, :], ALU.add, ALU.mult).then_inc(S["slot_ready"], 1)
                if live(t, "o0_ready1"):
                    k, p = t - LAG["o0_ready1"], (par - LAG["o0_ready1"]) % 2
                    done(dve, S["av_prod1"], k)
                    c = slice(1 * P // 2, 2 * P // 2)
                    nc.vector.reduce_sum(o0[:, c], prod_av[:, :].rearrange("p (c g) -> p c g", g=H0)[:, c, :], X).then_inc(S["o0_ready1"], 1)
                if live(t, "qk_prod"):
                    k, p = t - LAG["qk_prod"], (par - LAG["qk_prod"]) % 2
                    done(dve, S["qkv_ready"], k)
                    h = slice(0, H_DVE)
                    pqk = prod_qk[:, :].rearrange("p (h g d) -> p h g d", h=H0, g=H0)[:, h, :, :]
                    qv = bc(qkv[:, p, 0:P].rearrange("p (h d) -> p h d", h=H0)[:, h, :], 2, H0)
                    kv = bc(qkv[:, p, P:2 * P].rearrange("p (g d) -> p g d", g=H0), 1, h.stop - h.start)
                    nc.vector.tensor_tensor(pqk, qv, kv, ALU.mult).then_inc(S["qk_prod"], 1)
                if live(t, "mxB_ready"):
                    k, p = t - LAG["mxB_ready"], (par - LAG["mxB_ready"]) % 2
                    done(dve, S["pj_ready"], k)
                    nc.vector.reduce_max(mxB[:, :], pj[:, p, PROJ:PROJ + NR], X).then_inc(S["mxB_ready"], 1)
                if live(t, "ssm_ready"):
                    k = t - LAG["ssm_ready"]
                    done(dve, S["ss_ready"], k)
                    ts(ssm[:, :], ss[:, :], 1e-24, None, ALU.max).then_inc(S["ssm_ready"], 1)
                if live(t, "dlB_ready"):
                    k, p = t - LAG["dlB_ready"], (par - LAG["dlB_ready"]) % 2
                    done(dve, S["mxB_ready"], k)
                    ts(dlB[:, :], pj[:, p, PROJ:PROJ + NG], mxB[:, 0:1], None, ALU.subtract).then_inc(S["dlB_ready"], 1)
                if live(t, "s0_ready"):
                    k, p = t - LAG["s0_ready"], (par - LAG["s0_ready"]) % 2
                    done(dve, S["qk_prod"], k)
                    done(dve, S["qk_prod_rest"], k)
                    nc.vector.reduce_sum(s0[:, :], prod_qk[:, :].rearrange("p (s d) -> p s d", d=D0), X).then_inc(S["s0_ready"], 1)
                if live(t, "kk_ready"):
                    k = t - LAG["kk_ready"]
                    done(dve, S["dlB_ready"], k)
                    nc.vector.scalar_tensor_tensor(kk[:, :], dlB[:, 0:NR], 0.0, key15[:, :], ALU.is_ge, ALU.mult).then_inc(S["kk_ready"], 1)
                if live(t, "rsB_ready"):
                    k = t - LAG["rsB_ready"]
                    done(dve, S["exB_ready"], k)
                    nc.vector.reciprocal(rsB[:, :], smB[:, :]).then_inc(S["rsB_ready"], 1)
                if live(t, "km_ready"):
                    k = t - LAG["km_ready"]
                    done(dve, S["kk_ready"], k)
                    nc.vector.reduce_max(km[:, :], kk[:, :], X).then_inc(S["km_ready"], 1)
                if live(t, "mx0_ready"):
                    k, p = t - LAG["mx0_ready"], (par - LAG["mx0_ready"]) % 2
                    done(dve, S["s0_ready"], k)
                    nc.vector.reduce_max(mx0[:, :], s0[:, :].rearrange("p (h g) -> p h g", h=H0), X).then_inc(S["mx0_ready"], 1)
                if live(t, "oh15_ready"):
                    k = t - LAG["oh15_ready"]
                    done(dve, S["km_ready"], k)
                    ts(oh15[:, :], kk[:, :], km[:, 0:1], rsB[:, 0:1], ALU.is_equal, ALU.mult).then_inc(S["oh15_ready"], 1)
                if live(t, "s0m_ready"):
                    k, p = t - LAG["s0m_ready"], (par - LAG["s0m_ready"]) % 2
                    done(dve, S["mx0_ready"], k)
                    tt(s0m[:, :].rearrange("p (h g) -> p h g", h=H0), s0[:, :].rearrange("p (h g) -> p h g", h=H0), bc(mx0[:, :], 2, H0),
                       ALU.subtract).then_inc(S["s0m_ready"], 1)
                if live(t, "dw_ready"):
                    k, p = t - LAG["dw_ready"], (par - LAG["dw_ready"]) % 2
                    done(dve, S["oh15_ready"], k)
                    tt(dw[:, :], oh15[:, :], pj[:, p, PROJ + NG:], ALU.mult).then_inc(S["dw_ready"], 1)
                if live(t, "x3_ready"):
                    k = t - LAG["x3_ready"]
                    done(dve, S["y1_mm"], k)
                    tt(x3_at(k), x2[:, (par - LAG["x3_ready"]) % 2, :], PB["y1_mm"][:, 0:P], ALU.add).then_inc(S["x3_ready"], 1)
                if live(t, "nmx_ready1"):
                    k, p = t - LAG["nmx_ready1"], (par - LAG["nmx_ready1"]) % 2
                    done(dve, S["s1_mm1"], k)
                    nc.vector.tensor_reduce(nmx1[:, 1, :], PB["s1_mm1"][:, :].rearrange("p (h n) -> p h n", h=4), X, ALU.max,
                                            negate=True).then_inc(S["nmx_ready1"], 1)
                if live(t, "x1_ready"):
                    k, p = t - LAG["x1_ready"], (par - LAG["x1_ready"]) % 2
                    loaded(dve, xres_loaded, i, par, 2)
                    done(dve, S["y0_mm"], k)
                    tt(x1[:, p, :], x_res[:, p, :], PB["y0_mm"][:, 0:P], ALU.add).then_inc(S["x1_ready"], 1)
                if live(t, "x2_ready"):
                    k, p = t - LAG["x2_ready"], (par - LAG["x2_ready"]) % 2
                    done(dve, S["x3_ready"], k - 2)
                    done(dve, S["res0_mm"], k)
                    tt(x2[:, p, :], x1[:, p, :], PB["ffn0_mm"][:, 0:P], ALU.add).then_inc(S["x2_ready"], 1)
                if live(t, "nmx_ready0"):
                    k, p = t - LAG["nmx_ready0"], (par - LAG["nmx_ready0"]) % 2
                    done(dve, S["s1_mm0"], k)
                    nc.vector.tensor_reduce(nmx1[:, 0, :], PB["s1_mm0"][:, :].rearrange("p (h n) -> p h n", h=4), X, ALU.max,
                                            negate=True).then_inc(S["nmx_ready0"], 1)
                if live(t, "ln_stats"):
                    r = t - LAG["ln_stats"]
                    if slot_live(r, 0):
                        loaded(dve, x_loaded, i, par, 0)
                    done(dve, S["x1_ready"], r - LN_LAG[1])
                    done(dve, S["x2_ready"], r - LN_LAG[2])
                    done(dve, S["x3_ready"], r - LN_LAG[3])
                    lo, hi = ln_slots(r)
                    for n in range(lo, hi):
                        last = nc.vector.bn_stats(stats[:, n, :], ln_input(n, i, par, "ln_stats"))
                    last.then_inc(ln_stats, 1)
                if live(t, "ln_mv"):
                    r = t - LAG["ln_mv"]
                    ln_done(dve, ln_stats, r)
                if live(t, "rsD_ready"):
                    k = t - LAG["rsD_ready"]
                    done(dve, S["exD_ready"], k)
                    nc.vector.reciprocal(rsD[:, :], smD[:, :]).then_inc(S["rsD_ready"], 1)
                if live(t, "ln_mv"):
                    r = t - LAG["ln_mv"]
                    lo, hi = ln_slots(r)
                    for n in range(lo, hi):
                        last = nc.vector.bn_aggr(mv[:, n, :], stats[:, n, :])
                    last.then_inc(ln_mv, 1)
                if live(t, "top_ready"):
                    k = t - LAG["top_ready"]
                    done(dve, S["router_mm"], k)
                if live(t, "disp_ready"):
                    k = t - LAG["disp_ready"]
                    done(dve, S["slot_ready"], k)
                    done(dve, S["comb_ready"], k - 1)
                    tt(disp[:, :, :], bc(iota_slot[:, :], 1, E), bc(slot[:, :], 2, CAP), ALU.is_equal).then_inc(S["disp_ready"], 1)
                if live(t, "top_ready"):
                    nc.vector.max(top8[:, :], PB["router_mm"][:, 0:E]).then_inc(S["top_ready"], 1)

            steps(dve, step, (0, layer1_setup))

            def expert(e):
                for half in range(2):
                    dve.wait_ge(e_y_mm[half], e + 1)
                    r = slice(half * B // 2, (half + 1) * B // 2)
                    dst = yT[:, r, e, :] if isinstance(e, int) else yT[:, r, ds(e, 1), :].rearrange("p b a s -> p b (a s)")
                    bias = b2c[:, e:e + 1] if isinstance(e, int) else b2c[:, ds(e, 1)]
                    ts(dst, (psX, psQ)[half][:, 0:HB].rearrange("p (b s) -> p b s", s=CAP), bias, None,
                       ALU.add).then_inc(e_y_ready[half], 1)

            with dve.Fori(0, E) as e:
                expert(e)

            dve.wait_ge(S["combT_ready"], B)
            dve.wait_ge(e_y_ready[1], E)

            def gather(i, p, k):
                if not (isinstance(k, int) and k < 2):
                    dve.wait_ge(f_turned, k - 1)
                src = yT[:, k, :, :] if isinstance(k, int) else yT[:, ds(k, 1), :, :].rearrange("p a e s -> p (a e) s")
                ts(yTs[:, p, :].rearrange("p (e s) -> p e s", e=E), src, 1.0, None, ALU.mult).then_inc(f_yTs, 1)
                if not (isinstance(k, int) and k < 2):
                    dve.wait_ge(f_mm, k - 1)
                src = combT[:, k, :, :] if isinstance(k, int) else combT[:, ds(k, 1), :, :].rearrange("p a c n -> p (a c) n")
                ts(combs[:, p, :, :], src, 1.0, None, ALU.mult).then_inc(f_combs, 1)

            def finish(i, p, k):
                dve.wait_ge(f_mm, k + 1)
                if not (isinstance(k, int) and k < 2):
                    dve.wait_ge(f_stored[p], 16 * i)
                tt(o_out[:, p, :], x3_at(k), (K2, K3)[p][:, 0:P], ALU.add).then_inc(f_out, 1)

            gather(0, 0, 0)
            gather(0, 1, 1)
            finish(0, 0, 0)
            gather(1, 0, 2)
            finish(0, 1, 1)
            with dve.Fori(1, B // 2 - 1) as i:
                gather(i, 1, 2 * i + 1)
                finish(i, 0, 2 * i)
                gather(i, 0, 2 * i + 2)
                finish(i, 1, 2 * i + 1)
            gather(B // 2 - 1, 1, B - 1)
            finish(B // 2 - 1, 0, B - 2)
            finish(B // 2 - 1, 1, B - 1)


def kernel(**inputs):
    import numpy as np
    import concourse.bacc as bacc
    from concourse.bass_utils import run_bass_kernel_spmd

    def t(name):
        return np.ascontiguousarray(np.asarray(inputs[name]).T)

    f32 = np.float32
    import ml_dtypes
    bf16 = ml_dtypes.bfloat16
    arange = np.arange
    def every_row(values):
        return np.broadcast_to(np.asarray(values, f32), (P, len(values)))

    def zeros(*shape):
        return np.zeros(shape, f32)

    def given(name):
        return np.asarray(inputs[name])

    arrays = {
        "x": given("x"),
        "ctxT": np.ascontiguousarray(given("ctx_1024").transpose(0, 2, 1)),
        "mask": given("mask_BxS2_bk0"),
        "g_xattn": given("g_xattn"), "g_ffn": given("g_ffn"),
        "wp0": given("L0_ffn_Wp"), "bp0": given("L0_ffn_bp"), "temp": given("L0_ffn_temp"),
        "sim19": np.concatenate([np.repeat(given("L0_ffn_sim"), RANKS, axis=1), given("L0_ffn_sim")], axis=1),
        "wu0T": np.concatenate([t(f"L0_ffn_Wu{n}") for n in range(4)], axis=0),
        "W1": given("L1_ffn_W1"), "W2": given("L1_ffn_W2"),
        "b1T": np.ascontiguousarray(given("L1_ffn_b1").reshape(E, HC, P).transpose(0, 2, 1)),
        "biases": np.concatenate([given("L0_xattn_bq"), given("L0_xattn_bk"), given("L0_xattn_bv"), given("L0_xattn_bo"),
                                  zeros(P), given("L0_ffn_bp"), zeros(NG + NR), given("L1_ffn_br"), zeros(H1 * D1)]),
        "pack_a": np.concatenate([np.eye(P, dtype=f32), every_row(arange(E)), every_row(arange(1, CAP + 1)),
                        every_row(np.repeat(arange(4, 0, -1), RANKS)),
                        every_row([1, 1, 1 + 1e-5, 1]), every_row([1e-5, 1e-5, 1e-10, 1e-5]),
                        t("L0_xattn_Wq"), t("L0_xattn_Wk"), t("L0_xattn_Wv"), t("L0_xattn_Wo"),
                        t("L0_ffn_W"), t("L0_ffn_Wp"), zeros(P, NG), *[t(f"L0_ffn_Wd{n}") for n in range(4)],
                        given("L1_ffn_Wr"), t("L1_ffn_b2")], axis=1),
        "pack_b": np.concatenate([given("L1_xattn_Wq"), given("L1_xattn_Wkv"),
                                  given("L1_xattn_Wo").reshape(4, P, P).transpose(1, 0, 2).reshape(P, 4 * P),
                                  given("L1_xattn_ln_g")[:, None], given("L1_xattn_ln_b")[:, None]], axis=1),
        "before": (arange(P)[:, None] < arange(P)[None, :]).astype(bf16),
    }
    assert arrays["pack_a"].shape[1] == WIDTH_A and arrays["pack_b"].shape[1] == WIDTH_B
    assert arrays["biases"].shape[0] == BIASES
    nc = bacc.Bacc("TRN2", target_bir_lowering=False, num_devices=1)
    feed, args = {}, {}
    for name, arr in arrays.items():
        feed[f"in_{name}"] = arr
        args[name] = nc.dram_tensor(f"in_{name}", arr.shape, mybir.dt.from_np(arr.dtype), kind="ExternalInput").ap()
    out = nc.dram_tensor("out_0", (B, P, P), F32, kind="ExternalOutput").ap()
    build(nc, args, out)
    r = run_bass_kernel_spmd(nc, [feed], core_ids=[0])
    return r.results[0]["out_0"]
```

```python
from contextlib import ExitStack

import concourse.bass as bass
from concourse import mybir

ALU = mybir.AluOpType
ACT = mybir.ActivationFunctionType
F32 = mybir.dt.float32
BF16 = mybir.dt.bfloat16
U8 = mybir.dt.uint8
U32 = mybir.dt.uint32
X = mybir.AxisListType.X
ds = bass.ds

P = 128
B = 32
H0, D0 = 16, 8
H1, D1 = 8, 64
RANKS = (1, 2, 4, 8)
NR = sum(RANKS)
PROJ = 32
NG = NR + len(RANKS)
PJ = PROJ + NG + NR
H_DVE = 8
E = 8
HID = 512
HC = HID // P
CAP = 20
ES = E * CAP
HALF = ES // 2
MASKED = -float(2.0 ** 100)
CLAMP = 4.605170185988092


def layout(widths):
    at, out = 0, {}
    for name, w in widths:
        out[name] = (at, w)
        at += w
    return out, at


LAYOUT_A, WIDTH_A = layout([("ident", P), ("iota8", E), ("iota_slot", CAP), ("key15", NR), ("ln_mul", 4),
                            ("ln_add", 4), ("wqkv0", 3 * P), ("wo0", P), ("wffn0", P + PJ), ("wr", E), ("b2c", E)])
LAYOUT_B, WIDTH_B = layout([("wq1", H1 * D1), ("wkv1", 2 * H1 * D1), ("wo1", 4 * P), ("ln_g", 1), ("ln_b", 1)])
BIAS_AT, BIASES = layout([("qkv0", 3 * P), ("bo0", P), ("ffn0", P + PJ), ("br", E), ("q1", H1 * D1)])

LAG = {
    "x_loaded": 2, "ctxa_loaded": 2, "xres_loaded": 4, "ctxc_loaded": 4, "ln_stats": 0, "ln_mv": 0, "ln_v2": 0,
    "ln_rstd": 0, "ln_shift": 1, "ln_xn01": 2, "ln_xn23": 1, "ln_turned": 2, "ln_xnT": 2, "qkv_mm": 2, "qkv_ready": 2,
    "qk_prod": 1, "qk_prod_rest": 0, "s0_ready0": 1, "s0_ready1": 1, "mx0_ready": 1, "s0m_ready": 1, "e0_ready": 2,
    "sum0_ready": 1, "rs0_ready": 2, "av_prod0": 1, "av_prod1": 1, "av_prod2": 1, "av_prod3": 1, "o0_ready0": 2,
    "o0_ready1": 2, "o0n_ready": 1, "o0_turned": 4, "o0T_ready": 3, "y0_mm": 4, "x1_ready": 2, "ffn0_mm": 4,
    "pj_ready": 4, "ss_ready": 4, "ssm_ready": 3, "rn_ready": 2, "mxB_ready": 3, "dlB_ready": 3, "kk_ready": 3,
    "km_ready": 3, "exB_ready": 4, "rsB_ready": 3, "oh15_ready": 3, "dw_ready": 3, "dw_turned": 5, "dwT_ready": 4,
    "res0_mm": 5, "x2_ready": 3, "qT_mm": 5, "qT_ready": 5, "kT_mm": 4, "kT_ready": 4, "v_mm": 5, "v_ready": 5,
    "s1_mm0": 6, "s1_mm1": 6, "nmx_ready0": 4, "nmx_ready1": 4, "p1_ready0": 5, "p1_ready1": 5, "p_turned0": 6,
    "p_turned1": 6, "pT_ready0": 6, "pT_ready1": 6, "pv_mm0": 6, "pv_mm1": 6, "rs1_ready0": 5, "rs1_ready1": 5,
    "o1_ready0": 5, "o1_ready1": 5, "o1_turned": 6, "o1T_ready": 6, "y1_mm": 6, "x3_ready": 5, "router_mm": 8,
    "top_ready": 6, "idx_ready": 6, "idxf_ready": 6, "first_ready": 6, "chosen_ready": 7, "exD_ready": 8,
    "rsD_ready": 7, "gate_ready": 7, "pos_mm": 9, "slot_ready": 7, "disp_ready": 7, "comb_ready": 7, "disp_mm": 9,
    "bufT_ready": 9, "comb_turned": 10, "combT_ready": 10, "t_w_loaded": 0, "t_h_mm0": 0, "t_h_mm1": 0, "t_h_mm2": 0,
    "t_h_mm3": 1, "t_h_ready0": 0, "t_h_ready1": 0, "t_h_ready2": 0, "t_h_ready3": 0, "t_y_mm": 1, "t_y_ready": 0,
}
LN_LAG = (0, 2, 3, 5)
LN_ROUNDS = B + LN_LAG[3]
ROUNDS = {"ln_xn01": (0, B + LN_LAG[1]), "ln_xn23": (LN_LAG[2], B + LN_LAG[3] - LN_LAG[2])}
BANK = {
    "ln_turned": 3, "qkv_mm": 1, "o0_turned": 0, "y0_mm": 2, "ffn0_mm": 7, "dw_turned": 1, "qT_mm": 3, "kT_mm": 0,
    "v_mm": 6, "s1_mm0": 3, "s1_mm1": 4, "p_turned0": 7, "p_turned1": 3, "pv_mm0": 7, "pv_mm1": 1, "o1_turned": 4,
    "y1_mm": 5, "router_mm": 2, "pos_mm": 5, "disp_mm": 0, "comb_turned": 1, "t_h_mm0": 6, "t_h_mm1": 2, "t_h_mm2": 1,
    "t_h_mm3": 0, "t_y_mm": 5,
}
MAX_LAG = max(LAG.values())
STEPS = B + E + MAX_LAG
LOOP_FROM = 14


def build(nc, a, out):
    ctx = ExitStack()
    with ctx:
        def sb(name, shape, dt=F32):
            return ctx.enter_context(nc.sbuf_tensor(name, shape, dt))

        def bank(name):
            return ctx.enter_context(nc.psum_tensor(name, [P, 512], F32))

        def sem(name):
            return ctx.enter_context(nc.semaphore(name))

        pack_a = sb("pack_a", [P, WIDTH_A])
        pack_b = sb("pack_b", [P, WIDTH_B])
        pack_h = sb("pack_h", [P, P], BF16)

        def part(pack, layout, name):
            o, w = layout[name]
            return pack[:, o:o + w]

        ident, iota8, iota_slot, key15, ln_mul, ln_add, wqkv0, wo0, wffn0, wr, b2c = (
            part(pack_a, LAYOUT_A, n) for n in
            "ident iota8 iota_slot key15 ln_mul ln_add wqkv0 wo0 wffn0 wr b2c".split())
        wq1, wkv1, wo1f, ln_g, ln_b = (part(pack_b, LAYOUT_B, n) for n in "wq1 wkv1 wo1 ln_g ln_b".split())
        wo1 = wo1f.rearrange("p (c n) -> p c n", c=4)
        before = pack_h
        ones_rows = sb("ones_rows", [3, P], BF16)
        ones32 = sb("ones32", [PROJ, PROJ])
        minus_half = sb("minus_half", [P, 4])
        wu0 = sb("wu0", [NR, P])
        wp0 = sb("wp0", [PROJ, P])
        sim19 = sb("sim19", [PROJ, NG])
        simsq = sb("simsq", [PROJ, NG - NR])
        simrn = sb("simrn", [PROJ, NG - NR])
        bpcol = sb("bpcol", [PROJ, 1])
        bpwide = sb("bpwide", [PROJ, P])
        temp = sb("temp", [PROJ, 1])
        tscale = sb("tscale", [PROJ, 1])
        gates = sb("gates", [P, 4])
        tg = sb("tg", [P, 4])
        bias_rows = sb("bias_rows", [3, BIASES], BF16)
        lnb_wide = sb("lnb_wide", [P, 3])

        x_in = sb("x_in", [P, 2, P])
        ctx_a = sb("ctx_a", [P, 2, P])
        ctx_c = sb("ctx_c", [P, 2, P])
        mask_rows = sb("mask_rows", [1, B * P], BF16)
        x_res = sb("x_res", [P, 2, P])
        stats = sb("stats", [P, 4, 6])
        mv = sb("mv", [P, 4, 2])
        vr = sb("vr", [P, 4])
        vr2 = sb("vr2", [P, 4])
        rstd = sb("rstd", [P, 4])
        shift = sb("shift", [P, 4])
        xn = sb("xn", [P, 2, 4, P])
        xnT = sb("xnT", [P, 2, 4, P])
        qkv = sb("qkv", [P, 2, 3 * P])
        prod_qk = sb("prod_qk", [P, H0 * H0 * D0])
        prod_av = sb("prod_av", [P, H0 * H0 * D0])
        s0 = sb("s0", [P, H0 * H0])
        s0m = sb("s0m", [P, H0 * H0])
        e0 = sb("e0", [P, 2, H0 * H0])
        mx0 = sb("mx0", [P, H0])
        sum0 = sb("sum0", [P, H0])
        rs0 = sb("rs0", [P, H0])
        o0 = sb("o0", [P, P])
        o0n = sb("o0n", [P, P])
        o0T = sb("o0T", [P, P])
        x1 = sb("x1", [P, 2, P])
        pj = sb("pj", [P, 2, PJ])
        sq = sb("sq", [P, PROJ])
        ss = sb("ss", [P, 1])
        ssm = sb("ssm", [P, 1])
        rn = sb("rn", [P, 1])
        mxB = sb("mxB", [P, 1])
        dlB = sb("dlB", [P, NG])
        exB = sb("exB", [P, NG - NR])
        smB = sb("smB", [P, 1])
        rsB = sb("rsB", [P, 1])
        kk = sb("kk", [P, NR])
        km = sb("km", [P, 1])
        oh15 = sb("oh15", [P, NR])
        dw = sb("dw", [P, NR])
        dwT = sb("dwT", [NR, P])
        x2 = sb("x2", [P, 2, P])
        qT = sb("qT", [P, 2, 4, P])
        kT = sb("kT", [P, 2, 4, P])
        v1 = sb("v1", [P, 2, H1, D1 + 1])
        nmx1 = sb("nmx1", [P, 2, 4])
        p1 = sb("p1", [P, 2, 4, P])
        mask8 = p1[0:1, :, :, :].rearrange("p a b c -> p (a b c)").bitcast(U8)
        pT = sb("pT", [P, 2, 4, P])
        rs1 = sb("rs1", [P, 2, 4])
        o1 = sb("o1", [P, H1, D1])
        o1T = sb("o1T", [P, 4, P])
        x3 = sb("x3", [P, B, P])
        top8 = sb("top8", [P, 8])
        idx8 = sb("idx8", [P, 8], U32)
        idxf = sb("idxf", [P, 2])
        first = sb("first", [P, E])
        chosen = sb("chosen", [P, E], BF16)
        dlD = sb("dlD", [P, E])
        exD = sb("exD", [P, E])
        smD = sb("smD", [P, 1])
        rsD = sb("rsD", [P, 1])
        gate = sb("gate", [P, E])
        slot = sb("slot", [P, E])
        disp = sb("disp", [P, E, CAP])
        comb = sb("comb", [P, E, CAP])
        bufT = sb("bufT", [P, E, B * CAP])
        scratch = bufT[0:3, :, :].rearrange("p e n -> p (e n)")
        bias = scratch[:, 0:BIASES]
        bias_r = [scratch[:, n * BIASES:(n + 1) * BIASES] for n in (1, 2)]
        bias_p = [scratch[:, 3 * BIASES + n * (BIASES // 2):3 * BIASES + (n + 1) * (BIASES // 2)].bitcast(BF16)
                  for n in range(2)]
        bias_p.append(scratch[:, BIASES:BIASES + BIASES // 2].bitcast(BF16))
        yT = sb("yT", [P, B, E, CAP])
        combT = sb("combT", [HALF, B, 2, P])
        b1s = sb("b1s", [P, 2, HC])
        w1s = sb("w1s", [P, 2, HID])
        w2s = sb("w2s", [P, 2, HC, P])
        hT = sb("hT", [P, 2, HC, B * CAP // 2])
        yTs = prod_av[:, 8 * P:8 * P + 4 * ES].rearrange("p (b n) -> p b n", b=2)
        combs = prod_av[0:HALF, 0:8 * P].rearrange("p (b c n) -> p b c n", b=2, c=4)
        ys = prod_qk[0:HALF, 0:8 * P].rearrange("p (b c n) -> p b c n", b=2, c=4)
        o_out = prod_qk[:, 8 * P:12 * P].rearrange("p (b a n) -> p b a n", b=2, a=2)

        banks = [bank(f"bank{n}") for n in range(8)]
        PB = {piece: banks[n] for piece, n in BANK.items()}
        K0, K1, K2, K3, psX, psQ, psB, psD = banks

        s_small = sem("s_small")
        s_late = sem("s_late")
        s_bias = sem("s_bias")
        s_tanh = sem("s_tanh")
        s_setup_pool = sem("s_setup_pool")
        s_setup_dve = sem("s_setup_dve")
        s_setup_pe = sem("s_setup_pe")
        s_setup_act = sem("s_setup_act")
        LN = {n: sem(n) for n in LAG if n.startswith("ln_")}
        ln_var_scaled = sem("ln_var_scaled")
        TL = {n: sem(n) for n in LAG if n.startswith("t_") and n != "t_w_loaded"}
        t_w_loaded = [sem("t_w_loaded0"), sem("t_w_loaded1")]
        PAIRS = B // 2
        x_loaded = [sem("x_loaded0"), sem("x_loaded1")]
        ctxa_loaded = [sem("ctxa_loaded0"), sem("ctxa_loaded1")]
        ctxc_loaded = [sem("ctxc_loaded0"), sem("ctxc_loaded1")]
        xres_loaded = [sem("xres_loaded0"), sem("xres_loaded1")]
        S = {n: sem(n) for n in LAG if not n.startswith(("ln_", "t_")) and not n.endswith("_loaded")}

        def done(eng, s, k):
            if isinstance(k, int):
                k = min(k, B - 1)
                if k < 0:
                    return
            eng.wait_ge(s, k + 1)

        def ln_done(eng, piece, r):
            first, rounds = ROUNDS.get(piece, (0, LN_ROUNDS))
            if isinstance(r, int):
                r = min(r, first + rounds - 1)
                if r < first:
                    return
            eng.wait_ge(LN[piece], r + 1 - first)

        def expert_done(eng, piece, k):
            e = min(k - B, E - 1)
            if e < 0:
                return
            if piece == "t_w_loaded":
                eng.wait_ge(t_w_loaded[e % 2], 48 * (e // 2 + 1))
            else:
                eng.wait_ge(TL[piece], e + 1)

        def loaded(eng, sems, i, par, lag):
            if isinstance(i, int) and not 0 <= 2 * i + par - lag < B:
                return
            eng.wait_ge(sems[(par - lag) % 2], 16 * (i + (par - lag) // 2 + 1))

        def bank_free(eng, t, latest, earlier):
            for piece, k in latest + (earlier if isinstance(t, int) else []):
                if piece in LN:
                    ln_done(eng, piece, k)
                elif piece in TL:
                    expert_done(eng, piece, k)
                else:
                    done(eng, S[piece], k)

        def live(t, piece):
            if piece.startswith("t_"):
                return isinstance(t, int) and B <= t - LAG[piece] < B + E
            first, count = ROUNDS.get(piece, (0, LN_ROUNDS if piece.startswith("ln_") else B))
            return (not isinstance(t, int)) or first <= t - LAG[piece] < first + count

        def slot_live(r, n):
            return (not isinstance(r, int)) or 0 <= r - LN_LAG[n] < B

        def ln_slots(r, among=range(4)):
            on = [n for n in among if slot_live(r, n)]
            return on[0], on[-1] + 1

        def steps(eng, body, before_step={}):
            lo = LOOP_FROM
            hi = B
            for t in range(lo):
                if t in before_step:
                    before_step[t]()
                body(t // 2, t % 2, t)
            with eng.Fori(lo // 2, hi // 2) as i:
                body(i, 0, 2 * i)
                body(i, 1, 2 * i + 1)
            for t in range(hi, STEPS):
                body(t // 2, t % 2, t)

        def x3_at(k):
            return x3[:, k, :] if isinstance(k, int) else x3[:, ds(k, 1), :].rearrange("p a c -> p (a c)")

        def ln_input(n, i, par, piece):
            if n == 3:
                return x3_at(2 * i + par - LAG[piece] - LN_LAG[3])
            return (x_in, x1, x2)[n][:, (par - LAG[piece] - LN_LAG[n]) % 2, :]

        def xn_of(n, par, piece):
            return xn[:, (par - LAG[piece] + LN_LAG[n]) % 2, n, :]

        def xnT_of(n, par, piece):
            return xnT[:, (par - LAG[piece] + LN_LAG[n]) % 2, n, :]

        def mask_row(k):
            row = mask_rows[:, k * P:(k + 1) * P] if isinstance(k, int) else mask_rows[:, ds(k * P, P)]
            return bc(row, 1, 4)

        def pv_bank(g):
            return PB[f"pv_mm{g}"][:, 0:4 * (D1 + 1)].rearrange("p (h d) -> p h d", h=4)

        def bc(ap, axis, n):
            ap = ap.unsqueeze(axis)
            shape = list(ap.shape)
            shape[axis] = n
            return ap.broadcast_to(shape)

        E_LOOP = E // 2
        HB = B * CAP // 2
        e_w1_loaded = [sem("e_w1_loaded0"), sem("e_w1_loaded1")]
        e_w2_loaded = [sem("e_w2_loaded0"), sem("e_w2_loaded1")]
        e_h_mm, e_h_ready, e_y_mm, e_y_ready = sem("e_h_mm"), sem("e_h_ready"), sem("e_y_mm"), sem("e_y_ready")
        f_yTs, f_turned, f_ys, f_mm, f_out = sem("f_yTs"), sem("f_turned"), sem("f_ys"), sem("f_mm"), sem("f_out")
        f_combs = sem("f_combs")
        f_stored = [sem("f_stored0"), sem("f_stored1")]
        block = ctx.enter_context(nc.Block())

        small = [
            (pack_a[:, :], a["pack_a"]), (gates[:, 0:2], a["g_xattn"].partition_broadcast(P)),
            (gates[:, 2:4], a["g_ffn"].partition_broadcast(P)), (bias[:, :], a["biases"].partition_broadcast(3)),
            (sim19[:, :], a["sim19"]), (temp[:, :], a["temp"].partition_broadcast(PROJ)), (wp0[:, :], a["wp0"]),
            (bpcol[:, :], a["bp0"].rearrange("(p o) -> p o", o=1)), (wu0[:, :], a["wu0T"]),
        ]
        late = [(mask8[:, :], a["mask"].rearrange("b p -> (b p)").rearrange("(o n) -> o n", o=1)),
                (pack_b[:, :], a["pack_b"]), (pack_h[:, :], a["before"])]

        @block.sync
        def _(sp):
            def sample(dram, k):
                return dram[k] if isinstance(k, int) else dram[ds(k, 1)].rearrange("a p c -> (a p) c")

            def step(i, par, t):
                if live(t, "xres_loaded"):
                    k, p = t - LAG["xres_loaded"], (par - LAG["xres_loaded"]) % 2
                    done(sp, S["x1_ready"], k - 2)
                    sp.dma_start(x_res[:, p, :], sample(a["x"], k)).then_inc(xres_loaded[p], 16)
                if live(t, "x_loaded"):
                    k, p = t - LAG["x_loaded"], (par - LAG["x_loaded"]) % 2
                    ln_done(sp, "ln_xn01", k - 2)
                    sp.dma_start(x_in[:, p, :], sample(a["x"], k)).then_inc(x_loaded[p], 16)
                if live(t, "ctxc_loaded"):
                    k, p = t - LAG["ctxc_loaded"], (par - LAG["ctxc_loaded"]) % 2
                    done(sp, S["v_mm"], k - 2)
                    sp.dma_start(ctx_c[:, p, :], sample(a["ctxT"], k)).then_inc(ctxc_loaded[p], 16)
                if live(t, "t_w_loaded"):
                    k, p = t - LAG["t_w_loaded"], (par - LAG["t_w_loaded"]) % 2
                    expert_done(sp, "t_y_mm", k - 2)
                    e = k - B
                    sp.dma_start(w1s[:, p, :], a["W1"][e]).then_inc(t_w_loaded[p], 16)
                    sp.dma_start(b1s[:, p, :], a["b1T"][e]).then_inc(t_w_loaded[p], 16)
                    sp.dma_start(w2s[:, p, :, :], a["W2"][e].rearrange("(c p) n -> p c n", p=P)).then_inc(t_w_loaded[p],
                                                                                                          16)
                if live(t, "ctxa_loaded"):
                    k, p = t - LAG["ctxa_loaded"], (par - LAG["ctxa_loaded"]) % 2
                    done(sp, S["qkv_mm"], k - 2)
                    sp.dma_start(ctx_a[:, p, :], sample(a["ctxT"], k)).then_inc(ctxa_loaded[p], 16)

            for dst, src in small:
                sp.dma_start(dst, src).then_inc(s_small, 16)
            steps(sp, step, {0: lambda: [sp.dma_start(dst, src).then_inc(s_late, 16) for dst, src in late]})

            def weights(p, e):
                if isinstance(e, int) and e < 2:
                    expert_done(sp, "t_y_mm", B + E - 2 + e)
                else:
                    sp.wait_ge(e_h_mm, HC * (e - 1))
                    sp.wait_ge(e_h_ready, HC * (e - 1))
                w1 = a["W1"][e] if isinstance(e, int) else a["W1"][ds(e, 1)].rearrange("a p c -> (a p) c")
                b1 = a["b1T"][e] if isinstance(e, int) else a["b1T"][ds(e, 1)].rearrange("a p c -> (a p) c")
                w2 = a["W2"][e] if isinstance(e, int) else a["W2"][ds(e, 1)].rearrange("a p c -> (a p) c")
                sp.dma_start(w1s[:, p, :], w1).then_inc(e_w1_loaded[p], 16)
                sp.dma_start(b1s[:, p, :], b1).then_inc(e_w1_loaded[p], 16)
                if not (isinstance(e, int) and e < 2):
                    sp.wait_ge(e_y_mm, e - 1)
                sp.dma_start(w2s[:, p, :, :], w2.rearrange("(c p) n -> p c n", p=P)).then_inc(e_w2_loaded[p], 16)

            weights(0, 0)
            weights(1, 1)
            with sp.Fori(1, E_LOOP) as i:
                weights(0, 2 * i)
                weights(1, 2 * i + 1)

            def store(i, p, j):
                sp.wait_ge(f_out, j + 1)
                o = out[2 * j:2 * j + 2] if isinstance(j, int) else out[ds(2 * j, 2)]
                sp.dma_start(o.rearrange("b p c -> p b c"), o_out[:, p, :, :]).then_inc(f_stored[p], 16)

            with sp.Fori(0, PAIRS // 2) as i:
                store(i, 0, 2 * i)
                store(i, 1, 2 * i + 1)
            for p in range(2):
                sp.wait_ge(f_stored[p], 16 * (PAIRS // 2))

        @block.gpsimd
        def _(pool):
            nc.gpsimd.memset(minus_half[:, :], -0.5).then_inc(s_setup_pool, 1)
            nc.gpsimd.memset(ones32[:, :], 1.0).then_inc(s_setup_pool, 1)
            nc.gpsimd.memset(v1[:, 0, :, D1:D1 + 1], 1.0).then_inc(s_setup_pool, 1)
            nc.gpsimd.memset(v1[:, 1, :, D1:D1 + 1], 1.0).then_inc(s_setup_pool, 1)
            nc.gpsimd.memset(ones_rows[:, :], 1.0).then_inc(s_setup_pool, 1)
            pool.wait_ge(s_small, 16 * len(small))
            nc.gpsimd.tensor_tensor(simsq[:, :], sim19[:, NR:NG], sim19[:, NR:NG], ALU.mult).then_inc(s_setup_pool, 1)
            pool.wait_ge(s_setup_dve, 1)
            pool.wait_ge(s_setup_pool, 6)
            nc.gpsimd.tensor_tensor(simrn[:, :], simrn[:, :], minus_half[0:PROJ, 0:NG - NR],
                                    ALU.pow).then_inc(s_setup_pool, 1)

            def step(i, par, t):
                if live(t, "av_prod0"):
                    k, p = t - LAG["av_prod0"], (par - LAG["av_prod0"]) % 2
                    done(pool, S["e0_ready"], k)
                    h = slice(0 * H0 // 4, 1 * H0 // 4)
                    pav = prod_av[:, :].rearrange("p (h d g) -> p h d g", h=H0, d=D0)[:, h, :, :]
                    ev = bc(e0[:, p, :].rearrange("p (h g) -> p h g", h=H0)[:, h, :], 2, D0)
                    vv = bc(qkv[:, p, 2 * P:3 * P].rearrange("p (g d) -> p d g", g=H0), 1, H0 // 4)
                    nc.gpsimd.tensor_tensor(pav, ev, vv, ALU.mult).then_inc(S["av_prod0"], 1)
                if live(t, "av_prod3"):
                    k, p = t - LAG["av_prod3"], (par - LAG["av_prod3"]) % 2
                    h = slice(3 * H0 // 4, 4 * H0 // 4)
                    pav = prod_av[:, :].rearrange("p (h d g) -> p h d g", h=H0, d=D0)[:, h, :, :]
                    ev = bc(e0[:, p, :].rearrange("p (h g) -> p h g", h=H0)[:, h, :], 2, D0)
                    vv = bc(qkv[:, p, 2 * P:3 * P].rearrange("p (g d) -> p d g", g=H0), 1, H0 // 4)
                    nc.gpsimd.tensor_tensor(pav, ev, vv, ALU.mult).then_inc(S["av_prod3"], 1)
                if live(t, "ln_v2"):
                    r = t - LAG["ln_v2"]
                    ln_done(pool, "ln_mv", r)
                    lo, hi = ln_slots(r)
                    nc.gpsimd.tensor_tensor(vr[:, lo:hi], mv[:, lo:hi, 1], ln_mul[:, lo:hi],
                                            ALU.mult).then_inc(ln_var_scaled, 1)
                    pool.wait_ge(ln_var_scaled, r + 1)
                    nc.gpsimd.tensor_tensor(vr2[:, lo:hi], vr[:, lo:hi], ln_add[:, lo:hi],
                                            ALU.add).then_inc(LN["ln_v2"], 1)
                if live(t, "ln_rstd"):
                    r = t - LAG["ln_rstd"]
                    ln_done(pool, "ln_v2", r)
                    lo, hi = ln_slots(r)
                    nc.gpsimd.tensor_tensor(rstd[:, lo:hi], vr2[:, lo:hi], minus_half[:, lo:hi],
                                            ALU.pow).then_inc(LN["ln_rstd"], 1)
                if live(t, "av_prod2"):
                    k, p = t - LAG["av_prod2"], (par - LAG["av_prod2"]) % 2
                    h = slice(2 * H0 // 4, 3 * H0 // 4)
                    pav = prod_av[:, :].rearrange("p (h d g) -> p h d g", h=H0, d=D0)[:, h, :, :]
                    ev = bc(e0[:, p, :].rearrange("p (h g) -> p h g", h=H0)[:, h, :], 2, D0)
                    vv = bc(qkv[:, p, 2 * P:3 * P].rearrange("p (g d) -> p d g", g=H0), 1, H0 // 4)
                    nc.gpsimd.tensor_tensor(pav, ev, vv, ALU.mult).then_inc(S["av_prod2"], 1)
                if live(t, "av_prod1"):
                    k, p = t - LAG["av_prod1"], (par - LAG["av_prod1"]) % 2
                    h = slice(1 * H0 // 4, 2 * H0 // 4)
                    pav = prod_av[:, :].rearrange("p (h d g) -> p h d g", h=H0, d=D0)[:, h, :, :]
                    ev = bc(e0[:, p, :].rearrange("p (h g) -> p h g", h=H0)[:, h, :], 2, D0)
                    vv = bc(qkv[:, p, 2 * P:3 * P].rearrange("p (g d) -> p d g", g=H0), 1, H0 // 4)
                    nc.gpsimd.tensor_tensor(pav, ev, vv, ALU.mult).then_inc(S["av_prod1"], 1)
                if live(t, "qk_prod_rest"):
                    k, p = t - LAG["qk_prod_rest"], (par - LAG["qk_prod_rest"]) % 2
                    done(pool, S["qkv_ready"], k)
                    h = slice(H_DVE, H0)
                    pqk = prod_qk[:, :].rearrange("p (h g d) -> p h g d", h=H0, g=H0)[:, h, :, :]
                    qv = bc(qkv[:, p, 0:P].rearrange("p (h d) -> p h d", h=H0)[:, h, :], 2, H0)
                    kv = bc(qkv[:, p, P:2 * P].rearrange("p (g d) -> p g d", g=H0), 1, h.stop - h.start)
                    nc.gpsimd.tensor_tensor(pqk, qv, kv, ALU.mult).then_inc(S["qk_prod_rest"], 1)
                if live(t, "rn_ready"):
                    k = t - LAG["rn_ready"]
                    done(pool, S["ssm_ready"], k)
                    nc.gpsimd.tensor_tensor(rn[:, :], ssm[:, :], minus_half[:, 0:1], ALU.pow).then_inc(S["rn_ready"], 1)
                if live(t, "comb_ready"):
                    k = t - LAG["comb_ready"]
                    done(pool, S["disp_ready"], k)
                    done(pool, S["comb_turned"], k - 1)
                    nc.gpsimd.tensor_tensor(comb[:, :, :], disp[:, :, :], bc(gate[:, :], 2, CAP),
                                            ALU.mult).then_inc(S["comb_ready"], 1)
                if live(t, "o0n_ready"):
                    k, p = t - LAG["o0n_ready"], (par - LAG["o0n_ready"]) % 2
                    done(pool, S["o0_ready0"], k)
                    nc.gpsimd.tensor_tensor(o0n[:, :].rearrange("p (h d) -> p h d", h=H0),
                                            o0[:, :].rearrange("p (h d) -> p h d", h=H0),
                                            bc(rs0[:, :], 2, D0), ALU.mult).then_inc(S["o0n_ready"], 1)

            steps(pool, step)

        @block.scalar
        def _(act):
            act.wait_ge(s_small, 16 * len(small))
            nc.scalar.activation(tg[:, :], gates[:, :], ACT.Tanh).then_inc(s_tanh, 1)
            act.wait_ge(s_setup_dve, 2)
            nc.scalar.activation(tscale[:, :], temp[:, :], ACT.Exp).then_inc(s_setup_act, 1)

            def step(i, par, t):
                if live(t, "combT_ready"):
                    k = t - LAG["combT_ready"]
                    done(act, S["comb_turned"], k)
                if live(t, "pT_ready0"):
                    k, p = t - LAG["pT_ready0"], (par - LAG["pT_ready0"]) % 2
                    done(act, S["p_turned0"], k)
                    nc.scalar.copy(pT[:, 0, :, :],
                                   PB["p_turned0"][:, :].rearrange("p (h n) -> p h n", h=4)).then_inc(S["pT_ready0"], 1)
                if live(t, "combT_ready"):
                    k, p = t - LAG["combT_ready"], (par - LAG["combT_ready"]) % 2
                    c = combT[:, k, :, :] if isinstance(k, int) else \
                        combT[:, ds(k, 1), :, :].rearrange("p a c n -> p (a c) n")
                    nc.scalar.copy(c,
                                   PB["comb_turned"][0:HALF, 0:2 * P].rearrange("p (c n) -> p c n",
                                                                                c=2)).then_inc(S["combT_ready"], 1)
                if live(t, "pT_ready1"):
                    k, p = t - LAG["pT_ready1"], (par - LAG["pT_ready1"]) % 2
                    done(act, S["p_turned1"], k)
                    nc.scalar.copy(pT[:, 1, :, :],
                                   PB["p_turned1"][:, :].rearrange("p (h n) -> p h n", h=4)).then_inc(S["pT_ready1"], 1)
                if live(t, "exD_ready"):
                    k = t - LAG["exD_ready"]
                    done(act, S["idx_ready"], k)
                    nc.scalar.activation(exD[:, :], dlD[:, :], ACT.Exp, accum_out=smD[:, :]).then_inc(S["exD_ready"], 1)
                if live(t, "ln_xn01"):
                    r, p = t - LAG["ln_xn01"], (par - LAG["ln_xn01"]) % 2
                    ln_done(act, "ln_shift", r)
                    lo, hi = ln_slots(r, (0, 1))
                    for n in range(lo, hi):
                        last = nc.scalar.activation(xn[:, p, n, :], ln_input(n, i, par, "ln_xn01"), ACT.Identity,
                                                    bias=shift[:, n:n + 1],
                                                    scale=rstd[:, n:n + 1])
                    last.then_inc(LN["ln_xn01"], 1)
                if live(t, "bufT_ready"):
                    k = t - LAG["bufT_ready"]
                    done(act, S["disp_mm"], k)
                if live(t, "v_ready"):
                    k, p = t - LAG["v_ready"], (par - LAG["v_ready"]) % 2
                    done(act, S["v_mm"], k)
                    nc.scalar.copy(v1[:, p, :, 0:D1],
                                   PB["v_mm"][:, :].rearrange("p (h d) -> p h d", h=H1)).then_inc(S["v_ready"], 1)
                if live(t, "bufT_ready"):
                    k, p = t - LAG["bufT_ready"], (par - LAG["bufT_ready"]) % 2
                    b = bufT[:, :, k * CAP:(k + 1) * CAP] if isinstance(k, int) else bufT[:, :, ds(k * CAP, CAP)]
                    nc.scalar.copy(b,
                                   PB["disp_mm"][:, 0:ES].rearrange("p (e s) -> p e s", e=E)).then_inc(S["bufT_ready"], 1)
                if live(t, "ln_xnT"):
                    r, p = t - LAG["ln_xnT"], (par - LAG["ln_xnT"]) % 2
                    ln_done(act, "ln_turned", r)
                    lo, hi = ln_slots(r)
                    nc.scalar.copy(xnT[:, p, lo:hi, :],
                                   PB["ln_turned"][:, lo * P:hi * P].rearrange("p (s n) -> p s n",
                                                                               n=P)).then_inc(LN["ln_xnT"], 1)
                if live(t, "qkv_ready"):
                    k, p = t - LAG["qkv_ready"], (par - LAG["qkv_ready"]) % 2
                    done(act, S["qkv_mm"], k)
                    nc.scalar.copy(qkv[:, p, :], PB["qkv_mm"][:, 0:3 * P]).then_inc(S["qkv_ready"], 1)
                if live(t, "pj_ready"):
                    k, p = t - LAG["pj_ready"], (par - LAG["pj_ready"]) % 2
                    done(act, S["ffn0_mm"], k)
                    nc.scalar.copy(pj[:, p, :], PB["ffn0_mm"][:, P:P + PJ]).then_inc(S["pj_ready"], 1)
                if live(t, "o1T_ready"):
                    k, p = t - LAG["o1T_ready"], (par - LAG["o1T_ready"]) % 2
                    done(act, S["o1_turned"], k)
                    nc.scalar.copy(o1T[:, :, :],
                                   PB["o1_turned"][:, :].rearrange("p (c n) -> p c n", c=4)).then_inc(S["o1T_ready"], 1)
                if live(t, "ss_ready"):
                    k, p = t - LAG["ss_ready"], (par - LAG["ss_ready"]) % 2
                    done(act, S["pj_ready"], k)
                    nc.scalar.activation(sq[:, :], pj[:, p, 0:PROJ], ACT.Square,
                                         accum_out=ss[:, :]).then_inc(S["ss_ready"], 1)
                if live(t, "qT_ready"):
                    k, p = t - LAG["qT_ready"], (par - LAG["qT_ready"]) % 2
                    done(act, S["qT_mm"], k)
                    nc.scalar.copy(qT[:, p, :, :],
                                   PB["qT_mm"][:, :].rearrange("p (c n) -> p c n", c=4)).then_inc(S["qT_ready"], 1)
                if live(t, "t_h_ready1"):
                    k, p = t - LAG["t_h_ready1"], (par - LAG["t_h_ready1"]) % 2
                    expert_done(act, "t_h_mm1", k)
                    nc.scalar.activation(hT[:, 0, 1, :], PB["t_h_mm1"][:, 0:HB], ACT.Relu,
                                         bias=b1s[:, p, 1:2]).then_inc(TL["t_h_ready1"], 1)
                if live(t, "kT_ready"):
                    k, p = t - LAG["kT_ready"], (par - LAG["kT_ready"]) % 2
                    done(act, S["kT_mm"], k)
                    nc.scalar.copy(kT[:, p, :, :],
                                   PB["kT_mm"][:, :].rearrange("p (c n) -> p c n", c=4)).then_inc(S["kT_ready"], 1)
                if live(t, "exB_ready"):
                    k = t - LAG["exB_ready"]
                    done(act, S["rn_ready"], k)
                    done(act, S["dlB_ready"], k)
                    nc.scalar.activation(exB[:, :], dlB[:, NR:NG], ACT.Exp, scale=rn[:, 0:1],
                                         accum_out=smB[:, :]).then_inc(S["exB_ready"], 1)
                if live(t, "t_h_ready0"):
                    k, p = t - LAG["t_h_ready0"], (par - LAG["t_h_ready0"]) % 2
                    expert_done(act, "t_h_mm0", k)
                    nc.scalar.activation(hT[:, 0, 0, :], PB["t_h_mm0"][:, 0:HB], ACT.Relu,
                                         bias=b1s[:, p, 0:1]).then_inc(TL["t_h_ready0"], 1)
                if live(t, "t_h_ready2"):
                    k, p = t - LAG["t_h_ready2"], (par - LAG["t_h_ready2"]) % 2
                    expert_done(act, "t_h_mm2", k)
                    nc.scalar.activation(hT[:, 0, 2, :], PB["t_h_mm2"][:, 0:HB], ACT.Relu,
                                         bias=b1s[:, p, 2:3]).then_inc(TL["t_h_ready2"], 1)
                if live(t, "o0T_ready"):
                    k = t - LAG["o0T_ready"]
                    done(act, S["o0_turned"], k)
                    nc.scalar.copy(o0T[:, :], PB["o0_turned"][:, 0:P]).then_inc(S["o0T_ready"], 1)
                if live(t, "e0_ready"):
                    k, p = t - LAG["e0_ready"], (par - LAG["e0_ready"]) % 2
                    done(act, S["s0m_ready"], k)
                    nc.scalar.activation(e0[:, p, :], s0m[:, :], ACT.Exp,
                                         scale=float(D0) ** -0.5).then_inc(S["e0_ready"], 1)
                if live(t, "dwT_ready"):
                    k = t - LAG["dwT_ready"]
                    done(act, S["dw_turned"], k)
                    nc.scalar.copy(dwT[:, :], PB["dw_turned"][0:NR, 0:P]).then_inc(S["dwT_ready"], 1)
                if live(t, "p1_ready0"):
                    k = t - LAG["p1_ready0"]
                    done(act, S["nmx_ready0"], k)
                    for c in range(4):
                        last = nc.scalar.activation(p1[:, 0, c, :], PB["s1_mm0"][:, c * P:(c + 1) * P], ACT.Exp,
                                                    bias=nmx1[:, 0, c:c + 1])
                    last.then_inc(S["p1_ready0"], 1)
                if live(t, "t_h_ready3"):
                    k, p = t - LAG["t_h_ready3"], (par - LAG["t_h_ready3"]) % 2
                    expert_done(act, "t_h_mm3", k)
                    nc.scalar.activation(hT[:, 0, 3, :], PB["t_h_mm3"][:, 0:HB], ACT.Relu,
                                         bias=b1s[:, p, 3:4]).then_inc(TL["t_h_ready3"], 1)
                if live(t, "p1_ready1"):
                    k = t - LAG["p1_ready1"]
                    done(act, S["nmx_ready1"], k)
                    for c in range(4):
                        last = nc.scalar.activation(p1[:, 1, c, :], PB["s1_mm1"][:, c * P:(c + 1) * P], ACT.Exp,
                                                    bias=nmx1[:, 1, c:c + 1])
                    last.then_inc(S["p1_ready1"], 1)

            steps(act, step)

            def expert(i, p, e):
                act.wait_ge(e_w1_loaded[p], 32 * (i + 1))
                for c in range(HC):
                    act.wait_ge(e_h_mm, HC * e + c + 1)
                    if not (isinstance(e, int) and e < 2):
                        act.wait_ge(e_y_mm, e - 1)
                    nc.scalar.activation(hT[:, p, c, :], (K0, K1, K2, K3)[c][:, 0:HB], ACT.Relu,
                                         bias=b1s[:, p, c:c + 1]).then_inc(e_h_ready, 1)

            expert_done(act, "t_y_mm", B + E - 1)
            expert(0, 0, 0)
            expert(0, 1, 1)
            with act.Fori(1, E_LOOP) as i:
                expert(i, 0, 2 * i)
                expert(i, 1, 2 * i + 1)

            def combine(p, j):
                act.wait_ge(f_turned, j + 1)
                if not (isinstance(j, int) and j < 2):
                    act.wait_ge(f_mm, j - 1)
                nc.scalar.activation(ys[:, p, :, :], (K0, K1)[p][0:HALF, :].rearrange("p (c n) -> p c n", c=4), ACT.Copy,
                                     scale=tg[0:HALF, 3:4]).then_inc(f_ys, 1)

            combine(0, 0)
            combine(1, 1)
            with act.Fori(1, PAIRS // 2) as i:
                combine(0, 2 * i)
                combine(1, 2 * i + 1)

        @block.tensor
        def _(pe):
            mm = nc.tensor.matmul
            pe.wait_ge(s_small, 16 * len(small))
            pe.wait_ge(s_setup_pool, 6)
            mm(psB[0:PROJ, 0:NG - NR], ones32[:, :], simsq[:, :], start=True, stop=True).then_inc(s_setup_pe, 1)
            pe.wait_ge(s_setup_dve, 3)
            mm(psQ[:, 0:NG], wp0[:, :], sim19[:, :], start=True, stop=True).then_inc(s_setup_pe, 1)
            mm(psX[:, 0:NG], bpwide[:, :], sim19[:, :], start=True, stop=True).then_inc(s_setup_pe, 1)
            pe.wait_ge(s_late, 16 * len(late))
            pe.wait_ge(s_setup_dve, 6)
            mm(K0[0:3, :], lnb_wide[:, :], wq1[:, :], start=True, stop=True).then_inc(s_setup_pe, 1)

            def biased(o, name, *operands, rows=slice(0, P)):
                at, w = BIAS_AT[name]
                mm(o, *operands, start=True, stop=False)
                return mm(o, ones_rows[:, :], bias_rows[:, at:at + w], start=False, stop=True)

            def step(i, par, t):
                if live(t, "s1_mm0"):
                    k, p = t - LAG["s1_mm0"], (par - LAG["s1_mm0"]) % 2
                    done(pe, S["qT_ready"], k)
                    r = slice(0 * D1, 1 * D1)
                    for c in range(4):
                        mm(PB["s1_mm0"][:, c * P:(c + 1) * P], qT[r, p, c, :], kT[r, p, c, :], start=(c == 0),
                           stop=False, skip_group_check=True)
                    mm(PB["s1_mm0"][:, :], ones_rows[0:1, :], mask_row(k), start=False, stop=True,
                       skip_group_check=True).then_inc(S["s1_mm0"], 1)
                if live(t, "o0_turned"):
                    k = t - LAG["o0_turned"]
                    done(pe, S["o0n_ready"], k)
                    bank_free(pe, t, [("kT_ready", t - 1 - LAG["kT_mm"])],
                              [("bufT_ready", t - 1 - LAG["disp_mm"]), ("t_h_ready3", t - 1 - LAG["t_h_mm3"]),
                               ("o0T_ready", t - 1 - LAG["o0_turned"])])
                    nc.tensor.transpose(PB["o0_turned"][:, 0:P], o0n[:, :], ident[:, :]).then_inc(S["o0_turned"], 1)
                if live(t, "s1_mm1"):
                    k, p = t - LAG["s1_mm1"], (par - LAG["s1_mm1"]) % 2
                    r = slice(1 * D1, 2 * D1)
                    for c in range(4):
                        mm(PB["s1_mm1"][:, c * P:(c + 1) * P], qT[r, p, c, :], kT[r, p, c, :], start=(c == 0),
                           stop=False, skip_group_check=True)
                    mm(PB["s1_mm1"][:, :], ones_rows[0:1, :], mask_row(k), start=False, stop=True,
                       skip_group_check=True).then_inc(S["s1_mm1"], 1)
                if live(t, "y0_mm"):
                    k = t - LAG["y0_mm"]
                    done(pe, S["o0T_ready"], k)
                    biased(PB["y0_mm"][:, 0:P], "bo0", o0T[:, :], wo0[:, :]).then_inc(S["y0_mm"], 1)
                if live(t, "dw_turned"):
                    k = t - LAG["dw_turned"]
                    done(pe, S["dw_ready"], k)
                    bank_free(pe, t, [("qkv_ready", t - 1 - LAG["qkv_mm"])],
                              [("t_h_ready2", t - 1 - LAG["t_h_mm2"]), ("o1_ready1", t - 1 - LAG["pv_mm1"]),
                               ("combT_ready", t - 1 - LAG["comb_turned"]), ("dwT_ready", t - 1 - LAG["dw_turned"])])
                    nc.tensor.transpose(PB["dw_turned"][0:NR, 0:P], dw[:, :], ident[:, :]).then_inc(S["dw_turned"], 1)
                if live(t, "t_h_mm3"):
                    k, p = t - LAG["t_h_mm3"], (par - LAG["t_h_mm3"]) % 2
                    bank_free(pe, t, [("o0T_ready", t - LAG["o0_turned"]), ("kT_ready", t - 1 - LAG["kT_mm"]),
                               ("bufT_ready", t - 1 - LAG["disp_mm"]), ("t_h_ready3", t - 1 - LAG["t_h_mm3"])], [])
                    mm(PB["t_h_mm3"][:, 0:HB], w1s[:, p, 3 * P:4 * P], bufT[:, k - B, 0:HB], start=True,
                       stop=True).then_inc(TL["t_h_mm3"], 1)
                if live(t, "pos_mm"):
                    bank_free(pe, t, [("x3_ready", t - 1 - LAG["y1_mm"])],
                              [("t_y_ready", t - 1 - LAG["t_y_mm"]), ("slot_ready", t - 1 - LAG["pos_mm"])])
                    mm(PB["pos_mm"][:, 0:E], before[:, :], chosen[:, :], start=True, stop=True).then_inc(S["pos_mm"], 1)
                if live(t, "res0_mm"):
                    k = t - LAG["res0_mm"]
                    done(pe, S["dwT_ready"], k)
                    mm(PB["ffn0_mm"][:, 0:P], dwT[:, :], wu0[:, :], start=False, stop=True,
                       skip_group_check=True).then_inc(S["res0_mm"], 1)
                if live(t, "v_mm"):
                    k, p = t - LAG["v_mm"], (par - LAG["v_mm"]) % 2
                    mm(PB["v_mm"][:, :], ctx_c[:, p, :], wkv1[:, H1 * D1:], start=True, stop=True).then_inc(S["v_mm"], 1)
                if live(t, "router_mm"):
                    bank_free(pe, t, [("x1_ready", t - LAG["y0_mm"])],
                              [("t_h_ready1", t - 1 - LAG["t_h_mm1"]), ("idx_ready", t - 1 - LAG["router_mm"])])
                    biased(PB["router_mm"][:, 0:E], "br", xnT_of(3, par, "router_mm"),
                           wr[:, :]).then_inc(S["router_mm"], 1)
                if live(t, "comb_turned"):
                    k, p = t - LAG["comb_turned"], (par - LAG["comb_turned"]) % 2
                    done(pe, S["comb_ready"], k)
                    bank_free(pe, t, [("dwT_ready", t - LAG["dw_turned"])],
                              [("t_h_ready2", t - 1 - LAG["t_h_mm2"]), ("qkv_ready", t - 1 - LAG["qkv_mm"]),
                               ("o1_ready1", t - 1 - LAG["pv_mm1"]), ("combT_ready", t - 1 - LAG["comb_turned"])])
                    cm = comb[:, :, :].rearrange("p e s -> p (e s)")
                    for c in range(2):
                        last = nc.tensor.transpose(PB["comb_turned"][0:HALF, c * P:(c + 1) * P],
                                                   cm[:, c * HALF:(c + 1) * HALF], ident[:, :])
                    last.then_inc(S["comb_turned"], 1)
                if live(t, "p_turned0"):
                    k = t - LAG["p_turned0"]
                    done(pe, S["p1_ready0"], k)
                    bank_free(pe, t, [("x2_ready", t - 1 - LAG["ffn0_mm"])],
                              [("o1_ready0", t - 1 - LAG["pv_mm0"]), ("pT_ready0", t - 1 - LAG["p_turned0"])])
                    for c in range(4):
                        last = nc.tensor.transpose(PB["p_turned0"][:, c * P:(c + 1) * P], p1[:, 0, c, :], ident[:, :])
                    last.then_inc(S["p_turned0"], 1)
                if live(t, "t_y_mm"):
                    k, p = t - LAG["t_y_mm"], (par - LAG["t_y_mm"]) % 2
                    expert_done(pe, "t_h_ready3", k)
                    bank_free(pe, t, [("slot_ready", t - LAG["pos_mm"]), ("x3_ready", t - 1 - LAG["y1_mm"]),
                               ("t_y_ready", t - 1 - LAG["t_y_mm"])], [])
                    for c in range(HC):
                        last = mm(PB["t_y_mm"][:, 0:HB], w2s[:, p, c, :], hT[:, 0, c, :], start=(c == 0),
                                  stop=(c == HC - 1))
                    last.then_inc(TL["t_y_mm"], 1)
                if live(t, "p_turned1"):
                    k = t - LAG["p_turned1"]
                    done(pe, S["p1_ready1"], k)
                    for c in range(4):
                        last = nc.tensor.transpose(PB["p_turned1"][:, c * P:(c + 1) * P], p1[:, 1, c, :], ident[:, :])
                    last.then_inc(S["p_turned1"], 1)
                if live(t, "pv_mm0"):
                    k, p = t - LAG["pv_mm0"], (par - LAG["pv_mm0"]) % 2
                    done(pe, S["pT_ready0"], k)
                    for c in range(4):
                        last = mm(PB["pv_mm0"][:, c * (D1 + 1):(c + 1) * (D1 + 1)], pT[:, 0, c, :],
                                  v1[:, p, 2 * c + 0, :], start=True, stop=True)
                    last.then_inc(S["pv_mm0"], 1)
                if live(t, "disp_mm"):
                    k, p = t - LAG["disp_mm"], (par - LAG["disp_mm"]) % 2
                    done(pe, S["disp_ready"], k)
                    mm(PB["disp_mm"][:, 0:ES], xn_of(3, par, "disp_mm"), disp[:, :, :].rearrange("p e s -> p (e s)"),
                       start=True, stop=True).then_inc(S["disp_mm"], 1)
                if live(t, "pv_mm1"):
                    k, p = t - LAG["pv_mm1"], (par - LAG["pv_mm1"]) % 2
                    done(pe, S["pT_ready1"], k)
                    for c in range(4):
                        last = mm(PB["pv_mm1"][:, c * (D1 + 1):(c + 1) * (D1 + 1)], pT[:, 1, c, :],
                                  v1[:, p, 2 * c + 1, :], start=True, stop=True)
                    last.then_inc(S["pv_mm1"], 1)
                if live(t, "t_h_mm1"):
                    k, p = t - LAG["t_h_mm1"], (par - LAG["t_h_mm1"]) % 2
                    expert_done(pe, "t_w_loaded", k)
                    bank_free(pe, t, [("idx_ready", t - LAG["router_mm"]), ("x1_ready", t - LAG["y0_mm"]),
                               ("t_h_ready1", t - 1 - LAG["t_h_mm1"])], [])
                    mm(PB["t_h_mm1"][:, 0:HB], w1s[:, p, 1 * P:2 * P], bufT[:, k - B, 0:HB], start=True,
                       stop=True).then_inc(TL["t_h_mm1"], 1)
                if live(t, "ln_turned"):
                    r, p = t - LAG["ln_turned"], (par - LAG["ln_turned"]) % 2
                    ln_done(pe, "ln_xn01", r)
                    ln_done(pe, "ln_xn23", r)
                    lo, hi = ln_slots(r)
                    for n in range(lo, hi):
                        last = nc.tensor.transpose(PB["ln_turned"][:, n * P:(n + 1) * P], xn[:, p, n, :], ident[:, :])
                    last.then_inc(LN["ln_turned"], 1)
                if live(t, "o1_turned"):
                    k = t - LAG["o1_turned"]
                    done(pe, S["o1_ready1"], k)
                    for c in range(4):
                        last = nc.tensor.transpose(PB["o1_turned"][:, c * P:(c + 1) * P], o1[:, 2 * c:2 * c + 2, :],
                                                   ident[:, :])
                    last.then_inc(S["o1_turned"], 1)
                if live(t, "t_h_mm0"):
                    k, p = t - LAG["t_h_mm0"], (par - LAG["t_h_mm0"]) % 2
                    bank_free(pe, t, [("v_ready", t - LAG["v_mm"]), ("t_h_ready0", t - 1 - LAG["t_h_mm0"])], [])
                    mm(PB["t_h_mm0"][:, 0:HB], w1s[:, p, 0 * P:1 * P], bufT[:, k - B, 0:HB], start=True,
                       stop=True).then_inc(TL["t_h_mm0"], 1)
                if live(t, "qkv_mm"):
                    k, p = t - LAG["qkv_mm"], (par - LAG["qkv_mm"]) % 2
                    loaded(pe, ctxa_loaded, i, par, 2)
                    ln_done(pe, "ln_xnT", k)
                    at, _ = BIAS_AT["qkv0"]
                    mm(PB["qkv_mm"][:, 0:P], xnT_of(0, par, "qkv_mm"), wqkv0[:, 0:P], start=True, stop=False,
                       skip_group_check=True)
                    mm(PB["qkv_mm"][:, P:3 * P], ctx_a[:, p, :], wqkv0[:, P:3 * P], start=False, stop=False,
                       skip_group_check=True)
                    mm(PB["qkv_mm"][:, 0:3 * P], ones_rows[:, :], bias_rows[:, at:at + 3 * P], start=False, stop=True,
                       skip_group_check=True).then_inc(S["qkv_mm"], 1)
                if live(t, "ffn0_mm"):
                    k = t - LAG["ffn0_mm"]
                    ln_done(pe, "ln_xnT", k + LN_LAG[1])
                    biased(PB["ffn0_mm"][:, 0:P + PJ], "ffn0", xnT_of(1, par, "ffn0_mm"),
                           wffn0[:, :]).then_inc(S["ffn0_mm"], 1)
                if live(t, "kT_mm"):
                    k, p = t - LAG["kT_mm"], (par - LAG["kT_mm"]) % 2
                    loaded(pe, ctxc_loaded, i, par, 4)
                    for c in range(4):
                        last = mm(PB["kT_mm"][:, c * P:(c + 1) * P], wkv1[:, c * P:(c + 1) * P], ctx_c[:, p, :],
                                  start=True, stop=True)
                    last.then_inc(S["kT_mm"], 1)
                if live(t, "qT_mm"):
                    k = t - LAG["qT_mm"]
                    ln_done(pe, "ln_xnT", k + LN_LAG[2])
                    at, _ = BIAS_AT["q1"]
                    for c in range(4):
                        o = PB["qT_mm"][:, c * P:(c + 1) * P]
                        mm(o, wq1[:, c * P:(c + 1) * P], xnT_of(2, par, "qT_mm"), start=True, stop=False)
                        last = mm(o, bias_rows[:, at + c * P:at + (c + 1) * P], ones_rows[:, :], start=False, stop=True)
                    last.then_inc(S["qT_mm"], 1)
                if live(t, "t_h_mm2"):
                    k, p = t - LAG["t_h_mm2"], (par - LAG["t_h_mm2"]) % 2
                    bank_free(pe, t, [("qkv_ready", t - LAG["qkv_mm"]), ("o1_ready1", t - LAG["pv_mm1"]),
                               ("combT_ready", t - LAG["comb_turned"]), ("dwT_ready", t - LAG["dw_turned"]),
                               ("t_h_ready2", t - 1 - LAG["t_h_mm2"])], [])
                    mm(PB["t_h_mm2"][:, 0:HB], w1s[:, p, 2 * P:3 * P], bufT[:, k - B, 0:HB], start=True,
                       stop=True).then_inc(TL["t_h_mm2"], 1)
                if live(t, "y1_mm"):
                    k = t - LAG["y1_mm"]
                    done(pe, S["o1T_ready"], k)
                    bank_free(pe, t, [("slot_ready", t - LAG["pos_mm"])],
                              [("t_y_ready", t - LAG["t_y_mm"]), ("x3_ready", t - 1 - LAG["y1_mm"])])
                    for c in range(4):
                        last = mm(PB["y1_mm"][:, 0:P], o1T[:, c, :], wo1[:, c, :], start=(c == 0), stop=(c == 3))
                    last.then_inc(S["y1_mm"], 1)

            pe.wait_ge(s_setup_dve, 8)
            steps(pe, step, {5: lambda: pe.wait_ge(s_setup_dve, 11)})

            pe.wait_ge(S["bufT_ready"], B)
            pe.wait_ge(S["combT_ready"], B)
            expert_done(pe, "t_y_ready", B + E - 1)

            def up(i, p, e):
                pe.wait_ge(e_w1_loaded[p], 32 * (i + 1))
                for c in range(HC):
                    if not (isinstance(e, int) and e == 0):
                        pe.wait_ge(e_h_ready, HC * (e - 1) + c + 1)
                    rhs = bufT[:, e, HB:2 * HB] if isinstance(e, int) else \
                        bufT[:, ds(e, 1), HB:2 * HB].rearrange("p a n -> p (a n)")
                    mm((K0, K1, K2, K3)[c][:, 0:HB], w1s[:, p, c * P:(c + 1) * P], rhs, start=True,
                       stop=True).then_inc(e_h_mm, 1)

            def down(i, p, e):
                pe.wait_ge(e_w2_loaded[p], 16 * (i + 1))
                if not (isinstance(e, int) and e < 2):
                    pe.wait_ge(e_y_ready, e - 1)
                pe.wait_ge(e_h_ready, HC * (e + 1))
                for c in range(HC):
                    last = mm((psX, psQ)[p][:, 0:HB], w2s[:, p, c, :], hT[:, p, c, :], start=(c == 0), stop=(c == HC - 1))
                last.then_inc(e_y_mm, 1)

            up(0, 0, 0)
            up(0, 1, 1)
            down(0, 0, 0)
            with pe.Fori(1, E_LOOP) as i:
                up(i, 0, 2 * i)
                down(i - 1, 1, 2 * i - 1)
                up(i, 1, 2 * i + 1)
                down(i, 0, 2 * i)
            down(E_LOOP - 1, 1, E - 1)

            def turn(p, j):
                pe.wait_ge(f_yTs, j + 1)
                if not (isinstance(j, int) and j < 2):
                    pe.wait_ge(f_ys, j - 1)
                for c in range(4):
                    last = nc.tensor.transpose((K0, K1)[p][0:HALF, c * P:(c + 1) * P], yTs[:, p, c * HALF:(c + 1) * HALF],
                                               ident[:, :])
                last.then_inc(f_turned, 1)

            def combine(p, j):
                pe.wait_ge(f_ys, j + 1)
                pe.wait_ge(f_combs, j + 1)
                if not (isinstance(j, int) and j < 2):
                    pe.wait_ge(f_out, j - 1)
                for c in range(4):
                    last = mm((K2, K3)[p][:, (c // 2) * P:(c // 2 + 1) * P], combs[:, p, c, :], ys[:, p, c, :],
                              start=(c % 2 == 0), stop=(c % 2 == 1))
                last.then_inc(f_mm, 1)

            turn(0, 0)
            turn(1, 1)
            combine(0, 0)
            turn(0, 2)
            combine(1, 1)
            with pe.Fori(1, PAIRS // 2 - 1) as i:
                turn(1, 2 * i + 1)
                combine(0, 2 * i)
                turn(0, 2 * i + 2)
                combine(1, 2 * i + 1)
            turn(1, PAIRS - 1)
            combine(0, PAIRS - 2)
            combine(1, PAIRS - 1)

        @block.vector
        def _(dve):
            tt, ts = nc.vector.tensor_tensor, nc.vector.tensor_scalar
            dve.wait_ge(s_small, 16 * len(small))
            ts(temp[:, :], temp[:, :], CLAMP, None, ALU.min)
            dve.wait_ge(s_setup_pe, 1)
            ts(simrn[:, :], psB[0:PROJ, 0:NG - NR], 1e-24, None, ALU.max).then_inc(s_setup_dve, 2)
            dve.wait_ge(s_tanh, 1)
            ts(wo0[:, :], wo0[:, :], tg[:, 0:1], None, ALU.mult)
            ts(wffn0[:, 0:P], wffn0[:, 0:P], tg[:, 2:3], None, ALU.mult)
            ts(wu0[:, :], wu0[:, :], tg[0:NR, 2:3], None, ALU.mult)
            at, w = BIAS_AT["bo0"]
            ts(bias[:, at:at + w], bias[:, at:at + w], tg[0:3, 0:1], None, ALU.mult)
            dve.wait_ge(s_setup_pool, 7)
            dve.wait_ge(s_setup_act, 1)
            at = 0
            for e, r in enumerate(RANKS):
                ts(sim19[:, at:at + r], sim19[:, at:at + r], simrn[:, e:e + 1], tscale[:, 0:1], ALU.mult, ALU.mult)
                at += r
            nc.vector.scalar_tensor_tensor(sim19[:, NR:NG], simrn[:, :], tscale[:, 0:1], sim19[:, NR:NG], ALU.mult,
                                           ALU.mult)
            nc.vector.tensor_copy(bpwide[:, :], bpcol[:, 0:1].broadcast_to([PROJ, P])).then_inc(s_setup_dve, 1)
            dve.wait_ge(s_setup_pe, 2)
            nc.vector.tensor_copy(wffn0[:, P + PROJ:P + PROJ + NG], psQ[:, 0:NG]).then_inc(s_setup_dve, 1)
            dve.wait_ge(s_setup_pe, 3)
            at, w = BIAS_AT["ffn0"]
            nc.vector.tensor_copy(bias[:, at + P + PROJ:at + P + PROJ + NG], psX[0:3, 0:NG]).then_inc(s_setup_dve, 1)

            def split(r, n, signal):
                dve.wait_ge(s_setup_dve, n[0])
                nc.vector.tensor_copy(bias_p[0][:, r], bias[:, r]).then_inc(s_bias, 1)
                dve.wait_ge(s_bias, n[1] + 1)
                tt(bias_r[0][:, r], bias[:, r], bias_p[0][:, r], ALU.subtract).then_inc(s_bias, 1)
                dve.wait_ge(s_bias, n[1] + 2)
                nc.vector.tensor_copy(bias_p[1][:, r], bias_r[0][:, r]).then_inc(s_bias, 1)
                dve.wait_ge(s_bias, n[1] + 3)
                tt(bias_r[1][:, r], bias_r[0][:, r], bias_p[1][:, r], ALU.subtract).then_inc(s_bias, 1)
                dve.wait_ge(s_bias, n[1] + 4)
                nc.vector.tensor_copy(bias_p[2][:, r], bias_r[1][:, r]).then_inc(s_bias, 1)
                dve.wait_ge(s_bias, n[1] + 5)
                ts(bias_rows[:, r], bias_p[0][:, r], ident[0:3, 0:1], None, ALU.mult).then_inc(s_bias, 1)
                dve.wait_ge(s_bias, n[1] + 6)
                nc.vector.scalar_tensor_tensor(bias_rows[:, r], bias_p[1][:, r], ident[0:3, 1:2], bias_rows[:, r],
                                               ALU.mult, ALU.add).then_inc(s_bias, 1)
                dve.wait_ge(s_bias, n[1] + 7)
                nc.vector.scalar_tensor_tensor(bias_rows[:, r], bias_p[2][:, r], ident[0:3, 2:3], bias_rows[:, r],
                                               ALU.mult, ALU.add).then_inc(signal, 1)

            def first_biases():
                dve.wait_ge(s_late, 16 * len(late))
                nc.vector.tensor_copy(lnb_wide[:, :], ln_b.broadcast_to([P, 3])).then_inc(s_setup_dve, 1)
                split(slice(0, BIAS_AT["q1"][0]), (5, 0), s_setup_dve)
                dve.wait_ge(s_setup_pe, 4)
                at, w = BIAS_AT["q1"]
                ts(bias[:, at:at + w], K0[0:3, :], float(D1) ** -0.5, None, ALU.mult).then_inc(s_setup_dve, 1)

            def layer1_setup():
                ts(wo1[:, :, :], wo1[:, :, :], tg[:, 1:2], None, ALU.mult)
                ts(wq1[:, :], wq1[:, :], ln_g[:, 0:1], float(D1) ** -0.5, ALU.mult, ALU.mult).then_inc(s_setup_dve, 1)
                at, w = BIAS_AT["q1"]
                split(slice(at, at + w), (9, 7), s_setup_dve)
                ts(mask_rows[:, :], mask8[:, :], -MASKED, MASKED, ALU.mult, ALU.add).then_inc(s_setup_dve, 1)

            def step(i, par, t):
                if live(t, "rs1_ready0"):
                    k = t - LAG["rs1_ready0"]
                    done(dve, S["pv_mm0"], k)
                    nc.vector.reciprocal(rs1[:, 0, :], pv_bank(0)[:, :, D1]).then_inc(S["rs1_ready0"], 1)
                if live(t, "ln_shift"):
                    r = t - LAG["ln_shift"]
                    ln_done(dve, "ln_rstd", r)
                    lo, hi = ln_slots(r)
                    nc.vector.scalar_tensor_tensor(shift[:, lo:hi], mv[:, lo:hi, 0], -1.0, rstd[:, lo:hi], ALU.mult,
                                                   ALU.mult).then_inc(LN["ln_shift"], 1)
                if live(t, "ln_xn23"):
                    r, p = t - LAG["ln_xn23"], (par - LAG["ln_xn23"]) % 2
                    done(dve, S["disp_mm"], r - LN_LAG[3] - 2)
                    lo, hi = ln_slots(r, (2, 3))
                    for n in range(lo, hi):
                        last = ts(xn[:, p, n, :], ln_input(n, i, par, "ln_xn23"), mv[:, n, 0:1], rstd[:, n:n + 1],
                                  ALU.subtract, ALU.mult)
                    last.then_inc(LN["ln_xn23"], 1)
                if live(t, "o1_ready0"):
                    k = t - LAG["o1_ready0"]
                    done(dve, S["rs1_ready0"], k)
                    tt(o1[:, 0::2, :], pv_bank(0)[:, :, 0:D1], bc(rs1[:, 0, :], 2, D1),
                       ALU.mult).then_inc(S["o1_ready0"], 1)
                if live(t, "rs1_ready1"):
                    k = t - LAG["rs1_ready1"]
                    done(dve, S["pv_mm1"], k)
                    nc.vector.reciprocal(rs1[:, 1, :], pv_bank(1)[:, :, D1]).then_inc(S["rs1_ready1"], 1)
                if live(t, "chosen_ready"):
                    k = t - LAG["chosen_ready"]
                    done(dve, S["first_ready"], k)
                    nc.vector.scalar_tensor_tensor(chosen[:, :], iota8[:, :], idxf[:, 1:2], first[:, :], ALU.is_equal,
                                                   ALU.add).then_inc(S["chosen_ready"], 1)
                if live(t, "o1_ready1"):
                    k = t - LAG["o1_ready1"]
                    done(dve, S["rs1_ready1"], k)
                    tt(o1[:, 1::2, :], pv_bank(1)[:, :, 0:D1], bc(rs1[:, 1, :], 2, D1),
                       ALU.mult).then_inc(S["o1_ready1"], 1)
                if live(t, "rs0_ready"):
                    k = t - LAG["rs0_ready"]
                    done(dve, S["sum0_ready"], k)
                    nc.vector.reciprocal(rs0[:, :], sum0[:, :]).then_inc(S["rs0_ready"], 1)
                if live(t, "o0_ready1"):
                    k, p = t - LAG["o0_ready1"], (par - LAG["o0_ready1"]) % 2
                    done(dve, S["av_prod2"], k)
                    c = slice(1 * P // 2, 2 * P // 2)
                    nc.vector.reduce_sum(o0[:, c], prod_av[:, :].rearrange("p (c g) -> p c g", g=H0)[:, c, :],
                                         X).then_inc(S["o0_ready1"], 1)
                if live(t, "o0_ready0"):
                    k, p = t - LAG["o0_ready0"], (par - LAG["o0_ready0"]) % 2
                    done(dve, S["av_prod1"], k)
                    c = slice(0 * P // 2, 1 * P // 2)
                    nc.vector.reduce_sum(o0[:, c], prod_av[:, :].rearrange("p (c g) -> p c g", g=H0)[:, c, :],
                                         X).then_inc(S["o0_ready0"], 1)
                if live(t, "t_y_ready"):
                    k, p = t - LAG["t_y_ready"], (par - LAG["t_y_ready"]) % 2
                    expert_done(dve, "t_y_mm", k)
                    ts(yT[:, 0:B // 2, k - B, :], PB["t_y_mm"][:, 0:HB].rearrange("p (b s) -> p b s", s=CAP),
                       b2c[:, k - B:k - B + 1], None,
                       ALU.add).then_inc(TL["t_y_ready"], 1)
                if live(t, "qk_prod"):
                    k, p = t - LAG["qk_prod"], (par - LAG["qk_prod"]) % 2
                    done(dve, S["qkv_ready"], k)
                    h = slice(0, H_DVE)
                    pqk = prod_qk[:, :].rearrange("p (h g d) -> p h g d", h=H0, g=H0)[:, h, :, :]
                    qv = bc(qkv[:, p, 0:P].rearrange("p (h d) -> p h d", h=H0)[:, h, :], 2, H0)
                    kv = bc(qkv[:, p, P:2 * P].rearrange("p (g d) -> p g d", g=H0), 1, h.stop - h.start)
                    nc.vector.tensor_tensor(pqk, qv, kv, ALU.mult).then_inc(S["qk_prod"], 1)
                if live(t, "mxB_ready"):
                    k, p = t - LAG["mxB_ready"], (par - LAG["mxB_ready"]) % 2
                    done(dve, S["pj_ready"], k)
                    nc.vector.reduce_max(mxB[:, :], pj[:, p, PROJ:PROJ + NR], X).then_inc(S["mxB_ready"], 1)
                if live(t, "ssm_ready"):
                    k = t - LAG["ssm_ready"]
                    done(dve, S["ss_ready"], k)
                    ts(ssm[:, :], ss[:, :], 1e-24, None, ALU.max).then_inc(S["ssm_ready"], 1)
                if live(t, "dlB_ready"):
                    k, p = t - LAG["dlB_ready"], (par - LAG["dlB_ready"]) % 2
                    done(dve, S["mxB_ready"], k)
                    ts(dlB[:, :], pj[:, p, PROJ:PROJ + NG], mxB[:, 0:1], None, ALU.subtract).then_inc(S["dlB_ready"], 1)
                if live(t, "s0_ready0"):
                    k, p = t - LAG["s0_ready0"], (par - LAG["s0_ready0"]) % 2
                    done(dve, S["qk_prod"], k)
                    h = slice(0, H0 * H_DVE)
                    nc.vector.reduce_sum(s0[:, h], prod_qk[:, :].rearrange("p (s d) -> p s d", d=D0)[:, h, :],
                                         X).then_inc(S["s0_ready0"], 1)
                if live(t, "kk_ready"):
                    k = t - LAG["kk_ready"]
                    done(dve, S["dlB_ready"], k)
                    nc.vector.scalar_tensor_tensor(kk[:, :], dlB[:, 0:NR], 0.0, key15[:, :], ALU.is_ge,
                                                   ALU.mult).then_inc(S["kk_ready"], 1)
                if live(t, "s0_ready1"):
                    k, p = t - LAG["s0_ready1"], (par - LAG["s0_ready1"]) % 2
                    done(dve, S["qk_prod_rest"], k)
                    h = slice(H0 * H_DVE, H0 * H0)
                    nc.vector.reduce_sum(s0[:, h], prod_qk[:, :].rearrange("p (s d) -> p s d", d=D0)[:, h, :],
                                         X).then_inc(S["s0_ready1"], 1)
                if live(t, "rsB_ready"):
                    k = t - LAG["rsB_ready"]
                    done(dve, S["exB_ready"], k)
                    nc.vector.reciprocal(rsB[:, :], smB[:, :]).then_inc(S["rsB_ready"], 1)
                if live(t, "km_ready"):
                    k = t - LAG["km_ready"]
                    done(dve, S["kk_ready"], k)
                    nc.vector.reduce_max(km[:, :], kk[:, :], X).then_inc(S["km_ready"], 1)
                if live(t, "mx0_ready"):
                    k, p = t - LAG["mx0_ready"], (par - LAG["mx0_ready"]) % 2
                    done(dve, S["s0_ready1"], k)
                    nc.vector.reduce_max(mx0[:, :], s0[:, :].rearrange("p (h g) -> p h g", h=H0),
                                         X).then_inc(S["mx0_ready"], 1)
                if live(t, "oh15_ready"):
                    k = t - LAG["oh15_ready"]
                    done(dve, S["km_ready"], k)
                    ts(oh15[:, :], kk[:, :], km[:, 0:1], rsB[:, 0:1], ALU.is_equal, ALU.mult).then_inc(S["oh15_ready"], 1)
                if live(t, "s0m_ready"):
                    k, p = t - LAG["s0m_ready"], (par - LAG["s0m_ready"]) % 2
                    done(dve, S["mx0_ready"], k)
                    tt(s0m[:, :].rearrange("p (h g) -> p h g", h=H0), s0[:, :].rearrange("p (h g) -> p h g", h=H0),
                       bc(mx0[:, :], 2, H0),
                       ALU.subtract).then_inc(S["s0m_ready"], 1)
                if live(t, "dw_ready"):
                    k, p = t - LAG["dw_ready"], (par - LAG["dw_ready"]) % 2
                    done(dve, S["oh15_ready"], k)
                    tt(dw[:, :], oh15[:, :], pj[:, p, PROJ + NG:], ALU.mult).then_inc(S["dw_ready"], 1)
                if live(t, "nmx_ready0"):
                    k, p = t - LAG["nmx_ready0"], (par - LAG["nmx_ready0"]) % 2
                    done(dve, S["s1_mm0"], k)
                    nc.vector.tensor_reduce(nmx1[:, 0, :], PB["s1_mm0"][:, :].rearrange("p (h n) -> p h n", h=4), X,
                                            ALU.max,
                                            negate=True).then_inc(S["nmx_ready0"], 1)
                if live(t, "x3_ready"):
                    k = t - LAG["x3_ready"]
                    done(dve, S["y1_mm"], k)
                    tt(x3_at(k), x2[:, (par - LAG["x3_ready"]) % 2, :], PB["y1_mm"][:, 0:P],
                       ALU.add).then_inc(S["x3_ready"], 1)
                if live(t, "nmx_ready1"):
                    k, p = t - LAG["nmx_ready1"], (par - LAG["nmx_ready1"]) % 2
                    done(dve, S["s1_mm1"], k)
                    nc.vector.tensor_reduce(nmx1[:, 1, :], PB["s1_mm1"][:, :].rearrange("p (h n) -> p h n", h=4), X,
                                            ALU.max,
                                            negate=True).then_inc(S["nmx_ready1"], 1)
                if live(t, "x1_ready"):
                    k, p = t - LAG["x1_ready"], (par - LAG["x1_ready"]) % 2
                    loaded(dve, xres_loaded, i, par, 2)
                    done(dve, S["y0_mm"], k)
                    tt(x1[:, p, :], x_res[:, p, :], PB["y0_mm"][:, 0:P], ALU.add).then_inc(S["x1_ready"], 1)
                if live(t, "x2_ready"):
                    k, p = t - LAG["x2_ready"], (par - LAG["x2_ready"]) % 2
                    done(dve, S["x3_ready"], k - 2)
                    done(dve, S["res0_mm"], k)
                    tt(x2[:, p, :], x1[:, p, :], PB["ffn0_mm"][:, 0:P], ALU.add).then_inc(S["x2_ready"], 1)
                if live(t, "slot_ready"):
                    k = t - LAG["slot_ready"]
                    done(dve, S["pos_mm"], k)
                    nc.vector.scalar_tensor_tensor(slot[:, :], PB["pos_mm"][:, 0:E], 1.0, chosen[:, :], ALU.add,
                                                   ALU.mult).then_inc(S["slot_ready"], 1)
                if live(t, "ln_stats"):
                    r = t - LAG["ln_stats"]
                    if slot_live(r, 0):
                        loaded(dve, x_loaded, i, par, 0)
                    done(dve, S["x1_ready"], r - LN_LAG[1])
                    done(dve, S["x2_ready"], r - LN_LAG[2])
                    lo, hi = ln_slots(r)
                    for n in range(lo, hi):
                        last = nc.vector.bn_stats(stats[:, n, :], ln_input(n, i, par, "ln_stats"))
                    last.then_inc(LN["ln_stats"], 1)
                if live(t, "ln_mv"):
                    r = t - LAG["ln_mv"]
                    ln_done(dve, "ln_stats", r)
                if live(t, "rsD_ready"):
                    nc.vector.reciprocal(rsD[:, :], smD[:, :]).then_inc(S["rsD_ready"], 1)
                if live(t, "ln_mv"):
                    r = t - LAG["ln_mv"]
                    lo, hi = ln_slots(r)
                    for n in range(lo, hi):
                        last = nc.vector.bn_aggr(mv[:, n, :], stats[:, n, :])
                    last.then_inc(LN["ln_mv"], 1)
                if live(t, "gate_ready"):
                    k = t - LAG["gate_ready"]
                    done(dve, S["rsD_ready"], k)
                    done(dve, S["comb_ready"], k - 1)
                    nc.vector.scalar_tensor_tensor(gate[:, :], exD[:, :], rsD[:, 0:1], chosen[:, :], ALU.mult,
                                                   ALU.mult).then_inc(S["gate_ready"], 1)
                if live(t, "top_ready"):
                    k = t - LAG["top_ready"]
                    done(dve, S["router_mm"], k)
                if live(t, "disp_ready"):
                    tt(disp[:, :, :], bc(iota_slot[:, :], 1, E), bc(slot[:, :], 2, CAP),
                       ALU.is_equal).then_inc(S["disp_ready"], 1)
                if live(t, "top_ready"):
                    nc.vector.max(top8[:, :], PB["router_mm"][:, 0:E]).then_inc(S["top_ready"], 1)
                if live(t, "idx_ready"):
                    k = t - LAG["idx_ready"]
                    done(dve, S["top_ready"], k)
                    ts(dlD[:, :], PB["router_mm"][:, 0:E], top8[:, 0:1], None, ALU.subtract)
                    nc.vector.max_index(idx8[:, :], top8[:, :], PB["router_mm"][:, 0:E]).then_inc(S["idx_ready"], 1)
                if live(t, "idxf_ready"):
                    k = t - LAG["idxf_ready"]
                    done(dve, S["idx_ready"], k)
                    nc.vector.tensor_copy(idxf[:, :], idx8[:, 0:2]).then_inc(S["idxf_ready"], 1)
                if live(t, "sum0_ready"):
                    k, p = t - LAG["sum0_ready"], (par - LAG["sum0_ready"]) % 2
                    done(dve, S["e0_ready"], k)
                    nc.vector.reduce_sum(sum0[:, :], e0[:, p, :].rearrange("p (h g) -> p h g", h=H0),
                                         X).then_inc(S["sum0_ready"], 1)
                if live(t, "first_ready"):
                    k = t - LAG["first_ready"]
                    done(dve, S["idxf_ready"], k)
                    ts(first[:, :], iota8[:, :], idxf[:, 0:1], None, ALU.is_equal).then_inc(S["first_ready"], 1)

            steps(dve, step, {1: first_biases, 2: layer1_setup})

            def gather_weights(p, j):
                if not (isinstance(j, int) and j < 2):
                    dve.wait_ge(f_mm, j - 1)
                src = combT[:, 2 * j:2 * j + 2, :, :] if isinstance(j, int) else combT[:, ds(2 * j, 2), :, :]
                ts(combs[:, p, :, :], src.rearrange("p a c n -> p (a c) n"), 1.0, None, ALU.mult).then_inc(f_combs, 1)

            def gather_outputs(p, j):
                if not (isinstance(j, int) and j < 2):
                    dve.wait_ge(f_turned, j - 1)
                src = yT[:, 2 * j:2 * j + 2, :, :] if isinstance(j, int) else yT[:, ds(2 * j, 2), :, :]
                ts(yTs[:, p, :], src.rearrange("p a e s -> p (a e s)"), 1.0, None, ALU.mult).then_inc(f_yTs, 1)

            dve.wait_ge(S["combT_ready"], B)
            gather_weights(0, 0)
            gather_weights(1, 1)

            def expert(p, e):
                dve.wait_ge(e_y_mm, e + 1)
                ts(yT[:, B // 2:B, ds(e, 1), :].rearrange("p b a s -> p b (a s)"),
                   (psX, psQ)[p][:, 0:HB].rearrange("p (b s) -> p b s", s=CAP), b2c[:, ds(e, 1)], None,
                   ALU.add).then_inc(e_y_ready, 1)

            with dve.Fori(0, E_LOOP) as i:
                expert(0, 2 * i)
                expert(1, 2 * i + 1)
            expert_done(dve, "t_y_ready", B + E - 1)
            dve.wait_ge(e_y_ready, E)

            def finish(i, p, j):
                dve.wait_ge(f_mm, j + 1)
                if not (isinstance(j, int) and j < 2):
                    dve.wait_ge(f_stored[p], 16 * i)
                x = x3[:, 2 * j:2 * j + 2, :] if isinstance(j, int) else x3[:, ds(2 * j, 2), :]
                tt(o_out[:, p, :, :], x, (K2, K3)[p][:, 0:2 * P].rearrange("p (b n) -> p b n", b=2),
                   ALU.add).then_inc(f_out, 1)

            def pair(i, p, j):
                gather_outputs(p, j + 2)
                finish(i, p, j)
                gather_weights(p, j + 2)

            gather_outputs(0, 0)
            gather_outputs(1, 1)
            pair(0, 0, 0)
            pair(0, 1, 1)
            with dve.Fori(1, PAIRS // 2 - 1) as i:
                pair(i, 0, 2 * i)
                pair(i, 1, 2 * i + 1)
            finish(PAIRS // 2 - 1, 0, PAIRS - 2)
            finish(PAIRS // 2 - 1, 1, PAIRS - 1)


def kernel(**inputs):
    import numpy as np
    import concourse.bacc as bacc
    from concourse.bass_utils import run_bass_kernel_spmd

    def t(name):
        return np.ascontiguousarray(np.asarray(inputs[name]).T)

    f32 = np.float32
    import ml_dtypes
    bf16 = ml_dtypes.bfloat16
    arange = np.arange
    def every_row(values):
        return np.broadcast_to(np.asarray(values, f32), (P, len(values)))

    def zeros(*shape):
        return np.zeros(shape, f32)

    def given(name):
        return np.asarray(inputs[name])

    arrays = {
        "x": given("x"),
        "ctxT": np.ascontiguousarray(given("ctx_1024").transpose(0, 2, 1)),
        "mask": given("mask_BxS2_bk0"),
        "g_xattn": given("g_xattn"), "g_ffn": given("g_ffn"),
        "wp0": given("L0_ffn_Wp"), "bp0": given("L0_ffn_bp"), "temp": given("L0_ffn_temp"),
        "sim19": np.concatenate([np.repeat(given("L0_ffn_sim"), RANKS, axis=1), given("L0_ffn_sim")], axis=1),
        "wu0T": np.concatenate([t(f"L0_ffn_Wu{n}") for n in range(4)], axis=0),
        "W1": given("L1_ffn_W1"), "W2": given("L1_ffn_W2"),
        "b1T": np.ascontiguousarray(given("L1_ffn_b1").reshape(E, HC, P).transpose(0, 2, 1)),
        "biases": np.concatenate([given("L0_xattn_bq"), given("L0_xattn_bk"), given("L0_xattn_bv"), given("L0_xattn_bo"),
                                  zeros(P), given("L0_ffn_bp"), zeros(NG + NR), given("L1_ffn_br"), zeros(H1 * D1)]),
        "pack_a": np.concatenate([np.eye(P, dtype=f32), every_row(arange(E)), every_row(arange(1, CAP + 1)),
                        every_row(np.repeat(arange(4, 0, -1), RANKS)),
                        every_row([1, 1, 1 + 1e-5, 1]), every_row([1e-5, 1e-5, 1e-10, 1e-5]),
                        t("L0_xattn_Wq"), t("L0_xattn_Wk"), t("L0_xattn_Wv"), t("L0_xattn_Wo"),
                        t("L0_ffn_W"), t("L0_ffn_Wp"), zeros(P, NG), *[t(f"L0_ffn_Wd{n}") for n in range(4)],
                        given("L1_ffn_Wr"), t("L1_ffn_b2")], axis=1),
        "pack_b": np.concatenate([given("L1_xattn_Wq"), given("L1_xattn_Wkv"),
                                  given("L1_xattn_Wo").reshape(4, P, P).transpose(1, 0, 2).reshape(P, 4 * P),
                                  given("L1_xattn_ln_g")[:, None], given("L1_xattn_ln_b")[:, None]], axis=1),
        "before": (arange(P)[:, None] < arange(P)[None, :]).astype(bf16),
    }
    assert arrays["pack_a"].shape[1] == WIDTH_A and arrays["pack_b"].shape[1] == WIDTH_B
    assert arrays["biases"].shape[0] == BIASES
    nc = bacc.Bacc("TRN2", target_bir_lowering=False, num_devices=1)
    feed, args = {}, {}
    for name, arr in arrays.items():
        feed[f"in_{name}"] = arr
        args[name] = nc.dram_tensor(f"in_{name}", arr.shape, mybir.dt.from_np(arr.dtype), kind="ExternalInput").ap()
    out = nc.dram_tensor("out_0", (B, P, P), F32, kind="ExternalOutput").ap()
    build(nc, args, out)
    r = run_bass_kernel_spmd(nc, [feed], core_ids=[0])
    return r.results[0]["out_0"]
```
